# Optimizing a Trainium2 kernel written in Bass

```python
import numpy as np
import jax
import jax.numpy as jnp

def _softmax(x, axis=-1):
    return jax.nn.softmax(x, axis=axis)

def _gelu(x):
    return jax.nn.gelu(x, approximate=True)

def _silu(x):
    return jax.nn.silu(x)

def _sigmoid(x):
    return jax.nn.sigmoid(x)

def _layernorm(x, axis=-1, eps=1e-05):
    m = jnp.mean(x, axis=axis, keepdims=True)
    v = jnp.var(x, axis=axis, keepdims=True)
    return (x - m) / jnp.sqrt(v + eps)

def _scatter_add(tgt, idx, src, axis=0):
    return tgt.at[idx].add(src)

def _segment_sum(src, seg, n):
    return jax.ops.segment_sum(src, seg, n)
kernel_name = 'mk_gnn_resnorm_d4_gnn_r8_59459c'

def setup_inputs(seed: int=0):
    np.random.seed(seed)
    _w = jnp.asarray

    def _rec_inputs():
        import jax
        import jax.numpy as jnp
        _gk = jax.random.key(seed)
        x = -0.0001006 + 1 * jax.random.normal(jax.random.fold_in(_gk, 1), (6250, 96), jnp.float32)
        src = jax.random.randint(jax.random.fold_in(_gk, 2), (200000,), 0, 6250, jnp.int32)
        dst = jnp.minimum((6250 * jax.random.uniform(jax.random.fold_in(_gk, 3), (200000,)) ** 2.0).astype(jnp.int32), 49999)
        _o = jnp.argsort(dst, stable=True)
        src = src[_o]
        dst = dst[_o]
        edge_attr_32 = 0.000196303 + 1.00016 * jax.random.normal(jax.random.fold_in(_gk, 11), (200000, 32), jnp.float32)
        return (x, src, dst, edge_attr_32)
    x, src, dst, edge_attr_32 = _rec_inputs()

    def _L0_gnn_setup():
        import jax, jax.numpy as jnp
        import numpy as np
        N = 6250
        E = 100000
        DIM = 96
        HEADS = 4
        HEAD_DIM = DIM // HEADS
        SLOPE = 0.2
        EPS = 1e-05

        def _gat_layer(x, edge_index, W, att_src, att_dst, gat_bias, proj_W, proj_b, ln_g, ln_b):
            loop = jnp.arange(N, dtype=edge_index.dtype)
            src = jnp.concatenate([edge_index[0], loop])
            dst = jnp.concatenate([edge_index[1], loop])
            h = (x @ W).reshape(N, HEADS, HEAD_DIM)
            a_src = jnp.einsum('nhd,hd->nh', h, att_src)
            a_dst = jnp.einsum('nhd,hd->nh', h, att_dst)
            e = jax.nn.leaky_relu(a_src[src] + a_dst[dst], SLOPE)
            m = jax.ops.segment_max(e, dst, num_segments=N)
            e = jnp.exp(e - m[dst])
            denom = jax.ops.segment_sum(e, dst, num_segments=N)
            alpha = e / denom[dst]
            out = jax.ops.segment_sum(alpha[:, :, None] * h[src], dst, num_segments=N)
            out = out.reshape(N, HEADS * HEAD_DIM) + gat_bias
            proj = out @ proj_W.T + proj_b
            z = x + proj
            mu = jnp.mean(z, axis=-1, keepdims=True)
            var = jnp.mean((z - mu) ** 2, axis=-1, keepdims=True)
            return ln_g * (z - mu) / jnp.sqrt(var + EPS) + ln_b
        key = jax.random.key(seed)
        ks = jax.random.split(key, 10)
        s = 0.1
        return {'x': jax.random.normal(ks[0], (N, DIM), jnp.float32), 'edge_index': jax.random.randint(ks[1], (2, E), 0, N, dtype=jnp.int64), 'W': jax.random.normal(ks[2], (DIM, HEADS * HEAD_DIM), jnp.float32) * s, 'att_src': jax.random.normal(ks[3], (HEADS, HEAD_DIM), jnp.float32) * s, 'att_dst': jax.random.normal(ks[4], (HEADS, HEAD_DIM), jnp.float32) * s, 'gat_bias': jnp.zeros((DIM,), jnp.float32), 'proj_W': jax.random.normal(ks[5], (DIM, DIM), jnp.float32) * s, 'proj_b': jnp.zeros((DIM,), jnp.float32), 'ln_g': jnp.ones((DIM,), jnp.float32), 'ln_b': jnp.zeros((DIM,), jnp.float32)}
    _L0_gnn_all = _L0_gnn_setup()
    _L0_gnn_in = {k: v for k, v in _L0_gnn_all.items() if k in ('W', 'att_src', 'att_dst', 'gat_bias', 'proj_W', 'proj_b', 'ln_g', 'ln_b')}
    del _L0_gnn_all

    def _L1_gnn_setup():
        import jax, jax.numpy as jnp
        import numpy as np
        N, E = (6250, 100000)
        DIN = DOUT = 96
        DE = 32

        def _egnn_conv(x, src, dst, edge_attr, W_msg, W_edge, W_root, b):
            msg = x[src] @ W_msg + edge_attr @ W_edge
            agg = jax.ops.segment_max(msg, dst, num_segments=x.shape[0])
            agg = jnp.where(jnp.isneginf(agg), 0.0, agg)
            return agg + x @ W_root + b
        key = jax.random.key(seed)
        ks = jax.random.split(key, 10)
        rn = lambda k, sh, sc: jax.random.normal(k, sh, jnp.float32) * sc
        return {'X': rn(ks[0], (N, DIN), 1.0), 'edge_index': jax.random.randint(ks[1], (2, E), 0, N, jnp.int32), 'edge_attr': rn(ks[2], (E, DE), 1.0), 'W1_msg': rn(ks[3], (DIN, DOUT), DIN ** (-0.5)), 'W1_edge': rn(ks[4], (DE, DOUT), DE ** (-0.5)), 'W1_root': rn(ks[5], (DIN, DOUT), DIN ** (-0.5)), 'b1': jnp.zeros((DOUT,), jnp.float32), 'W2_msg': rn(ks[6], (DOUT, DOUT), DOUT ** (-0.5)), 'W2_edge': rn(ks[7], (DE, DOUT), DE ** (-0.5)), 'W2_root': rn(ks[8], (DOUT, DOUT), DOUT ** (-0.5)), 'b2': jnp.zeros((DOUT,), jnp.float32)}
    _L1_gnn_all = _L1_gnn_setup()
    _L1_gnn_in = {k: v for k, v in _L1_gnn_all.items() if k in ('W1_msg', 'W1_edge', 'W1_root', 'b1', 'W2_msg', 'W2_edge', 'W2_root', 'b2')}
    del _L1_gnn_all

    def _L2_gnn_setup():
        import jax, jax.numpy as jnp
        import numpy as np
        N_NODES = 6250
        N_EDGES = 100000
        D_IN = 96
        D_HID = 96
        D_OUT = 96

        def _sage_layer(h, src, dst, W_l, b_l, W_r):
            msgs = h[src]
            agg = jax.ops.segment_sum(msgs, dst, num_segments=N_NODES)
            cnt = jax.ops.segment_sum(jnp.ones((src.shape[0], 1), h.dtype), dst, num_segments=N_NODES)
            mean = agg / jnp.maximum(cnt, 1.0)
            return mean @ W_l + b_l + h @ W_r
        key = jax.random.key(seed)
        ks = jax.random.split(key, 8)
        x = jax.random.normal(ks[0], (N_NODES, D_IN), dtype=jnp.float32)
        edge_index = jax.random.randint(ks[1], (2, N_EDGES), 0, N_NODES, dtype=jnp.int32)
        s = 1.0 / np.sqrt(D_IN)
        W1_l = jax.random.uniform(ks[2], (D_IN, D_HID), jnp.float32, -s, s)
        W1_r = jax.random.uniform(ks[3], (D_IN, D_HID), jnp.float32, -s, s)
        b1 = jnp.zeros((D_HID,), jnp.float32)
        s2 = 1.0 / np.sqrt(D_HID)
        W2_l = jax.random.uniform(ks[4], (D_HID, D_OUT), jnp.float32, -s2, s2)
        W2_r = jax.random.uniform(ks[5], (D_HID, D_OUT), jnp.float32, -s2, s2)
        b2 = jnp.zeros((D_OUT,), jnp.float32)
        return {'x': x, 'edge_index': edge_index, 'W1_l': W1_l, 'b1': b1, 'W1_r': W1_r, 'W2_l': W2_l, 'b2': b2, 'W2_r': W2_r}
    _L2_gnn_all = _L2_gnn_setup()
    _L2_gnn_in = {k: v for k, v in _L2_gnn_all.items() if k in ('W1_l', 'b1', 'W1_r', 'W2_l', 'b2', 'W2_r')}
    del _L2_gnn_all

    def _L3_gnn_setup():
        import jax, jax.numpy as jnp
        import numpy as np
        N = 6250

        def gcn_conv(x, W, b, src, dst, deg_inv_sqrt):
            h = x @ W
            norm = deg_inv_sqrt[src] * deg_inv_sqrt[dst]
            msgs = h[src] * norm[:, None]
            out = jax.ops.segment_sum(msgs, dst, num_segments=N)
            out = out + h * (deg_inv_sqrt * deg_inv_sqrt)[:, None]
            return out + b
        key = jax.random.key(seed)
        ks = jax.random.split(key, 8)
        C = 96
        x = jax.random.normal(ks[0], (N, C), dtype=jnp.float32)
        edge_index = jax.random.randint(ks[1], (2, 100000), 0, N, dtype=jnp.int64)
        s = 1.0 / np.sqrt(C)
        W1 = jax.random.uniform(ks[2], (C, C), jnp.float32, -s, s)
        b1 = jnp.zeros((C,), jnp.float32)
        W2 = jax.random.uniform(ks[3], (C, C), jnp.float32, -s, s)
        b2 = jnp.zeros((C,), jnp.float32)
        W3 = jax.random.uniform(ks[4], (C, C), jnp.float32, -s, s)
        b3 = jnp.zeros((C,), jnp.float32)
        return {'x': x, 'edge_index': edge_index, 'W1': W1, 'b1': b1, 'W2': W2, 'b2': b2, 'W3': W3, 'b3': b3}
    _L3_gnn_all = _L3_gnn_setup()
    _L3_gnn_in = {k: v for k, v in _L3_gnn_all.items() if k in ('W1', 'b1', 'W2', 'b2', 'W3', 'b3')}
    del _L3_gnn_all
    return {'x': x, 'src': src, 'dst': dst, 'edge_attr_32': edge_attr_32, 'L0_gnn_W': _L0_gnn_in['W'], 'L0_gnn_att_src': _L0_gnn_in['att_src'], 'L0_gnn_att_dst': _L0_gnn_in['att_dst'], 'L0_gnn_gat_bias': _L0_gnn_in['gat_bias'], 'L0_gnn_proj_W': _L0_gnn_in['proj_W'], 'L0_gnn_proj_b': _L0_gnn_in['proj_b'], 'L0_gnn_ln_g': _L0_gnn_in['ln_g'], 'L0_gnn_ln_b': _L0_gnn_in['ln_b'], 'L1_gnn_W1_msg': _L1_gnn_in['W1_msg'], 'L1_gnn_W1_edge': _L1_gnn_in['W1_edge'], 'L1_gnn_W1_root': _L1_gnn_in['W1_root'], 'L1_gnn_b1': _L1_gnn_in['b1'], 'L1_gnn_W2_msg': _L1_gnn_in['W2_msg'], 'L1_gnn_W2_edge': _L1_gnn_in['W2_edge'], 'L1_gnn_W2_root': _L1_gnn_in['W2_root'], 'L1_gnn_b2': _L1_gnn_in['b2'], 'L2_gnn_W1_l': _L2_gnn_in['W1_l'], 'L2_gnn_b1': _L2_gnn_in['b1'], 'L2_gnn_W1_r': _L2_gnn_in['W1_r'], 'L2_gnn_W2_l': _L2_gnn_in['W2_l'], 'L2_gnn_b2': _L2_gnn_in['b2'], 'L2_gnn_W2_r': _L2_gnn_in['W2_r'], 'L3_gnn_W1': _L3_gnn_in['W1'], 'L3_gnn_b1': _L3_gnn_in['b1'], 'L3_gnn_W2': _L3_gnn_in['W2'], 'L3_gnn_b2': _L3_gnn_in['b2'], 'L3_gnn_W3': _L3_gnn_in['W3'], 'L3_gnn_b3': _L3_gnn_in['b3']}

def reference(x, src, dst, edge_attr_32, L0_gnn_W, L0_gnn_att_src, L0_gnn_att_dst, L0_gnn_gat_bias, L0_gnn_proj_W, L0_gnn_proj_b, L0_gnn_ln_g, L0_gnn_ln_b, L1_gnn_W1_msg, L1_gnn_W1_edge, L1_gnn_W1_root, L1_gnn_b1, L1_gnn_W2_msg, L1_gnn_W2_edge, L1_gnn_W2_root, L1_gnn_b2, L2_gnn_W1_l, L2_gnn_b1, L2_gnn_W1_r, L2_gnn_W2_l, L2_gnn_b2, L2_gnn_W2_r, L3_gnn_W1, L3_gnn_b1, L3_gnn_W2, L3_gnn_b2, L3_gnn_W3, L3_gnn_b3):
    import jax
    import jax.numpy as jnp

    def _L0_gnn_ref(x, edge_index, W, att_src, att_dst, gat_bias, proj_W, proj_b, ln_g, ln_b):
        import jax, jax.numpy as jnp
        import numpy as np
        N = 6250
        E = 100000
        DIM = 96
        HEADS = 4
        HEAD_DIM = DIM // HEADS
        SLOPE = 0.2
        EPS = 1e-05

        def _gat_layer(x, edge_index, W, att_src, att_dst, gat_bias, proj_W, proj_b, ln_g, ln_b):
            loop = jnp.arange(N, dtype=edge_index.dtype)
            src = jnp.concatenate([edge_index[0], loop])
            dst = jnp.concatenate([edge_index[1], loop])
            h = (x @ W).reshape(N, HEADS, HEAD_DIM)
            a_src = jnp.einsum('nhd,hd->nh', h, att_src)
            a_dst = jnp.einsum('nhd,hd->nh', h, att_dst)
            e = jax.nn.leaky_relu(a_src[src] + a_dst[dst], SLOPE)
            m = jax.ops.segment_max(e, dst, num_segments=N)
            e = jnp.exp(e - m[dst])
            denom = jax.ops.segment_sum(e, dst, num_segments=N)
            alpha = e / denom[dst]
            out = jax.ops.segment_sum(alpha[:, :, None] * h[src], dst, num_segments=N)
            out = out.reshape(N, HEADS * HEAD_DIM) + gat_bias
            proj = out @ proj_W.T + proj_b
            z = x + proj
            mu = jnp.mean(z, axis=-1, keepdims=True)
            var = jnp.mean((z - mu) ** 2, axis=-1, keepdims=True)
            return ln_g * (z - mu) / jnp.sqrt(var + EPS) + ln_b
        return _gat_layer(x, edge_index, W, att_src, att_dst, gat_bias, proj_W, proj_b, ln_g, ln_b)

    def _L1_gnn_ref(X, edge_index, edge_attr, W1_msg, W1_edge, W1_root, b1, W2_msg, W2_edge, W2_root, b2):
        import jax, jax.numpy as jnp
        import numpy as np
        N, E = (6250, 100000)
        DIN = DOUT = 96
        DE = 32

        def _egnn_conv(x, src, dst, edge_attr, W_msg, W_edge, W_root, b):
            msg = x[src] @ W_msg + edge_attr @ W_edge
            agg = jax.ops.segment_max(msg, dst, num_segments=x.shape[0])
            agg = jnp.where(jnp.isneginf(agg), 0.0, agg)
            return agg + x @ W_root + b
        src, dst = (edge_index[0], edge_index[1])
        c1 = jax.nn.leaky_relu(_egnn_conv(X, src, dst, edge_attr, W1_msg, W1_edge, W1_root, b1))
        c2 = jax.nn.leaky_relu(_egnn_conv(c1, src, dst, edge_attr, W2_msg, W2_edge, W2_root, b2))
        return c2

    def _L2_gnn_ref(x, edge_index, W1_l, b1, W1_r, W2_l, b2, W2_r):
        import jax, jax.numpy as jnp
        import numpy as np
        N_NODES = 6250
        N_EDGES = 100000
        D_IN = 96
        D_HID = 96
        D_OUT = 96

        def _sage_layer(h, src, dst, W_l, b_l, W_r):
            msgs = h[src]
            agg = jax.ops.segment_sum(msgs, dst, num_segments=N_NODES)
            cnt = jax.ops.segment_sum(jnp.ones((src.shape[0], 1), h.dtype), dst, num_segments=N_NODES)
            mean = agg / jnp.maximum(cnt, 1.0)
            return mean @ W_l + b_l + h @ W_r
        src, dst = (edge_index[0], edge_index[1])
        h = jax.nn.relu(_sage_layer(x, src, dst, W1_l, b1, W1_r))
        out = _sage_layer(h, src, dst, W2_l, b2, W2_r)
        return out

    def _L3_gnn_ref(x, edge_index, W1, b1, W2, b2, W3, b3):
        import jax, jax.numpy as jnp
        import numpy as np
        N = 6250

        def gcn_conv(x, W, b, src, dst, deg_inv_sqrt):
            h = x @ W
            norm = deg_inv_sqrt[src] * deg_inv_sqrt[dst]
            msgs = h[src] * norm[:, None]
            out = jax.ops.segment_sum(msgs, dst, num_segments=N)
            out = out + h * (deg_inv_sqrt * deg_inv_sqrt)[:, None]
            return out + b
        src, dst = (edge_index[0], edge_index[1])
        deg = jax.ops.segment_sum(jnp.ones(src.shape[0], x.dtype), dst, num_segments=N) + 1.0
        dis = jax.lax.rsqrt(deg)
        h = gcn_conv(x, W1, b1, src, dst, dis)
        h = jax.nn.relu(h)
        h = gcn_conv(h, W2, b2, src, dst, dis)
        h = jax.nn.relu(h)
        return gcn_conv(h, W3, b3, src, dst, dis)
    edge_index = jnp.stack([src, dst])
    x = _layernorm(x + _L0_gnn_ref(x, edge_index, L0_gnn_W, L0_gnn_att_src, L0_gnn_att_dst, L0_gnn_gat_bias, L0_gnn_proj_W, L0_gnn_proj_b, L0_gnn_ln_g, L0_gnn_ln_b), axis=-1)
    x = _layernorm(x + _L1_gnn_ref(x, edge_index, edge_attr_32, L1_gnn_W1_msg, L1_gnn_W1_edge, L1_gnn_W1_root, L1_gnn_b1, L1_gnn_W2_msg, L1_gnn_W2_edge, L1_gnn_W2_root, L1_gnn_b2), axis=-1)
    x = _layernorm(x + _L2_gnn_ref(x, edge_index, L2_gnn_W1_l, L2_gnn_b1, L2_gnn_W1_r, L2_gnn_W2_l, L2_gnn_b2, L2_gnn_W2_r), axis=-1)
    x = _layernorm(x + _L3_gnn_ref(x, edge_index, L3_gnn_W1, L3_gnn_b1, L3_gnn_W2, L3_gnn_b2, L3_gnn_W3, L3_gnn_b3), axis=-1)
    return x

_drawn_inputs = setup_inputs


def setup_inputs(seed=0):
    import zlib

    import numpy as np

    out = dict(_drawn_inputs(seed))
    spreads = {'L0_gnn_gat_bias': (0.0, 0.1),
     'L0_gnn_proj_b': (0.0, 0.1),
     'L0_gnn_ln_g': (1.0, 0.2),
     'L0_gnn_ln_b': (0.0, 0.311),
     'L1_gnn_b1': (0.0, 0.289),
     'L1_gnn_b2': (0.0, 0.311),
     'L2_gnn_b1': (0.0, 0.1),
     'L2_gnn_b2': (0.0, 0.1),
     'L3_gnn_b1': (0.0, 0.493),
     'L3_gnn_b2': (0.0, 0.1),
     'L3_gnn_b3': (0.0, 0.1)}
    factors = {'L0_gnn_att_dst': 5.641}
    for name, (base, spread) in spreads.items():
        noise = np.random.default_rng([zlib.crc32(name.encode()), seed]).standard_normal(out[name].shape)
        drawn = base * np.exp(spread * noise) if base else spread * noise
        out[name] = jnp.asarray(drawn.astype(out[name].dtype))
    for name, factor in factors.items():
        out[name] = (out[name] * factor).astype(out[name].dtype)
    return out
```

```python
from contextlib import ExitStack

import concourse.bass as bass
from concourse import mybir

P = 128
NODES = 6250
EDGES = 200000
DIM = 96
HEADS = 4
HDIM = DIM // HEADS
EDGE_DIM = 32
NB = -(-NODES // P)
NPAD = NB * P
LAST = NODES - (NB - 1) * P
GB = 7
NG = NB // GB
S = 8
T = -(-EDGES // (P * 2 * S)) * 2 * S
EPAD = P * T
ITERS = T // (2 * S)
HB = 16
HI = 64
HW = HDIM + 1
SW = HEADS * HW
W0 = SW + HEADS
BIG = 1e30
OUT_COLS = 256

F32 = mybir.dt.float32
I32 = mybir.dt.int32
BF16 = mybir.dt.bfloat16
ALU = mybir.AluOpType
ACT = mybir.ActivationFunctionType
AX = mybir.AxisListType

ATT, PROJ, MAX1, MAX2, MEAN1, MEAN2, GCN1, GCN2, GCN3 = range(9)
PHASE_COLS = [W0 + HEADS, DIM] + [2 * DIM] * 4 + [DIM] * 3
PASS_OF_PHASE = {ATT: 0, MAX1: 1, MAX2: 2, MEAN1: 3, MEAN2: 4, GCN1: 5, GCN2: 6, GCN3: 7}
MAX_PASSES = (1, 2)


def out_group_base(phase, kind):
    n = 0
    for f in range(9):
        if f == phase and kind == "rows":
            return n
        n += NG
        if f in PASS_OF_PHASE:
            if f == phase:
                return n
            n += NG


stage_base = out_group_base


def build(nc, x, src, dst, dst_before, edge_attr, att_W, att_src, att_dst, gat_bias, proj_WT, proj_b, ln_g, ln_b,
          m1_msg, m1_edge, m1_root, m1_b, m2_msg, m2_edge, m2_root, m2_b,
          s1_l, s1_b, s1_r, s2_l, s2_b, s2_r, g1_W, g1_b, g2_W, g2_b, g3_W, g3_b, out):
    ctx = ExitStack()

    def sb(name, shape, dt=F32, stack=ctx):
        return stack.enter_context(nc.sbuf_tensor(name, shape, dt))

    def sem(name):
        return ctx.enter_context(nc.semaphore(name))

    table0 = nc.dram_tensor("table0", (NPAD, W0), F32, kind="Internal").ap()
    table = nc.dram_tensor("table", (NPAD, DIM), F32, kind="Internal").ap()
    hist0 = nc.dram_tensor("hist0", (EPAD, W0), F32, kind="Internal").ap()
    hist = nc.dram_tensor("hist", (EPAD, DIM), F32, kind="Internal").ap()
    ad_nodes = nc.dram_tensor("ad_nodes", (NPAD, HEADS), F32, kind="Internal").ap()
    ad_starts = nc.dram_tensor("ad_starts", (EPAD, HEADS), F32, kind="Internal").ap()
    last_row = nc.dram_tensor("last_row", (HI * P,), F32, kind="Internal").ap()
    start_row = nc.dram_tensor("start_row", (HI * P,), F32, kind="Internal").ap()

    X = sb("X", [P, NB, DIM])
    C = sb("C", [P, NB, DIM])
    TB = sb("TB", [P, NB * W0])
    TB0 = TB[:, :].rearrange("p (b w) -> p b w", w=W0)
    TBW = TB[:, 0:NB * DIM].rearrange("p (b w) -> p b w", w=DIM)
    EG = sb("EG", [P, NB * W0])
    EG0 = EG[:, :].rearrange("p (b w) -> p b w", w=W0)
    EGW = EG[:, 0:NB * DIM].rearrange("p (b w) -> p b w", w=DIM)
    ARENA = sb("ARENA", [P, T * HEADS])
    AD = ARENA[:, :].rearrange("p (t h) -> p t h", h=HEADS)
    ROWB = ARENA[:, 0:NPAD]
    R = ARENA[:, 0:NB * DIM].rearrange("p (b w) -> p b w", w=DIM)
    CQ = ARENA[:, 0:NB * W0].rearrange("p (b w) -> p b w", w=W0)
    SEL = sb("SEL", [P, NPAD])
    SRC = sb("SRC", [P, T], I32)
    same = sb("same", [P, T])
    reset = sb("reset", [P, T])
    G = sb("G", [P, 2, S * W0])
    H = sb("H", [P, 2, S * W0])
    G0 = G[:, :, :].rearrange("p s (k w) -> p s k w", w=W0)
    H0 = H[:, :, :].rearrange("p s (k w) -> p s k w", w=W0)
    GW = G[:, :, 0:S * DIM].rearrange("p s (k w) -> p s k w", w=DIM)
    HWD = H[:, :, 0:S * DIM].rearrange("p s (k w) -> p s k w", w=DIM)
    EA = sb("EA", [EDGE_DIM, 2, S, P])
    idx = sb("idx", [P, 2, S], I32)
    Zs = sb("Zs", [P, S, HEADS])
    Rm = sb("Rm", [P, S + 1, HEADS])
    EX = sb("EX", [P, 2, S, HEADS])
    U = sb("U", [P, SW])
    WR = sb("WR", [DIM, 9, 2 * DIM])
    WE = sb("WE", [EDGE_DIM, 2, DIM])
    attv = sb("attv", [DIM, 2, DIM])
    attp = sb("attp", [DIM, 2, DIM])
    gbT = sb("gbT", [DIM, 1])
    rows = sb("rows", [P, 10, DIM])
    XT = sb("XT", [DIM, GB * P])
    STG = sb("STG", [P, GB * P])
    ident = sb("ident", [P, P])
    upper = sb("upper", [HI, HI])
    ones = sb("ones", [P, P])
    onesrow = sb("onesrow", [P, W0])
    iota_i = sb("iota_i", [P, P], I32)
    bound_i = sb("bound_i", [P, 1], I32)
    iota_b = sb("iota_b", [P, P], BF16)
    bound = sb("bound", [P, 2])
    whole = sb("whole", [P, 1])
    wdiag = sb("wdiag", [P, P])
    wrow = sb("wrow", [W0, P])
    wneg = sb("wneg", [W0, P])
    deg = sb("deg", [HI, P])
    zero64 = sb("zero64", [HI, P])
    ends = sb("ends", [HI, P])
    starts = sb("starts", [HI, P])
    lastf = sb("lastf", [HI, P])
    offs = sb("offs", [HI, 1])
    degN = sb("degN", [P, HI])
    endN = sb("endN", [P, HI])
    valid = sb("valid", [P, NB])
    vpen = sb("vpen", [P, NB])
    cpen = sb("cpen", [P, NB])
    rcnt = sb("rcnt", [P, NB])
    dis = sb("dis", [P, NB])
    nf = sb("nf", [P, NB])
    last_i = sb("last_i", [P, NB], I32)
    start_i = sb("start_i", [P, NB], I32)
    ADN = sb("ADN", [P, NB, HEADS])
    zself = sb("zself", [P, NB, HEADS])
    mx = sb("mx", [P, NB, HEADS])
    E3 = sb("E3", [P, 3, NB, HEADS])
    rden = sb("rden", [P, NB, HEADS])
    stat = sb("stat", [P, 2, NB])
    dst0 = sb("dst0", [P, 1], I32)
    F0 = sb("F0", [P, W0 + SW])
    QT = sb("QT", [SW, 4, P])
    Q = sb("Q", [P, W0])
    DST = C[:, :, :].rearrange("p b d -> p (b d)")[:, 0:T].bitcast(I32)
    PREV = C[:, :, :].rearrange("p b d -> p (b d)")[:, T:2 * T].bitcast(I32)
    HILO = C[:, :, :].rearrange("p b d -> p (b d)")[:, 2 * T:3 * T].bitcast(BF16)
    HIB, LOB = HILO[:, 0:T], HILO[:, T:2 * T]
    TMPI = EG[:, 0:T].bitcast(I32)
    OH = EG[:, T:T + HB * (HI + P)].bitcast(BF16)
    OHHI = OH[:, 0:2 * HB * HI].rearrange("p (s k m) -> p s k m", s=2, k=HB)
    OHLO = OH[:, 2 * HB * HI:2 * HB * (HI + P)].rearrange("p (s k m) -> p s k m", s=2, k=HB)

    psX = ctx.enter_context(nc.psum_tensor("psX", [P, 1024], F32))
    psO = ctx.enter_context(nc.psum_tensor("psO", [P, 2048], F32))
    psA = ctx.enter_context(nc.psum_tensor("psA", [P, 512], F32))
    psB = ctx.enter_context(nc.psum_tensor("psB", [P, 512], F32))
    OUTG = psO[:, 0:GB * OUT_COLS].rearrange("p (j c) -> p j c", c=OUT_COLS)
    ETERM = psO[:, :].rearrange("p (s b c) -> p s b c", s=2, b=2)
    psM = [psA, psB]

    inputs_loaded = sem("inputs_loaded")
    pads_zeroed = sem("pads_zeroed")
    consts_made = sem("consts_made")
    filled = sem("filled")
    weights_made = sem("weights_made")
    rows_ready = sem("rows_ready")
    staged = sem("staged")
    transposed = sem("transposed")
    xt_copied = sem("xt_copied")
    out_ready = sem("out_ready")
    out_used = sem("out_used")
    table_made = sem("table_made")
    table_stored = sem("table_stored")
    onehots = [sem("onehots0"), sem("onehots1")]
    counted = [sem("counted0"), sem("counted1")]
    small_ready = sem("small_ready")
    small_done = sem("small_done")
    rows_out = sem("rows_out")
    ends_stored = sem("ends_stored")
    rowb_used = sem("rowb_used")
    rowb_loaded = sem("rowb_loaded")
    node_idx = sem("node_idx")
    zero_ready = sem("zero_ready")
    starts_zeroed = sem("starts_zeroed")
    ad_made = sem("ad_made")
    ad_stored = sem("ad_stored")
    ad_scattered = sem("ad_scattered")
    ad_loaded = sem("ad_loaded")
    ad_first = sem("ad_first")
    gathered_of = [[sem(f"gathered{s}_passes{c}") for s in range(2)] for c in range(0, 8, 4)]
    idx_ready = [sem("idx_ready0"), sem("idx_ready1")]
    block_done = [sem("block_done0"), sem("block_done1")]
    hist_stored = [sem("hist_stored0"), sem("hist_stored1")]
    ea_loaded = [sem("ea_loaded0"), sem("ea_loaded1")]
    eterm_ready = [sem("eterm_ready0"), sem("eterm_ready1")]
    exp_in = sem("exp_in")
    exp_done = sem("exp_done")
    sqrt_in = sem("sqrt_in")
    sqrt_done = sem("sqrt_done")
    end_gathered = sem("end_gathered")
    end_free = sem("end_free")
    turn = {e: sem(f"turn_{e}") for e in ("pe", "act", "dve", "pool")}
    dve_step = sem("dve_step")
    act_step = sem("act_step")
    out_stored = sem("out_stored")
    N_INPUTS = 0

    block = ctx.enter_context(nc.Block())
    vec_rows = [proj_b, ln_g, ln_b, m1_b, m2_b, s1_b, s2_b, g1_b, g2_b, g3_b]
    PB, LG, LB, B_M1, B_M2, B_S1, B_S2, B_G1, B_G2, B_G3 = range(10)

    input_loads = [(X[:, 0:NB - 1, :], x[0:(NB - 1) * P, :].rearrange("(b p) d -> p b d", p=P)),
                   (X[0:LAST, NB - 1, :], x[(NB - 1) * P:NODES, :]),
                   (SRC[:, :], src), (DST, dst), (PREV, dst_before),
                   (WR[:, 0, 0:SW].rearrange("k (h w) -> k h w", w=HW)[:, :, 0:HDIM],
                    att_W.rearrange("k (h w) -> k h w", w=HDIM)),
                   (attv[:, 0, :], att_src.rearrange("h k -> (h k)").partition_broadcast(DIM)),
                   (attv[:, 1, :], att_dst.rearrange("h k -> (h k)").partition_broadcast(DIM)),
                   (gbT[:, :], gat_bias.rearrange("(k a) -> k a", a=1)),
                   (WR[:, PROJ, 0:DIM], proj_WT),
                   (WR[:, MAX1, 0:DIM], m1_msg), (WR[:, MAX1, DIM:2 * DIM], m1_root),
                   (WR[:, MAX2, 0:DIM], m2_msg), (WR[:, MAX2, DIM:2 * DIM], m2_root),
                   (WE[:, 0, :], m1_edge), (WE[:, 1, :], m2_edge),
                   (WR[:, MEAN1, 0:DIM], s1_l), (WR[:, MEAN1, DIM:2 * DIM], s1_r),
                   (WR[:, MEAN2, 0:DIM], s2_l), (WR[:, MEAN2, DIM:2 * DIM], s2_r),
                   (WR[:, GCN1, 0:DIM], g1_W), (WR[:, GCN2, 0:DIM], g2_W), (WR[:, GCN3, 0:DIM], g3_W)]
    input_loads += [(rows[:, j, :], v.partition_broadcast(P)) for j, v in enumerate(vec_rows)]
    ALL_LOADED = 16 * len(input_loads)

    @block.gpsimd
    def _(pool):
        nc.gpsimd.memset(ident[:, :], 0.0).then_inc(turn["pool"], 1)
        nc.gpsimd.memset(upper[:, :], 1.0).then_inc(turn["pool"], 1)
        pool.wait_ge(turn["pool"], 2)
        nc.gpsimd.affine_select(out=ident[:, :], in_=ident[:, :], compare_op=ALU.not_equal, fill=1.0, base=0,
                                pattern=[[-1, P]], channel_multiplier=1).then_inc(consts_made, 1)
        nc.gpsimd.affine_select(out=upper[:, :], in_=upper[:, :], compare_op=ALU.is_gt, fill=0.0, base=0,
                                pattern=[[1, HI]], channel_multiplier=-1).then_inc(consts_made, 1)
        nc.gpsimd.iota(iota_i[:, :], pattern=[[1, P]], base=0, channel_multiplier=0).then_inc(consts_made, 1)
        nc.gpsimd.iota(bound_i[:, :], pattern=[[0, 1]], base=T, channel_multiplier=T).then_inc(consts_made, 1)

        pool.wait_ge(node_idx, 1)
        pool.wait_ge(ad_made, 1)
        pool.wait_ge(starts_zeroed, 16)
        for b in range(NB):
            pool.indirect_dma_start(out=ad_starts, out_offset=bass.IndirectOffsetOnAxis(ap=start_i[:, b:b + 1], axis=0),
                                    in_=ADN[:, b, :], in_offset=None,
                                    bounds_check=EPAD - 1, oob_is_err=False).then_inc(ad_scattered, 16)
        pool.wait_ge(ad_stored, 16)
        pool.wait_ge(ad_loaded, 16)
        pool.indirect_dma_start(out=AD[:, 0, :], out_offset=None, in_=ad_nodes,
                                in_offset=bass.IndirectOffsetOnAxis(ap=dst0[:, 0:1], axis=0)).then_inc(ad_first, 16)

        for q in range(8):
            tab = table0 if q == 0 else table
            rec = hist0 if q == 0 else hist
            width = W0 if q == 0 else DIM
            pool.wait_ge(table_stored, 16 * NG * (q + 1))
            with pool.Fori(0, ITERS) as i:
                for s in range(2):
                    pool.wait_ge(idx_ready[s], i + (q * ITERS + 1))
                    pool.sem_inc(turn["pool"], 1)
                    pool.wait_ge(block_done[s], i + (q * ITERS + 1))
                    pool.sem_inc(turn["pool"], 1)
                    for k in range(S):
                        pool.indirect_dma_start(
                            out=G[:, s, k * width:(k + 1) * width], out_offset=None, in_=tab,
                            in_offset=bass.IndirectOffsetOnAxis(ap=idx[:, s, k:k + 1], axis=0)).then_inc(
                                gathered_of[q // 4][s], 16)
            pool.wait_ge(hist_stored[0], 32 + 16 * ITERS * (q + 1))
            pool.wait_ge(hist_stored[1], 32 + 16 * ITERS * (q + 1))
            pool.wait_ge(end_free, q + 1)
            for b in range(NB):
                pool.indirect_dma_start(
                    out=EG[:, b * width:(b + 1) * width], out_offset=None, in_=rec,
                    in_offset=bass.IndirectOffsetOnAxis(ap=last_i[:, b:b + 1], axis=0)).then_inc(end_gathered, 16)

    @block.sync
    def _(sp):
        sp.wait_ge(pads_zeroed, 1)
        for a, b in input_loads:
            sp.dma_start(a, b).then_inc(inputs_loaded, 16)
        sp.wait_ge(filled, 1)
        hv0 = hist0.rearrange("(p t) w -> p (t w)", p=P)
        hv = hist.rearrange("(p t) w -> p (t w)", p=P)
        for s in range(2):
            sp.dma_start(hv0[:, s * S * W0:(s + 1) * S * W0], H[:, s, :]).then_inc(hist_stored[s], 16)
            sp.dma_start(hv[:, s * S * DIM:(s + 1) * S * DIM], H[:, s, 0:S * DIM]).then_inc(hist_stored[s], 16)
        sp.wait_ge(zero_ready, 1)
        sp.dma_start(ad_starts.rearrange("(p t) h -> p (t h)", p=P), SEL[:, :]).then_inc(starts_zeroed, 16)
        ea = edge_attr

        def store_table(q):
            tab = (table0 if q == 0 else table).rearrange("(b p) w -> p b w", p=P)
            tv = TB0 if q == 0 else TBW
            with sp.Fori(0, NG) as g:
                sp.wait_ge(table_made, g + (q * NG + 1))
                sp.dma_start(tab[:, bass.ds(g * GB, GB), :], tv[:, bass.ds(g * GB, GB), :]).then_inc(table_stored, 16)

        def edge_pass(q):
            rec = hv0 if q == 0 else hv
            width = W0 if q == 0 else DIM
            if q in MAX_PASSES:
                for s in range(2):
                    if q == MAX_PASSES[1]:
                        sp.wait_ge(eterm_ready[s], ITERS)
                    sp.dma_start(EA[:, s, :, :], ea[:, s * S:(s + 1) * S, :]).then_inc(ea_loaded[s], 16)

            def store(i, s):
                sp.wait_ge(block_done[s], i + (q * ITERS + 2))
                sp.dma_start(rec[:, bass.ds(i * (2 * S * width) + s * S * width, S * width)],
                             H[:, s, 0:S * width]).then_inc(hist_stored[s], 16)

            if q in MAX_PASSES:
                n0 = MAX_PASSES.index(q) * ITERS
                with sp.Fori(0, ITERS - 1) as i:
                    for s in range(2):
                        store(i, s)
                        sp.wait_ge(eterm_ready[s], i + (n0 + 1))
                        sp.dma_start(EA[:, s, :, :], ea[:, bass.ds(i * (2 * S) + (s * S + 2 * S), S), :]).then_inc(ea_loaded[s], 16)
                for s in range(2):
                    sp.wait_ge(block_done[s], (q + 1) * ITERS + 1)
                    sp.dma_start(rec[:, (T - 2 * S + s * S) * width:(T - 2 * S + s * S + S) * width],
                                 H[:, s, 0:S * width]).then_inc(hist_stored[s], 16)
            else:
                with sp.Fori(0, ITERS) as i:
                    for s in range(2):
                        store(i, s)

        store_table(0)
        sp.wait_ge(ad_made, 1)
        sp.dma_start(ad_nodes.rearrange("(b p) h -> p b h", p=P), ADN[:, :, :]).then_inc(ad_stored, 16)
        sp.wait_ge(rows_out, 1)
        sp.dma_start(last_row.rearrange("(a b) -> a b", b=P), lastf[:, :]).then_inc(ends_stored, 16)
        sp.dma_start(start_row.rearrange("(a b) -> a b", b=P), starts[:, :]).then_inc(ends_stored, 16)
        sp.wait_ge(ends_stored, 32)
        sp.dma_start(ROWB, last_row[0:NPAD].partition_broadcast(P)).then_inc(rowb_loaded, 16)
        sp.wait_ge(rowb_used, 1)
        sp.dma_start(ROWB, start_row[0:NPAD].partition_broadcast(P)).then_inc(rowb_loaded, 16)
        sp.wait_ge(rowb_used, 2)
        sp.wait_ge(ad_scattered, 16 * NB)
        sp.dma_start(ARENA[:, :], ad_starts.rearrange("(p t) h -> p (t h)", p=P)).then_inc(ad_loaded, 16)
        for q in range(8):
            if q > 0:
                store_table(q)
            edge_pass(q)
        sp.wait_ge(rows_ready, 9)
        sp.dma_start(out[0:(NB - 1) * P, :].rearrange("(b p) d -> p b d", p=P), X[:, 0:NB - 1, :]).then_inc(out_stored, 16)
        sp.dma_start(out[(NB - 1) * P:NODES, :], X[0:LAST, NB - 1, :]).then_inc(out_stored, 16)
        sp.wait_ge(out_stored, 32)

    @block.tensor
    def _(pe):
        def node_phase(f):
            cols = PHASE_COLS[f]
            base = out_group_base(f, "rows")
            with pe.Fori(0, NG) as g:
                pe.wait_ge(staged, g + (stage_base(f, "rows") + 1))
                pe.sem_inc(turn["pe"], 1)
                for j in range(GB):
                    mm = pe.transpose(psX[0:DIM, j * P:(j + 1) * P], STG[:, j * DIM:(j + 1) * DIM], ident[:, :])
                mm.then_inc(transposed, 1)
                pe.wait_ge(xt_copied, g + (f * NG + 1))
                pe.sem_inc(turn["pe"], 1)
                pe.wait_ge(out_used, g + (base + 1))
                pe.sem_inc(turn["pe"], 1)
                for j in range(GB):
                    mm = pe.matmul(OUTG[:, j, 0:cols], XT[:, j * P:(j + 1) * P], WR[:, f, 0:cols], start=True, stop=True)
                mm.then_inc(out_ready, 1)

        def edge_terms(q):
            n0 = MAX_PASSES.index(q) * ITERS
            pe.wait_ge(out_used, out_group_base({1: MAX1, 2: MAX2}[q], "carry") + 1)
            with pe.Fori(0, ITERS) as i:
                for s in range(2):
                    pe.wait_ge(ea_loaded[s], i * 16 + 16 * (n0 + 1))
                    pe.sem_inc(turn["pe"], 1)
                    pe.wait_ge(block_done[s], i + (q * ITERS + 1))
                    pe.sem_inc(turn["pe"], 1)
                    for k in range(S):
                        mm = pe.matmul(ETERM[:, s, k // 4, (k % 4) * DIM:(k % 4 + 1) * DIM], EA[:, s, k, :],
                                       WE[:, n0 // ITERS, :], start=True, stop=True)
                    mm.then_inc(eterm_ready[s], 1)

        small = [0]

        def carries(f, q):
            def wait_small():
                small[0] += 1
                pe.wait_ge(small_ready, small[0])
            wait_small()
            if q == 0:
                pe.transpose(psA[0:SW, 0:P], F0[:, 0:SW], ident[:, :])
                pe.transpose(psA[0:SW, P:2 * P], F0[:, W0:W0 + SW], ident[:, :]).then_inc(small_done, 1)
                wait_small()
                pe.transpose(psB[:, 0:SW], QT[:, 2, :], ident[0:SW, 0:SW])
                pe.transpose(psB[:, P:P + SW], QT[:, 0, :], ident[0:SW, 0:SW]).then_inc(small_done, 1)
            else:
                pe.transpose(psA[0:DIM, 0:P], HWD[:, 1, S - 1, :], ident[:, :]).then_inc(small_done, 1)
                wait_small()
                pe.transpose(psB[:, 0:DIM], QT[0:DIM, 0, :], ident[0:DIM, 0:DIM]).then_inc(small_done, 1)
            wait_small()
            width = W0 if q == 0 else DIM
            base = out_group_base(f, "carry")
            with pe.Fori(0, NG) as g:
                pe.wait_ge(out_used, g + (base + 1))
                pe.sem_inc(turn["pe"], 1)
                pe.wait_ge(staged, g + (stage_base(f, "carry") + 1))
                pe.sem_inc(turn["pe"], 1)
                for j in range(GB):
                    mm = pe.matmul(OUTG[:, j, 0:width], STG[:, j * P:(j + 1) * P], Q[:, 0:width],
                                   start=True, stop=True)
                mm.then_inc(out_ready, 1)

        pe.wait_ge(consts_made, 4)
        pe.wait_ge(weights_made, 1)
        node_phase(ATT)
        with pe.Fori(0, T // (2 * HB)) as i:
            for s in range(2):
                pe.wait_ge(onehots[s], i + 1)
                for k in range(HB):
                    mm = pe.matmul(psM[s][0:HI, 0:P], OHHI[:, s, k, :], OHLO[:, s, k, :], start=(k == 0), stop=(k == HB - 1))
                mm.then_inc(counted[s], 1)
        small[0] += 1
        pe.wait_ge(small_ready, small[0])
        pe.matmul(psA[0:HI, 0:1], upper[:, :], ends[:, P - 1:P], start=True, stop=True).then_inc(small_done, 1)
        small[0] += 1
        pe.wait_ge(small_ready, small[0])
        pe.transpose(psB[:, 0:HI], ends[:, :], ident[0:HI, 0:HI])
        pe.transpose(psB[:, HI:2 * HI], deg[:, :], ident[0:HI, 0:HI]).then_inc(small_done, 1)
        small[0] += 1
        pe.wait_ge(small_ready, small[0])
        pe.matmul(psA[0:W0, 0:P], ones[:, 0:W0], wdiag[:, :], start=True, stop=True).then_inc(small_done, 1)
        small[0] += 1
        pe.wait_ge(small_ready, small[0])
        for b in range(NB):
            mm = pe.matmul(psB[:, b:b + 1], SEL[:, b * P:(b + 1) * P], ones[:, 0:1], start=True, stop=True)
        mm.then_inc(small_done, 1)

        carries(ATT, 0)
        node_phase(PROJ)
        for f in (MAX1, MAX2, MEAN1, MEAN2, GCN1, GCN2, GCN3):
            q = PASS_OF_PHASE[f]
            node_phase(f)
            if q in MAX_PASSES:
                edge_terms(q)
            carries(f, q)

    @block.scalar
    def _(act):
        def node_phase(f):
            rowsrc = X if f in (ATT, MAX1, MEAN1, GCN1) else C
            if f > 0:
                act.wait_ge(rows_ready, f)
            act.wait_ge(out_ready, stage_base(f, "rows")) if f > 0 else None
            act.sem_inc(turn["act"], 1)
            with act.Fori(0, NG) as g:
                nc.scalar.copy(STG[:, 0:GB * DIM].rearrange("p (j d) -> p j d", d=DIM),
                               rowsrc[:, bass.ds(g * GB, GB), :]).then_inc(staged, 1)
                act.wait_ge(transposed, g + (f * NG + 1))
                if f == PROJ:
                    nc.scalar.activation(XT[:, :], psX[0:DIM, 0:GB * P], ACT.Identity, bias=gbT[:, 0:1]).then_inc(xt_copied, 1)
                else:
                    nc.scalar.copy(XT[:, :], psX[0:DIM, 0:GB * P]).then_inc(xt_copied, 1)

        def edge_pass(q):
            with act.Fori(0, ITERS - 1) as i:
                for s in range(2):
                    if q == 0:
                        act.wait_ge(exp_in, i * 2 + (s + 1))
                        nc.scalar.activation(EX[:, :, :, :], EX[:, :, :, :], ACT.Exp).then_inc(exp_done, 1)
                    act.wait_ge(gathered_of[q // 4][s], i * (16 * S) + 16 * S * (q % 4 * ITERS + 1))
                    act.sem_inc(turn["act"], 1)
                    nc.scalar.copy(idx[:, s, :], SRC[:, bass.ds(i * (2 * S) + (2 * S + s * S), S)]).then_inc(idx_ready[s], 1)
            for s in range(2):
                if q == 0:
                    act.wait_ge(exp_in, 2 * (ITERS - 1) + s + 1)
                    nc.scalar.activation(EX[:, :, :, :], EX[:, :, :, :], ACT.Exp).then_inc(exp_done, 1)
                if q < 7:
                    act.wait_ge(gathered_of[q // 4][s], 16 * S * ITERS * (q % 4 + 1))
                    nc.scalar.copy(idx[:, s, :], SRC[:, s * S:(s + 1) * S]).then_inc(idx_ready[s], 1)

        def carries(f):
            with act.Fori(0, NG) as g:
                act.wait_ge(out_ready, g + stage_base(f, "carry"))
                act.sem_inc(turn["act"], 1)
                nc.scalar.copy(STG[:, :], SEL[:, bass.ds(g * (GB * P), GB * P)]).then_inc(staged, 1)

        exps = [2 * ITERS]

        def exp(ap):
            exps[0] += 1
            act.wait_ge(exp_in, exps[0])
            nc.scalar.activation(ap, ap, ACT.Exp).then_inc(exp_done, 1)

        roots = [0]

        def root(ap):
            roots[0] += 1
            act.wait_ge(sqrt_in, roots[0])
            nc.scalar.activation(ap, ap, ACT.Sqrt).then_inc(sqrt_done, 1)

        act.wait_ge(inputs_loaded, ALL_LOADED)
        for s in range(2):
            nc.scalar.copy(idx[:, s, :], SRC[:, s * S:(s + 1) * S]).then_inc(idx_ready[s], 1)
        node_phase(ATT)
        root(dis[:, :])
        edge_pass(0)
        exp(QT[:, 1, :])
        exp(QT[:, 3, :])
        carries(ATT)
        exp(E3[:, :, :, :])
        node_phase(PROJ)
        root(stat[:, 1, :])
        root(stat[:, 1, :])
        for f in (MAX1, MAX2, MEAN1, MEAN2, GCN1, GCN2, GCN3):
            node_phase(f)
            edge_pass(PASS_OF_PHASE[f])
            carries(f)
            if f in (MAX2, MEAN2, GCN3):
                root(stat[:, 1, :])

    @block.vector
    def _(dve):
        steps = [0, 0]

        def link(ins):
            steps[0] += 1
            ins.then_inc(dve_step, 1)
            dve.wait_ge(dve_step, steps[1] + steps[0])

        def per(v, n, w):
            return v.unsqueeze(2).broadcast_to([P, n, w])

        def row(j, n):
            return rows[:, j:j + 1, :].broadcast_to([P, n, DIM])

        tt = nc.vector.tensor_tensor
        ts = nc.vector.tensor_scalar
        stt = nc.vector.scalar_tensor_tensor

        nc.vector.memset(X[96:P, NB - 1, :], 0.0).then_inc(pads_zeroed, 1)
        link(nc.vector.memset(H[:, :, :], 0.0))
        nc.vector.memset(zero64[:, :], 0.0).then_inc(filled, 1)
        link(nc.vector.memset(ones[:, :], 1.0))
        link(nc.vector.memset(onesrow[:, :], 0.0))
        link(nc.vector.memset(onesrow[:, HDIM:SW:HW], 1.0))
        link(nc.vector.memset(Rm[:, :, :], 0.0))
        link(nc.vector.memset(deg[:, :], 0.0))
        nc.vector.memset(SEL[:, :], 0.0).then_inc(zero_ready, 1)
        dve.wait_ge(consts_made, 4)
        link(nc.vector.tensor_copy(iota_b[:, :], iota_i[:, :]))
        link(nc.vector.tensor_copy(bound[:, 0:1], bound_i[:, :]))
        link(ts(bound[:, 1:2], bound[:, 0:1], float(T), None, ALU.add))

        dve.wait_ge(inputs_loaded, ALL_LOADED)
        link(nc.vector.memset(WR[:, ATT, HDIM:SW:HW], 0.0))
        for j, a in enumerate((0, 1)):
            link(tt(attp[:, a, :].rearrange("k (h w) -> k h w", w=HDIM),
                    WR[:, ATT, 0:SW].rearrange("k (h w) -> k h w", w=HW)[:, :, 0:HDIM],
                    attv[:, a, :].rearrange("k (h w) -> k h w", w=HDIM), ALU.mult))
            link(nc.vector.reduce_sum(WR[:, ATT, SW + a * HEADS:SW + (a + 1) * HEADS],
                                      attp[:, a, :].rearrange("k (h w) -> k h w", w=HDIM), AX.X))
        nc.vector.memset(U[:, :], 0.0).then_inc(weights_made, 1)
        dve.sem_inc(out_used, 1)
        dve.sem_inc(block_done[0], 1)
        dve.sem_inc(block_done[1], 1)

        link(nc.vector.tensor_copy(dst0[:, :], DST[:, 0:1]))
        link(tt(same[:, :], DST, PREV, ALU.is_equal))
        link(nc.vector.tensor_reduce(whole[:, :], same[:, :], AX.X, ALU.min))
        link(ts(wdiag[:, :], ident[:, :], whole[:, 0:1], None, ALU.mult))
        link(nc.vector.memset(same[:, 0:1], 0.0))
        link(ts(reset[:, :], same[:, :], -1.0, BIG, ALU.add, ALU.mult))
        link(ts(TMPI, DST, 7, None, ALU.logical_shift_right))
        link(nc.vector.tensor_copy(HIB, TMPI))
        link(ts(TMPI, DST, P - 1, None, ALU.bitwise_and))
        link(nc.vector.tensor_copy(LOB, TMPI))

        def node_rows(f):
            base = out_group_base(f, "rows")
            with dve.Fori(0, NG) as g:
                here = bass.ds(g * GB, GB)
                dve.wait_ge(out_ready, g + (base + 1))
                dve.sem_inc(turn["dve"], 1)
                if f == ATT:
                    tt(TB0[:, here, :], OUTG[:, :, 0:W0], onesrow[:, :].unsqueeze(1).broadcast_to([P, GB, W0]),
                       ALU.add).then_inc(table_made, 1)
                    ts(ADN[:, here, :], OUTG[:, :, W0:W0 + HEADS], 1.0, None, ALU.mult).then_inc(out_used, 1)
                elif f == PROJ:
                    tt(C[:, here, :], OUTG[:, :, 0:DIM], X[:, here, :], ALU.add).then_inc(out_used, 1)
                elif f in (MAX1, MAX2, MEAN1, MEAN2):
                    ts(TBW[:, here, :], OUTG[:, :, 0:DIM], 1.0, None, ALU.mult).then_inc(table_made, 1)
                    b = {MAX1: B_M1, MAX2: B_M2, MEAN1: B_S1, MEAN2: B_S2}[f]
                    tt(R[:, here, :], OUTG[:, :, DIM:2 * DIM], row(b, GB), ALU.add).then_inc(out_used, 1)
                else:
                    steps[0] += 1
                    base_step, steps[1] = steps[0], g
                    tt(TBW[:, here, :], OUTG[:, :, 0:DIM], dis[:, here].unsqueeze(2).broadcast_to([P, GB, DIM]),
                       ALU.mult).then_inc(table_made, 1)
                    steps[0] -= 1
                    steps[1] = 0
                    dve.wait_ge(table_made, g + (PASS_OF_PHASE[f] * NG + 1))
                    dve.sem_inc(out_used, 1)
            if f in PASS_OF_PHASE:
                dve.wait_ge(table_made, (PASS_OF_PHASE[f] + 1) * NG)
            dve.wait_ge(out_used, base + NG + 1)

        node_rows(ATT)
        dve.sem_inc(ad_made, 1)

        base = steps[0]
        with dve.Fori(0, T // (2 * HB)) as i:
            steps[1] = i * 4
            for s in range(2):
                here = bass.ds(i * (2 * HB) + s * HB, HB)
                for oh, key, m in ((OHHI, HIB, HI), (OHLO, LOB, P)):
                    ins = tt(oh[:, s, :, :], iota_b[:, 0:m].unsqueeze(1).broadcast_to([P, HB, m]),
                             key[:, here].unsqueeze(2).broadcast_to([P, HB, m]), ALU.is_equal)
                    if oh is OHHI:
                        link(ins)
                ins.then_inc(onehots[s], 1)
            for s in range(2):
                dve.wait_ge(counted[s], i + 1)
                link(tt(deg[:, :], deg[:, :], psM[s][0:HI, 0:P], ALU.add))
        steps[0] = base + 4 * (T // (2 * HB))
        steps[1] = 0

        link(nc.vector.tensor_tensor_scan(out=ends[:, :], data0=zero64[:, :], data1=deg[:, :], initial=0.0,
                                          op0=ALU.add, op1=ALU.add))
        dve.sem_inc(small_ready, 1)
        dve.wait_ge(small_done, 1)
        link(nc.vector.tensor_copy(offs[:, :], psA[0:HI, 0:1]))
        link(ts(ends[:, :], ends[:, :], offs[:, 0:1], None, ALU.add))
        link(tt(starts[:, :], ends[:, :], deg[:, :], ALU.subtract))
        link(ts(lastf[:, :], ends[:, :], -1.0, 0.0, ALU.add, ALU.max))
        dve.sem_inc(rows_out, 1)
        dve.sem_inc(small_ready, 1)
        dve.wait_ge(small_done, 2)
        link(nc.vector.tensor_copy(endN[:, :], psB[:, 0:HI]))
        link(nc.vector.tensor_copy(degN[:, :], psB[:, HI:2 * HI]))
        dve.sem_inc(small_ready, 1)
        link(ts(valid[:, :], degN[:, 0:NB], 1.0, None, ALU.min))
        link(ts(vpen[:, :], valid[:, :], -1.0, BIG, ALU.add, ALU.mult))
        link(ts(nf[:, :], endN[:, 0:NB], -1.0, 0.0, ALU.add, ALU.max))
        link(nc.vector.tensor_copy(last_i[:, :], nf[:, :]))
        link(tt(nf[:, :], endN[:, 0:NB], degN[:, 0:NB], ALU.subtract))
        link(stt(nf[:, :], valid[:, :], -float(2 * EPAD), nf[:, :], ALU.mult, ALU.add))
        link(ts(nf[:, :], nf[:, :], float(2 * EPAD), None, ALU.add))
        nc.vector.tensor_copy(start_i[:, :], nf[:, :]).then_inc(node_idx, 1)
        link(ts(rcnt[:, :], degN[:, 0:NB], 1.0, None, ALU.max))
        link(nc.vector.reciprocal(rcnt[:, :], rcnt[:, :]))
        link(ts(dis[:, :], degN[:, 0:NB], 1.0, None, ALU.add))
        roots = [1]
        dve.sem_inc(sqrt_in, 1)
        dve.wait_ge(sqrt_done, 1)
        link(nc.vector.reciprocal(dis[:, :], dis[:, :]))
        dve.wait_ge(small_done, 3)
        link(nc.vector.tensor_copy(wrow[:, :], psA[0:W0, 0:P]))
        link(ts(wneg[:, :], wrow[:, :], -1.0, BIG, ALU.add, ALU.mult))

        dve.wait_ge(rowb_loaded, 16)
        dve.wait_ge(starts_zeroed, 16)
        link(ts(SEL[:, :], ROWB, bound[:, 0:1], None, ALU.is_ge))
        link(stt(SEL[:, :], ROWB, bound[:, 1:2], SEL[:, :], ALU.is_lt, ALU.mult))
        dve.sem_inc(rowb_used, 1)
        dve.wait_ge(rowb_loaded, 32)
        link(stt(SEL[:, :], ROWB, bound[:, 0:1], SEL[:, :], ALU.is_lt, ALU.mult))
        dve.sem_inc(rowb_used, 1)
        dve.sem_inc(small_ready, 1)
        dve.wait_ge(small_done, 4)
        link(ts(cpen[:, :], psB[:, 0:NB], -1.0, BIG, ALU.add, ALU.mult))
        small = [4, 4]

        def small_sent():
            small[0] += 1
            dve.sem_inc(small_ready, 1)

        def small_got():
            small[1] += 1
            dve.wait_ge(small_done, small[1])

        dve.wait_ge(ad_first, 16)
        for h in range(HEADS):
            link(nc.vector.tensor_tensor_scan(out=AD[:, :, h], data0=same[:, :], data1=AD[:, :, h], initial=0.0,
                                              op0=ALU.mult, op1=ALU.add))

        def prev_state(view, s, k, w):
            return view[:, s, k - 1, 0:w] if k else view[:, 1 - s, S - 1, 0:w]

        def attention_pass():
            base = steps[0]
            with dve.Fori(0, ITERS) as i:
                for s in range(2):
                    here = bass.ds(i * (2 * S) + s * S, S)
                    steps[1] = i * (2 * ATT_LINKS)
                    dve.wait_ge(gathered_of[0][s], i * (16 * S) + 16 * S)
                    dve.sem_inc(turn["dve"], 1)
                    link(tt(Zs[:, :, :], G0[:, s, :, SW:W0], AD[:, here, :], ALU.add))
                    link(stt(Zs[:, :, :], Zs[:, :, :], 0.2, Zs[:, :, :], ALU.mult, ALU.max))
                    for h in range(HEADS):
                        link(nc.vector.tensor_tensor_scan(out=Rm[:, 1:S + 1, h], data0=reset[:, here], data1=Zs[:, :, h],
                                                          initial=Rm[:, 0:1, h], op0=ALU.add, op1=ALU.max))
                    link(tt(EX[:, 0, :, :], Rm[:, 0:S, :], reset[:, here].unsqueeze(2).broadcast_to([P, S, HEADS]), ALU.add))
                    link(tt(EX[:, 0, :, :], EX[:, 0, :, :], Rm[:, 1:S + 1, :], ALU.subtract))
                    link(tt(EX[:, 1, :, :], Zs[:, :, :], Rm[:, 1:S + 1, :], ALU.subtract))
                    dve.sem_inc(exp_in, 1)
                    dve.wait_ge(hist_stored[s], i * 16 + 32)
                    link(nc.vector.tensor_copy(H0[:, s, :, SW:W0], Rm[:, 1:S + 1, :]))
                    link(nc.vector.tensor_copy(Rm[:, 0, :], Rm[:, S, :]))
                    dve.wait_ge(exp_done, i * 2 + (s + 1))
                    link(tt(G0[:, s, :, 0:SW].rearrange("p k (h w) -> p k h w", w=HW),
                            G0[:, s, :, 0:SW].rearrange("p k (h w) -> p k h w", w=HW),
                            EX[:, 1, :, :].unsqueeze(3).broadcast_to([P, S, HEADS, HW]), ALU.mult))
                    for k in range(S):
                        link(tt(U[:, :].rearrange("p (h w) -> p h w", w=HW),
                                prev_state(H0, s, k, SW).rearrange("p (h w) -> p h w", w=HW),
                                EX[:, 0, k, :].unsqueeze(2).broadcast_to([P, HEADS, HW]), ALU.mult))
                        link(tt(H0[:, s, k, 0:SW], U[:, :], G0[:, s, k, 0:SW], ALU.add))
                    dve.sem_inc(block_done[s], 1)
                assert steps[0] - base == 2 * ATT_LINKS
            steps[0] = base + 2 * ATT_LINKS * ITERS
            steps[1] = 0

        ATT_LINKS = 2 + HEADS + 3 + 2 + 1 + 2 * S

        def running_pass(q):
            base = steps[0]
            biggest = q in MAX_PASSES
            mask, op0, op1 = (reset, ALU.add, ALU.max) if biggest else (same, ALU.mult, ALU.add)
            links = S + (2 if biggest else 0)
            with dve.Fori(0, ITERS) as i:
                for s in range(2):
                    steps[1] = i * (2 * links)
                    dve.wait_ge(gathered_of[q // 4][s], i * (16 * S) + 16 * S * (q % 4 * ITERS + 1))
                    dve.sem_inc(turn["dve"], 1)
                    if biggest:
                        dve.wait_ge(eterm_ready[s], i + (MAX_PASSES.index(q) * ITERS + 1))
                        for h in range(2):
                            ks = slice(4 * h, 4 * h + 4)
                            link(tt(GW[:, s, ks, :], GW[:, s, ks, :],
                                    ETERM[:, s, h, 0:4 * DIM].rearrange("p (k w) -> p k w", w=DIM), ALU.add))
                    dve.wait_ge(hist_stored[s], i * 16 + 16 * (q * ITERS + 2))
                    dve.sem_inc(turn["dve"], 1)
                    for k in range(S):
                        link(stt(HWD[:, s, k, :], prev_state(HWD, s, k, DIM), mask[:, bass.ds(i * (2 * S) + (s * S + k), 1)],
                                 GW[:, s, k, :], op0, op1))
                    dve.sem_inc(block_done[s], 1)
                assert steps[0] - base == 2 * links
            steps[0] = base + 2 * links * ITERS
            steps[1] = 0

        def carries(f, q):
            base = out_group_base(f, "carry")
            if q == 0:
                link(nc.vector.tensor_copy(F0[:, 0:SW], H0[:, 1, S - 1, 0:SW]))
                link(nc.vector.tensor_copy(F0[:, W0:W0 + SW].rearrange("p (h w) -> p h w", w=HW),
                                           H0[:, 1, S - 1, SW:W0].unsqueeze(2).broadcast_to([P, HEADS, HW])))
                small_sent()
                small_got()
                link(nc.vector.tensor_tensor_scan(out=QT[:, 0, :], data0=wneg[0:SW, :], data1=psA[0:SW, P:2 * P],
                                                  initial=0.0, op0=ALU.add, op1=ALU.max))
                link(nc.vector.tensor_copy(QT[:, 1, 0:1], wneg[0:SW, 0:1]))
                link(tt(QT[:, 1, 1:P], QT[:, 0, 0:P - 1], wneg[0:SW, 1:P], ALU.add))
                link(tt(QT[:, 1, 1:P], QT[:, 1, 1:P], QT[:, 0, 1:P], ALU.subtract))
                link(tt(QT[:, 3, :], psA[0:SW, P:2 * P], QT[:, 0, :], ALU.subtract))
                dve.sem_inc(exp_in, 2)
                dve.wait_ge(exp_done, 2 * ITERS + 2)
                link(tt(QT[:, 3, :], QT[:, 3, :], psA[0:SW, 0:P], ALU.mult))
                link(nc.vector.tensor_tensor_scan(out=QT[:, 2, :], data0=QT[:, 1, :], data1=QT[:, 3, :],
                                                  initial=0.0, op0=ALU.mult, op1=ALU.add))
                small_sent()
                small_got()
                link(nc.vector.tensor_copy(Q[:, 0:SW], psB[:, 0:SW]))
                link(nc.vector.tensor_copy(Q[:, SW:W0], psB[:, P:P + SW:HW]))
                small_sent()
            else:
                wm, op0, op1 = (wneg, ALU.add, ALU.max) if q in MAX_PASSES else (wrow, ALU.mult, ALU.add)
                small_sent()
                small_got()
                link(nc.vector.tensor_tensor_scan(out=QT[0:DIM, 0, :], data0=wm[0:DIM, :], data1=psA[0:DIM, 0:P],
                                                  initial=0.0, op0=op0, op1=op1))
                small_sent()
                small_got()
                link(nc.vector.tensor_copy(Q[:, 0:DIM], psB[:, 0:DIM]))
                small_sent()
                dve.wait_ge(end_gathered, 16 * NB * (q + 1))
                if q not in MAX_PASSES:
                    link(tt(EGW, EGW, per(valid[:, :], NB, DIM), ALU.mult))
            start = steps[0]
            with dve.Fori(0, NG) as g:
                steps[1] = g
                here = bass.ds(g * GB, GB)
                dve.wait_ge(out_ready, g + (base + 1))
                dve.sem_inc(turn["dve"], 1)
                if q == 0:
                    link(ts(CQ[:, here, :], OUTG[:, :, 0:W0], 1.0, None, ALU.mult))
                elif q in MAX_PASSES:
                    steps[1] = g * 2
                    link(tt(C[:, here, :], OUTG[:, :, 0:DIM],
                            cpen[:, here].unsqueeze(2).broadcast_to([P, GB, DIM]), ALU.add))
                    link(tt(EGW[:, here, :], EGW[:, here, :], C[:, here, :], ALU.max))
                else:
                    link(tt(EGW[:, here, :], EGW[:, here, :], OUTG[:, :, 0:DIM], ALU.add))
                dve.sem_inc(out_used, 1)
            steps[0] = start + (steps[0] - start) * NG
            steps[1] = 0
            if q in MAX_PASSES:
                link(tt(EGW, EGW, per(valid[:, :], NB, DIM), ALU.mult))

        def layernorm(V, tmp):
            link(nc.vector.reduce_sum(stat[:, 0, :], V, AX.X))
            link(ts(stat[:, 0, :], stat[:, 0, :], 1.0 / DIM, None, ALU.mult))
            link(tt(V, V, per(stat[:, 0, :], NB, DIM), ALU.subtract))
            link(tt(tmp, V, V, ALU.mult))
            link(nc.vector.reduce_sum(stat[:, 1, :], tmp, AX.X))
            link(ts(stat[:, 1, :], stat[:, 1, :], 1.0 / DIM, 1e-5, ALU.mult, ALU.add))
            roots[0] += 1
            dve.sem_inc(sqrt_in, 1)
            dve.wait_ge(sqrt_done, roots[0])
            link(nc.vector.reciprocal(stat[:, 1, :], stat[:, 1, :]))
            link(tt(V, V, per(stat[:, 1, :], NB, DIM), ALU.mult))

        def next_x():
            link(tt(X[:, :, :], X[:, :, :], EGW, ALU.add))
            layernorm(X[:, :, :], EGW)
            dve.sem_inc(rows_ready, 1)

        dve.sem_inc(end_free, 1)
        attention_pass()
        carries(ATT, 0)
        dve.wait_ge(end_gathered, 16 * NB)
        link(tt(zself[:, :, :], TB0[:, :, SW:W0], ADN[:, :, :], ALU.add))
        link(stt(zself[:, :, :], zself[:, :, :], 0.2, zself[:, :, :], ALU.mult, ALU.max))
        link(tt(EG0[:, :, SW:W0], EG0[:, :, SW:W0], per(vpen[:, :], NB, HEADS), ALU.add))
        link(tt(CQ[:, :, SW:W0], CQ[:, :, SW:W0], per(cpen[:, :], NB, HEADS), ALU.add))
        link(tt(mx[:, :, :], EG0[:, :, SW:W0], CQ[:, :, SW:W0], ALU.max))
        link(tt(mx[:, :, :], mx[:, :, :], zself[:, :, :], ALU.max))
        link(tt(E3[:, 0, :, :], EG0[:, :, SW:W0], mx[:, :, :], ALU.subtract))
        link(tt(E3[:, 1, :, :], CQ[:, :, SW:W0], mx[:, :, :], ALU.subtract))
        link(tt(E3[:, 2, :, :], zself[:, :, :], mx[:, :, :], ALU.subtract))
        dve.sem_inc(exp_in, 1)
        dve.wait_ge(exp_done, 2 * ITERS + 3)
        for j, V in enumerate((EG0, CQ, TB0)):
            Vh = V[:, :, 0:SW].rearrange("p b (h w) -> p b h w", w=HW)
            link(tt(Vh, Vh, E3[:, j, :, :].unsqueeze(3).broadcast_to([P, NB, HEADS, HW]), ALU.mult))
        link(tt(EG0[:, :, 0:SW], EG0[:, :, 0:SW], CQ[:, :, 0:SW], ALU.add))
        link(tt(EG0[:, :, 0:SW], EG0[:, :, 0:SW], TB0[:, :, 0:SW], ALU.add))
        link(nc.vector.reciprocal(rden[:, :, :], EG0[:, :, HDIM:SW:HW]))
        link(tt(C[:, :, :].rearrange("p b (h w) -> p b h w", w=HDIM),
                EG0[:, :, 0:SW].rearrange("p b (h w) -> p b h w", w=HW)[:, :, :, 0:HDIM],
                rden[:, :, :].unsqueeze(3).broadcast_to([P, NB, HEADS, HDIM]), ALU.mult))
        dve.sem_inc(rows_ready, 1)
        node_rows(PROJ)
        link(tt(C[:, :, :], C[:, :, :], row(PB, NB), ALU.add))
        layernorm(C[:, :, :], EGW)
        link(tt(C[:, :, :], C[:, :, :], row(LG, NB), ALU.mult))
        link(tt(EGW, C[:, :, :], row(LB, NB), ALU.add))
        next_x()

        for f in (MAX1, MAX2, MEAN1, MEAN2, GCN1, GCN2, GCN3):
            q = PASS_OF_PHASE[f]
            node_rows(f)
            dve.sem_inc(end_free, 1)
            running_pass(q)
            carries(f, q)
            if f in (MAX1, MAX2):
                link(tt(EGW, EGW, R, ALU.add))
                act_out = C[:, :, :] if f == MAX1 else EGW
                link(stt(act_out, EGW, 0.01, EGW, ALU.mult, ALU.max))
            elif f in (MEAN1, MEAN2):
                link(tt(EGW, EGW, per(rcnt[:, :], NB, DIM), ALU.mult))
                link(tt(EGW, EGW, R, ALU.add))
                if f == MEAN1:
                    link(ts(C[:, :, :], EGW, 0.0, None, ALU.max))
            else:
                link(tt(EGW, EGW, TBW, ALU.add))
                link(tt(EGW, EGW, per(dis[:, :], NB, DIM), ALU.mult))
                link(tt(EGW, EGW, row({GCN1: B_G1, GCN2: B_G2, GCN3: B_G3}[f], NB), ALU.add))
                if f != GCN3:
                    link(ts(C[:, :, :], EGW, 0.0, None, ALU.max))
            if f in (MAX2, MEAN2, GCN3):
                next_x()
            else:
                dve.sem_inc(rows_ready, 1)

    ctx.close()


_INS = ["x", "src", "dst", "dst_before", "edge_attr", "L0_gnn_W", "L0_gnn_att_src", "L0_gnn_att_dst",
        "L0_gnn_gat_bias", "L0_gnn_proj_WT", "L0_gnn_proj_b", "L0_gnn_ln_g", "L0_gnn_ln_b",
        "L1_gnn_W1_msg", "L1_gnn_W1_edge", "L1_gnn_W1_root", "L1_gnn_b1",
        "L1_gnn_W2_msg", "L1_gnn_W2_edge", "L1_gnn_W2_root", "L1_gnn_b2",
        "L2_gnn_W1_l", "L2_gnn_b1", "L2_gnn_W1_r", "L2_gnn_W2_l", "L2_gnn_b2", "L2_gnn_W2_r",
        "L3_gnn_W1", "L3_gnn_b1", "L3_gnn_W2", "L3_gnn_b2", "L3_gnn_W3", "L3_gnn_b3"]


def kernel(**inputs):
    import numpy as _np
    import concourse.bacc as _bacc
    from concourse import mybir as _mybir
    from concourse.bass_utils import run_bass_kernel_spmd as _run

    src = _np.zeros((EPAD,), _np.int32)
    src[:EDGES] = inputs["src"]
    dst = _np.full((EPAD + 1,), NODES, _np.int32)
    dst[1:EDGES + 1] = inputs["dst"]
    attr = _np.zeros((EPAD, EDGE_DIM), _np.float32)
    attr[:EDGES] = inputs["edge_attr_32"]
    laid = dict(inputs)
    laid["src"] = src.reshape(P, T)
    laid["dst"] = dst[1:].reshape(P, T)
    laid["dst_before"] = dst[:-1].reshape(P, T)
    laid["edge_attr"] = attr.reshape(P, T, EDGE_DIM).transpose(2, 1, 0)
    laid["L0_gnn_proj_WT"] = _np.asarray(inputs["L0_gnn_proj_W"]).T

    nc = _bacc.Bacc("TRN2", target_bir_lowering=False, num_devices=1)
    arrays, args = {}, []
    for name in _INS:
        a = _np.ascontiguousarray(laid[name])
        arrays[f"in_{name}"] = a
        args.append(nc.dram_tensor(f"in_{name}", a.shape, _mybir.dt.from_np(a.dtype), kind="ExternalInput").ap())
    args.append(nc.dram_tensor("out_0", (NODES, DIM), F32, kind="ExternalOutput").ap())
    build(nc, *args)
    r = _run(nc, [arrays], core_ids=[0])
    return r.results[0]["out_0"]
```

```python
from contextlib import ExitStack

import concourse.bass as bass
from concourse import mybir

P = 128
NODES = 6250
EDGES = 200000
DIM = 96
HEADS = 4
HDIM = DIM // HEADS
EDGE_DIM = 32
NB = -(-NODES // P)
NPAD = NB * P
LAST = NODES - (NB - 1) * P
GB = 7
NG = NB // GB
S = 8
T = -(-EDGES // (P * 2 * S)) * 2 * S
EPAD = P * T
ITERS = T // (2 * S)
HB = 16
HI = 64
HW = HDIM + 1
SW = HEADS * HW
W0 = SW + HEADS
BIG = 1e30
OUT_COLS = 256
CB = NB + 1
ROW = 64 * P
KC = 7
NK = NB // KC
CS = 4
COUNT_PASSES = (1, 2)
assert 2 * CS * ITERS * len(COUNT_PASSES) == T

F32 = mybir.dt.float32
I32 = mybir.dt.int32
BF16 = mybir.dt.bfloat16
ALU = mybir.AluOpType
ACT = mybir.ActivationFunctionType
AX = mybir.AxisListType

ATT, PROJ, MAX1, MAX2, MEAN1, MEAN2, GCN1, GCN2, GCN3 = range(9)
PHASE_COLS = [W0 + HEADS, DIM] + [2 * DIM] * 4 + [DIM] * 3
PASS_OF_PHASE = {ATT: 0, MAX1: 1, MAX2: 2, MEAN1: 3, MEAN2: 4, GCN1: 5, GCN2: 6, GCN3: 7}
GATHER_PASSES = 3
MAX_PASSES = (1, 2)


def out_group_base(phase, kind):
    n = 0
    for f in range(9):
        if f == phase and kind == "rows":
            return n
        n += NG
        if f in PASS_OF_PHASE:
            if f == phase:
                return n
            n += NG


stage_base = out_group_base


def build(nc, x, src, dst, dst_before, edge_attr, att_W, att_src, att_dst, gat_bias, proj_WT, proj_b, ln_g, ln_b,
          m1_msg, m1_edge, m1_root, m1_b, m2_msg, m2_edge, m2_root, m2_b,
          s1_l, s1_b, s1_r, s2_l, s2_b, s2_r, g1_W, g1_b, g2_W, g2_b, g3_W, g3_b, out):
    ctx = ExitStack()

    def sb(name, shape, dt=F32, stack=ctx):
        return stack.enter_context(nc.sbuf_tensor(name, shape, dt))

    def sem(name):
        return ctx.enter_context(nc.semaphore(name))

    table0 = nc.dram_tensor("table0", (NPAD, W0), F32, kind="Internal").ap()
    table = nc.dram_tensor("table", (NPAD, DIM), F32, kind="Internal").ap()
    hist0 = nc.dram_tensor("hist0", (EPAD, W0), F32, kind="Internal").ap()
    hist = nc.dram_tensor("hist", (EPAD, DIM), F32, kind="Internal").ap()
    counts = nc.dram_tensor("counts", (CB * P, ROW), F32, kind="Internal").ap()
    ad_nodes = nc.dram_tensor("ad_nodes", (NPAD, HEADS), F32, kind="Internal").ap()
    ad_starts = nc.dram_tensor("ad_starts", (EPAD, HEADS), F32, kind="Internal").ap()
    last_row = nc.dram_tensor("last_row", (HI * P,), F32, kind="Internal").ap()
    start_row = nc.dram_tensor("start_row", (HI * P,), F32, kind="Internal").ap()

    X = sb("X", [P, NB, DIM])
    C = sb("C", [P, NB, DIM])
    TB = sb("TB", [P, NB * W0])
    TB0 = TB[:, :].rearrange("p (b w) -> p b w", w=W0)
    TBW = TB[:, 0:NB * DIM].rearrange("p (b w) -> p b w", w=DIM)
    EG = sb("EG", [P, NB * W0])
    EG0 = EG[:, :].rearrange("p (b w) -> p b w", w=W0)
    EGD = EG[:, 0:CB * DIM].rearrange("p (b w) -> p b w", w=DIM)
    EGW = EG[:, 0:NB * DIM].rearrange("p (b w) -> p b w", w=DIM)
    ARENA = sb("ARENA", [P, T * HEADS])
    AD = ARENA[:, :].rearrange("p (t h) -> p t h", h=HEADS)
    ROWB = ARENA[:, 0:NPAD]
    R = ARENA[:, 0:NB * DIM].rearrange("p (b w) -> p b w", w=DIM)
    CQ = ARENA[:, 0:NB * W0].rearrange("p (b w) -> p b w", w=W0)
    SEL = sb("SEL", [P, NPAD])
    EDG = sb("EDG", [P, 4, T])
    SRC, CELL = EDG[:, 0, :].bitcast(I32), EDG[:, 3, :].bitcast(I32)
    same, reset = EDG[:, 1, :], EDG[:, 2, :]
    CNT = EDG[:, :, :].rearrange("p a t -> p (a t)").rearrange("p (c k m) -> p c k m", c=NK, k=KC)
    G = sb("G", [P, 2, S * W0])
    H = sb("H", [P, 2, S * W0])
    G0 = G[:, :, :].rearrange("p s (k w) -> p s k w", w=W0)
    H0 = H[:, :, :].rearrange("p s (k w) -> p s k w", w=W0)
    GW = G[:, :, 0:S * DIM].rearrange("p s (k w) -> p s k w", w=DIM)
    HWD = H[:, :, 0:S * DIM].rearrange("p s (k w) -> p s k w", w=DIM)
    EAZ = sb("EAZ", [P, 2 * S * P])
    EA = EAZ[0:EDGE_DIM, :].rearrange("p (s k m) -> p s k m", s=2, k=S)
    cidx = sb("cidx", [P, 2, CS], I32)
    count_one = sb("count_one", [P, 2])
    lead = sb("lead", [P, 1])
    chunk_f = sb("chunk_f", [P, 1])
    chunk_i = sb("chunk_i", [P, 1], I32)
    idx = sb("idx", [P, 2, S], I32)
    Zs = sb("Zs", [P, S, HEADS])
    Rm = sb("Rm", [P, S + 1, HEADS])
    EX = sb("EX", [P, 2, S, HEADS])
    U = sb("U", [P, SW])
    WR = sb("WR", [DIM, 9, 2 * DIM])
    WE = sb("WE", [EDGE_DIM, 2, DIM])
    attv = sb("attv", [DIM, 2, DIM])
    attp = sb("attp", [DIM, 2, DIM])
    gbT = sb("gbT", [DIM, 1])
    rows = sb("rows", [P, 10, DIM])
    XT = sb("XT", [DIM, GB * P])
    STG = sb("STG", [P, GB * P])
    ident = sb("ident", [P, P])
    upper = sb("upper", [HI, HI])
    ones = sb("ones", [P, P])
    onesrow = sb("onesrow", [P, W0])
    iota_i = sb("iota_i", [P, P], I32)
    bound_i = sb("bound_i", [P, 1], I32)
    iota_b = sb("iota_b", [P, P], BF16)
    bound = sb("bound", [P, 2])
    whole = sb("whole", [P, 1])
    wdiag = sb("wdiag", [P, P])
    wrow = sb("wrow", [W0, P])
    wneg = sb("wneg", [W0, P])
    deg = sb("deg", [HI, P])
    zero64 = sb("zero64", [HI, P])
    ends = sb("ends", [HI, P])
    starts = sb("starts", [HI, P])
    lastf = sb("lastf", [HI, P])
    offs = sb("offs", [HI, 1])
    degN = sb("degN", [P, HI])
    endN = sb("endN", [P, HI])
    valid = sb("valid", [P, NB])
    vpen = sb("vpen", [P, NB])
    cpen = sb("cpen", [P, NB])
    rcnt = sb("rcnt", [P, NB])
    dis = sb("dis", [P, NB])
    nf = sb("nf", [P, NB])
    last_i = sb("last_i", [P, NB], I32)
    start_i = sb("start_i", [P, NB], I32)
    ADN = sb("ADN", [P, NB, HEADS])
    small_G = G[:, :, :].rearrange("p s w -> p (s w)")[:, 0:6 * NB * HEADS].rearrange("p (a b h) -> p a b h", a=6, h=HEADS)
    E3, zself, mx, rden = small_G[:, 0:3], small_G[:, 3], small_G[:, 4], small_G[:, 5]
    stat = sb("stat", [P, 2, NB])
    dst0 = sb("dst0", [P, 1], I32)
    F0 = sb("F0", [P, W0 + SW])
    QT = sb("QT", [SW, 4, P])
    Q = sb("Q", [P, W0])
    LEADS = ARENA[:, 0:T]
    COLF = ARENA[:, T:2 * T]
    COLI = ARENA[:, 2 * T:3 * T].bitcast(I32)
    NODE_IOTA = ARENA[:, 0:NPAD].bitcast(I32)
    DST = C[:, :, :].rearrange("p b d -> p (b d)")[:, 0:T].bitcast(I32)
    PREV = C[:, :, :].rearrange("p b d -> p (b d)")[:, T:2 * T].bitcast(I32)
    HILO = C[:, :, :].rearrange("p b d -> p (b d)")[:, 2 * T:3 * T].bitcast(BF16)
    HIB, LOB = HILO[:, 0:T], HILO[:, T:2 * T]
    TMPI = EG[:, 0:T].bitcast(I32)
    OH = EG[:, T:T + HB * (HI + P)].bitcast(BF16)
    OHHI = OH[:, 0:2 * HB * HI].rearrange("p (s k m) -> p s k m", s=2, k=HB)
    OHLO = OH[:, 2 * HB * HI:2 * HB * (HI + P)].rearrange("p (s k m) -> p s k m", s=2, k=HB)

    psX = ctx.enter_context(nc.psum_tensor("psX", [P, 1024], F32))
    psO = ctx.enter_context(nc.psum_tensor("psO", [P, 2048], F32))
    psA = ctx.enter_context(nc.psum_tensor("psA", [P, 512], F32))
    psB = ctx.enter_context(nc.psum_tensor("psB", [P, 512], F32))
    OUTG = psO[:, 0:GB * OUT_COLS].rearrange("p (j c) -> p j c", c=OUT_COLS)
    ETERM = psO[:, :].rearrange("p (s b c) -> p s b c", s=2, b=2)
    psM = [psA, psB]

    inputs_loaded = sem("inputs_loaded")
    pads_zeroed = sem("pads_zeroed")
    consts_made = sem("consts_made")
    filled = sem("filled")
    weights_made = sem("weights_made")
    rows_ready = sem("rows_ready")
    staged = sem("staged")
    transposed = sem("transposed")
    xt_copied = sem("xt_copied")
    out_ready = sem("out_ready")
    out_used = sem("out_used")
    table_made = sem("table_made")
    table_stored = sem("table_stored")
    onehots = [sem("onehots0"), sem("onehots1")]
    counted = [sem("counted0"), sem("counted1")]
    small_ready = sem("small_ready")
    small_done = sem("small_done")
    rows_out = sem("rows_out")
    ends_stored = sem("ends_stored")
    rowb_used = sem("rowb_used")
    rowb_loaded = sem("rowb_loaded")
    node_idx = sem("node_idx")
    zero_ready = sem("zero_ready")
    starts_zeroed = sem("starts_zeroed")
    ad_made = sem("ad_made")
    ad_stored = sem("ad_stored")
    ad_scattered = sem("ad_scattered")
    ad_loaded = sem("ad_loaded")
    ad_first = sem("ad_first")
    gathered = [sem("gathered0"), sem("gathered1")]
    counts_zeroed = sem("counts_zeroed")
    counted_edges = sem("counted_edges")
    cells_ready = [sem("cells_ready0"), sem("cells_ready1")]
    piece_loaded = [sem(f"piece_loaded{c}") for c in range(NK)]
    pieces_used = sem("pieces_used")
    sums_ready = [sem("sums_ready0"), sem("sums_ready1")]
    sums_used = [sem("sums_used0"), sem("sums_used1")]
    iota_wanted = sem("iota_wanted")
    iota_made = sem("iota_made")
    idx_ready = [sem("idx_ready0"), sem("idx_ready1")]
    block_done = [sem("block_done0"), sem("block_done1")]
    hist_stored = [sem("hist_stored0"), sem("hist_stored1")]
    ea_loaded = [sem("ea_loaded0"), sem("ea_loaded1")]
    eterm_ready = [sem("eterm_ready0"), sem("eterm_ready1")]
    exp_in = sem("exp_in")
    exp_done = sem("exp_done")
    sqrt_in = sem("sqrt_in")
    sqrt_done = sem("sqrt_done")
    end_gathered = sem("end_gathered")
    end_free = sem("end_free")
    turn = {e: sem(f"turn_{e}") for e in ("pe", "act", "dve", "pool")}
    dve_step = sem("dve_step")
    act_step = sem("act_step")
    out_stored = sem("out_stored")
    N_INPUTS = 0

    block = ctx.enter_context(nc.Block())
    vec_rows = [proj_b, ln_g, ln_b, m1_b, m2_b, s1_b, s2_b, g1_b, g2_b, g3_b]
    PB, LG, LB, B_M1, B_M2, B_S1, B_S2, B_G1, B_G2, B_G3 = range(10)

    input_loads = [(X[:, 0:NB - 1, :], x[0:(NB - 1) * P, :].rearrange("(b p) d -> p b d", p=P)),
                   (X[0:LAST, NB - 1, :], x[(NB - 1) * P:NODES, :]),
                   (SRC[:, :], src), (DST, dst), (PREV, dst_before),
                   (WR[:, 0, 0:SW].rearrange("k (h w) -> k h w", w=HW)[:, :, 0:HDIM],
                    att_W.rearrange("k (h w) -> k h w", w=HDIM)),
                   (attv[:, 0, :], att_src.rearrange("h k -> (h k)").partition_broadcast(DIM)),
                   (attv[:, 1, :], att_dst.rearrange("h k -> (h k)").partition_broadcast(DIM)),
                   (gbT[:, :], gat_bias.rearrange("(k a) -> k a", a=1)),
                   (WR[:, PROJ, 0:DIM], proj_WT),
                   (WR[:, MAX1, 0:DIM], m1_msg), (WR[:, MAX1, DIM:2 * DIM], m1_root),
                   (WR[:, MAX2, 0:DIM], m2_msg), (WR[:, MAX2, DIM:2 * DIM], m2_root),
                   (WE[:, 0, :], m1_edge), (WE[:, 1, :], m2_edge),
                   (WR[:, MEAN1, 0:DIM], s1_l), (WR[:, MEAN1, DIM:2 * DIM], s1_r),
                   (WR[:, MEAN2, 0:DIM], s2_l), (WR[:, MEAN2, DIM:2 * DIM], s2_r),
                   (WR[:, GCN1, 0:DIM], g1_W), (WR[:, GCN2, 0:DIM], g2_W), (WR[:, GCN3, 0:DIM], g3_W)]
    input_loads += [(rows[:, j, :], v.partition_broadcast(P)) for j, v in enumerate(vec_rows)]
    ALL_LOADED = 16 * len(input_loads)

    @block.gpsimd
    def _(pool):
        nc.gpsimd.memset(ident[:, :], 0.0).then_inc(turn["pool"], 1)
        nc.gpsimd.memset(upper[:, :], 1.0).then_inc(turn["pool"], 1)
        pool.wait_ge(turn["pool"], 2)
        nc.gpsimd.affine_select(out=ident[:, :], in_=ident[:, :], compare_op=ALU.not_equal, fill=1.0, base=0,
                                pattern=[[-1, P]], channel_multiplier=1).then_inc(consts_made, 1)
        nc.gpsimd.affine_select(out=upper[:, :], in_=upper[:, :], compare_op=ALU.is_gt, fill=0.0, base=0,
                                pattern=[[1, HI]], channel_multiplier=-1).then_inc(consts_made, 1)
        nc.gpsimd.iota(iota_i[:, :], pattern=[[1, P]], base=0, channel_multiplier=0).then_inc(consts_made, 1)
        nc.gpsimd.iota(bound_i[:, :], pattern=[[0, 1]], base=T, channel_multiplier=T).then_inc(consts_made, 1)
        nc.gpsimd.iota(chunk_i[:, :], pattern=[[0, 1]], base=0, channel_multiplier=1).then_inc(consts_made, 1)

        pool.wait_ge(node_idx, 1)
        pool.wait_ge(ad_made, 1)
        pool.wait_ge(starts_zeroed, 16)
        for b in range(NB):
            pool.indirect_dma_start(out=ad_starts, out_offset=bass.IndirectOffsetOnAxis(ap=start_i[:, b:b + 1], axis=0),
                                    in_=ADN[:, b, :], in_offset=None,
                                    bounds_check=EPAD - 1, oob_is_err=False).then_inc(ad_scattered, 16)
        pool.wait_ge(ad_stored, 16)
        pool.wait_ge(ad_loaded, 16)
        pool.indirect_dma_start(out=AD[:, 0, :], out_offset=None, in_=ad_nodes,
                                in_offset=bass.IndirectOffsetOnAxis(ap=dst0[:, 0:1], axis=0)).then_inc(ad_first, 16)

        count_cells = counts.rearrange("r (c o) -> (r c) o", o=1)

        def count_edges(column, cells):
            pool.indirect_dma_start(out=count_cells, out_offset=bass.IndirectOffsetOnAxis(ap=cells, axis=0),
                                    in_=count_one[:, column:column + 1], in_offset=None,
                                    compute_op=ALU.add).then_inc(counted_edges, 16)

        for q in range(GATHER_PASSES):
            tab = table0 if q == 0 else table
            rec = hist0 if q == 0 else hist
            width = W0 if q == 0 else DIM
            pool.wait_ge(table_stored, 16 * NG * (q + 1))
            if q == COUNT_PASSES[0]:
                pool.wait_ge(counts_zeroed, 16 * 2 * CB)
                pool.wait_ge(cells_ready[0], 1)
                count_edges(0, cidx[:, 0, 0:1])
            with pool.Fori(0, ITERS) as i:
                for s in range(2):
                    if q in COUNT_PASSES:
                        n0 = COUNT_PASSES.index(q) * ITERS
                        pool.wait_ge(cells_ready[s], i + (n0 + 1))
                        pool.sem_inc(turn["pool"], 1)
                    pool.wait_ge(idx_ready[s], i + (q * ITERS + 1))
                    pool.sem_inc(turn["pool"], 1)
                    pool.wait_ge(block_done[s], i + (q * ITERS + 1))
                    pool.sem_inc(turn["pool"], 1)
                    for k in range(S):
                        pool.indirect_dma_start(
                            out=G[:, s, k * width:(k + 1) * width], out_offset=None, in_=tab,
                            in_offset=bass.IndirectOffsetOnAxis(ap=idx[:, s, k:k + 1], axis=0)).then_inc(
                                gathered[s], 16)
                        if q in COUNT_PASSES and k % 2 == 1:
                            pool.wait_ge(counted_edges, i * (16 * 2 * CS) + 16 * (n0 * 2 * CS + s * CS + k // 2 + 1))
                            pool.sem_inc(turn["pool"], 1)
                            count_edges(1, cidx[:, s, k // 2:k // 2 + 1])
            pool.wait_ge(hist_stored[0], 32 + 16 * ITERS * (q + 1))
            pool.wait_ge(hist_stored[1], 32 + 16 * ITERS * (q + 1))
            pool.wait_ge(end_free, q + 1)
            for b in range(NB):
                pool.indirect_dma_start(
                    out=EG[:, b * width:(b + 1) * width], out_offset=None, in_=rec,
                    in_offset=bass.IndirectOffsetOnAxis(ap=last_i[:, b:b + 1], axis=0)).then_inc(end_gathered, 16)
        pool.wait_ge(iota_wanted, 1)
        nc.gpsimd.iota(NODE_IOTA, pattern=[[1, NPAD]], base=0, channel_multiplier=0).then_inc(iota_made, 1)

    @block.sync
    def _(sp):
        sp.wait_ge(pads_zeroed, 1)
        for a, b in input_loads:
            sp.dma_start(a, b).then_inc(inputs_loaded, 16)
        sp.wait_ge(filled, 1)
        hv0 = hist0.rearrange("(p t) w -> p (t w)", p=P)
        hv = hist.rearrange("(p t) w -> p (t w)", p=P)
        for s in range(2):
            sp.dma_start(hv0[:, s * S * W0:(s + 1) * S * W0], H[:, s, :]).then_inc(hist_stored[s], 16)
            sp.dma_start(hv[:, s * S * DIM:(s + 1) * S * DIM], H[:, s, 0:S * DIM]).then_inc(hist_stored[s], 16)
        sp.wait_ge(zero_ready, 1)
        sp.dma_start(ad_starts.rearrange("(p t) h -> p (t h)", p=P), SEL[:, :]).then_inc(starts_zeroed, 16)
        ea = edge_attr

        def store_table(q):
            tab = (table0 if q == 0 else table).rearrange("(b p) w -> p b w", p=P)
            tv = TB0 if q == 0 else TBW
            with sp.Fori(0, NG) as g:
                sp.wait_ge(table_made, g + (q * NG + 1))
                sp.dma_start(tab[:, bass.ds(g * GB, GB), :], tv[:, bass.ds(g * GB, GB), :]).then_inc(table_stored, 16)

        def edge_pass(q):
            rec = hv0 if q == 0 else hv
            width = W0 if q == 0 else DIM
            if q in MAX_PASSES:
                sp.wait_ge(counts_zeroed, 16 * 2 * CB)
                for s in range(2):
                    if q == MAX_PASSES[1]:
                        sp.wait_ge(eterm_ready[s], ITERS)
                    sp.dma_start(EA[:, s, :, :], ea[:, s * S:(s + 1) * S, :]).then_inc(ea_loaded[s], 16)

            def store(i, s):
                sp.wait_ge(block_done[s], i + (q * ITERS + 2))
                sp.dma_start(rec[:, bass.ds(i * (2 * S * width) + s * S * width, S * width)],
                             H[:, s, 0:S * width]).then_inc(hist_stored[s], 16)

            if q in MAX_PASSES:
                n0 = MAX_PASSES.index(q) * ITERS
                with sp.Fori(0, ITERS - 1) as i:
                    for s in range(2):
                        store(i, s)
                        sp.wait_ge(eterm_ready[s], i + (n0 + 1))
                        sp.dma_start(EA[:, s, :, :], ea[:, bass.ds(i * (2 * S) + (s * S + 2 * S), S), :]).then_inc(ea_loaded[s], 16)
                for s in range(2):
                    sp.wait_ge(block_done[s], (q + 1) * ITERS + 1)
                    sp.dma_start(rec[:, (T - 2 * S + s * S) * width:(T - 2 * S + s * S + S) * width],
                                 H[:, s, 0:S * width]).then_inc(hist_stored[s], 16)
            else:
                with sp.Fori(0, ITERS) as i:
                    for s in range(2):
                        store(i, s)

        store_table(0)
        sp.wait_ge(ad_made, 1)
        sp.dma_start(ad_nodes.rearrange("(b p) h -> p b h", p=P), ADN[:, :, :]).then_inc(ad_stored, 16)
        sp.wait_ge(rows_out, 1)
        sp.dma_start(last_row.rearrange("(a b) -> a b", b=P), lastf[:, :]).then_inc(ends_stored, 16)
        sp.dma_start(start_row.rearrange("(a b) -> a b", b=P), starts[:, :]).then_inc(ends_stored, 16)
        sp.wait_ge(ends_stored, 32)
        sp.dma_start(ROWB, last_row[0:NPAD].partition_broadcast(P)).then_inc(rowb_loaded, 16)
        sp.wait_ge(rowb_used, 1)
        sp.dma_start(ROWB, start_row[0:NPAD].partition_broadcast(P)).then_inc(rowb_loaded, 16)
        sp.wait_ge(rowb_used, 2)
        sp.wait_ge(ad_scattered, 16 * NB)
        sp.dma_start(ARENA[:, :], ad_starts.rearrange("(p t) h -> p (t h)", p=P)).then_inc(ad_loaded, 16)
        for q in range(GATHER_PASSES):
            if q > 0:
                store_table(q)
            edge_pass(q)
        sp.wait_ge(counted_edges, 16 * (T + 1))
        sp.wait_ge(rows_ready, MEAN1)
        blocks = counts.rearrange("(b p) c -> b p c", p=P)
        for n in range(8 - GATHER_PASSES):
            with sp.Fori(0, CB) as b:
                for c in range(NK):
                    sp.wait_ge(pieces_used, b * NK + (n * CB * NK + c + 1))
                    sp.dma_start(CNT[:, c, :, :].rearrange("p k m -> p (k m)"),
                                 blocks[bass.ds(b, 1), :, c * KC * P:(c + 1) * KC * P].rearrange("a p c -> (a p) c")
                                 ).then_inc(piece_loaded[c], 16)
        sp.wait_ge(rows_ready, 9)
        sp.dma_start(out[0:(NB - 1) * P, :].rearrange("(b p) d -> p b d", p=P), X[:, 0:NB - 1, :]).then_inc(out_stored, 16)
        sp.dma_start(out[(NB - 1) * P:NODES, :], X[0:LAST, NB - 1, :]).then_inc(out_stored, 16)
        sp.wait_ge(out_stored, 32)

    @block.tensor
    def _(pe):
        def node_phase(f):
            cols = PHASE_COLS[f]
            base = out_group_base(f, "rows")
            with pe.Fori(0, NG) as g:
                pe.wait_ge(staged, g + (stage_base(f, "rows") + 1))
                pe.sem_inc(turn["pe"], 1)
                for j in range(GB):
                    mm = pe.transpose(psX[0:DIM, j * P:(j + 1) * P], STG[:, j * DIM:(j + 1) * DIM], ident[:, :])
                mm.then_inc(transposed, 1)
                pe.wait_ge(xt_copied, g + (f * NG + 1))
                pe.sem_inc(turn["pe"], 1)
                pe.wait_ge(out_used, g + (base + 1))
                pe.sem_inc(turn["pe"], 1)
                for j in range(GB):
                    mm = pe.matmul(OUTG[:, j, 0:cols], XT[:, j * P:(j + 1) * P], WR[:, f, 0:cols], start=True, stop=True)
                mm.then_inc(out_ready, 1)

        def edge_terms(q):
            n0 = MAX_PASSES.index(q) * ITERS
            pe.wait_ge(out_used, out_group_base({1: MAX1, 2: MAX2}[q], "carry") + 1)
            with pe.Fori(0, ITERS) as i:
                for s in range(2):
                    pe.wait_ge(ea_loaded[s], i * 16 + 16 * (n0 + 1))
                    pe.sem_inc(turn["pe"], 1)
                    pe.wait_ge(block_done[s], i + (q * ITERS + 1))
                    pe.sem_inc(turn["pe"], 1)
                    for k in range(S):
                        mm = pe.matmul(ETERM[:, s, k // 4, (k % 4) * DIM:(k % 4 + 1) * DIM], EA[:, s, k, :],
                                       WE[:, n0 // ITERS, :], start=True, stop=True)
                    mm.then_inc(eterm_ready[s], 1)

        def sum_by_counts(n):
            pe.wait_ge(table_made, (n + GATHER_PASSES + 1) * NG)
            with pe.Fori(0, CB // 2) as i:
                for half in range(2):
                    pe.wait_ge(sums_used[half], i + (n * CB // 2 + 1))
                    pe.sem_inc(turn["pe"], 1)
                    for c in range(NK):
                        pe.wait_ge(piece_loaded[c], i * 32 + 16 * (n * CB + half + 1))
                        for k in range(KC):
                            b = c * KC + k
                            mm = pe.matmul(psM[half][:, 0:DIM], CNT[:, c, k, :], TBW[:, b, :],
                                           start=(b == 0), stop=(b == NB - 1))
                        if c < NK - 1:
                            mm.then_inc(pieces_used, 1)
                    mm.then_inc(sums_ready[half], 1)
                    pe.wait_ge(sums_ready[half], i + (n * CB // 2 + 1))
                    pe.sem_inc(pieces_used, 1)

        def spread_leads(f):
            small[0] += 1
            pe.wait_ge(small_ready, small[0])
            base = out_group_base(f, "carry")
            with pe.Fori(0, NG) as g:
                pe.wait_ge(out_used, g + (base + 1))
                pe.sem_inc(turn["pe"], 1)
                pe.wait_ge(staged, g + (stage_base(f, "carry") + 1))
                pe.sem_inc(turn["pe"], 1)
                for j in range(GB):
                    mm = pe.matmul(OUTG[:, j, 0:DIM], STG[:, j * P:(j + 1) * P], EGD[:, 0, :], start=True, stop=True)
                mm.then_inc(out_ready, 1)

        small = [0]

        def carries(f, q):
            def wait_small():
                small[0] += 1
                pe.wait_ge(small_ready, small[0])
            wait_small()
            if q == 0:
                pe.transpose(psA[0:SW, 0:P], F0[:, 0:SW], ident[:, :])
                pe.transpose(psA[0:SW, P:2 * P], F0[:, W0:W0 + SW], ident[:, :]).then_inc(small_done, 1)
                wait_small()
                pe.transpose(psB[:, 0:SW], QT[:, 2, :], ident[0:SW, 0:SW])
                pe.transpose(psB[:, P:P + SW], QT[:, 0, :], ident[0:SW, 0:SW]).then_inc(small_done, 1)
            else:
                pe.transpose(psA[0:DIM, 0:P], HWD[:, 1, S - 1, :], ident[:, :]).then_inc(small_done, 1)
                wait_small()
                pe.transpose(psB[:, 0:DIM], QT[0:DIM, 0, :], ident[0:DIM, 0:DIM]).then_inc(small_done, 1)
            wait_small()
            width = W0 if q == 0 else DIM
            base = out_group_base(f, "carry")
            with pe.Fori(0, NG) as g:
                pe.wait_ge(out_used, g + (base + 1))
                pe.sem_inc(turn["pe"], 1)
                pe.wait_ge(staged, g + (stage_base(f, "carry") + 1))
                pe.sem_inc(turn["pe"], 1)
                for j in range(GB):
                    mm = pe.matmul(OUTG[:, j, 0:width], STG[:, j * P:(j + 1) * P], Q[:, 0:width],
                                   start=True, stop=True)
                mm.then_inc(out_ready, 1)

        pe.wait_ge(consts_made, 5)
        pe.wait_ge(weights_made, 1)
        node_phase(ATT)
        with pe.Fori(0, T // (2 * HB)) as i:
            for s in range(2):
                pe.wait_ge(onehots[s], i + 1)
                for k in range(HB):
                    mm = pe.matmul(psM[s][0:HI, 0:P], OHHI[:, s, k, :], OHLO[:, s, k, :], start=(k == 0), stop=(k == HB - 1))
                mm.then_inc(counted[s], 1)
        small[0] += 1
        pe.wait_ge(small_ready, small[0])
        pe.matmul(psA[0:HI, 0:1], upper[:, :], ends[:, P - 1:P], start=True, stop=True).then_inc(small_done, 1)
        small[0] += 1
        pe.wait_ge(small_ready, small[0])
        pe.transpose(psB[:, 0:HI], ends[:, :], ident[0:HI, 0:HI])
        pe.transpose(psB[:, HI:2 * HI], deg[:, :], ident[0:HI, 0:HI]).then_inc(small_done, 1)
        small[0] += 1
        pe.wait_ge(small_ready, small[0])
        pe.matmul(psA[0:W0, 0:P], ones[:, 0:W0], wdiag[:, :], start=True, stop=True).then_inc(small_done, 1)
        small[0] += 1
        pe.wait_ge(small_ready, small[0])
        for b in range(NB):
            mm = pe.matmul(psB[:, b:b + 1], SEL[:, b * P:(b + 1) * P], ones[:, 0:1], start=True, stop=True)
        mm.then_inc(small_done, 1)

        carries(ATT, 0)
        node_phase(PROJ)
        for f in (MAX1, MAX2, MEAN1, MEAN2, GCN1, GCN2, GCN3):
            q = PASS_OF_PHASE[f]
            node_phase(f)
            if q in MAX_PASSES:
                edge_terms(q)
                carries(f, q)
            else:
                sum_by_counts(q - GATHER_PASSES)
                spread_leads(f)

    @block.scalar
    def _(act):
        small_of_leads = 4 + 3 * GATHER_PASSES + 1

        def node_phase(f):
            rowsrc = X if f in (ATT, MAX1, MEAN1, GCN1) else C
            if f > 0:
                act.wait_ge(rows_ready, f)
            act.wait_ge(out_ready, stage_base(f, "rows")) if f > 0 else None
            act.sem_inc(turn["act"], 1)
            with act.Fori(0, NG) as g:
                nc.scalar.copy(STG[:, 0:GB * DIM].rearrange("p (j d) -> p j d", d=DIM),
                               rowsrc[:, bass.ds(g * GB, GB), :]).then_inc(staged, 1)
                act.wait_ge(transposed, g + (f * NG + 1))
                if f == PROJ:
                    nc.scalar.activation(XT[:, :], psX[0:DIM, 0:GB * P], ACT.Identity, bias=gbT[:, 0:1]).then_inc(xt_copied, 1)
                else:
                    nc.scalar.copy(XT[:, :], psX[0:DIM, 0:GB * P]).then_inc(xt_copied, 1)

        def zero_counts(rows64):
            act.dma_start(counts[rows64, 0:NB * P].rearrange("p (a c) -> p a c", a=NK),
                          EAZ[0:64, 0:KC * P].unsqueeze(1).broadcast_to([64, NK, KC * P])).then_inc(counts_zeroed, 16)

        def cell_columns(first, s):
            nc.scalar.copy(cidx[:, s, :], CELL[:, first]).then_inc(cells_ready[s], 1)

        def edge_pass(q):
            if q == COUNT_PASSES[0]:
                for s in range(2):
                    cell_columns(slice(s * CS, (s + 1) * CS), s)
            with act.Fori(0, ITERS - 1) as i:
                if q == 0:
                    zero_counts(bass.ds(i * 64, 64))
                for s in range(2):
                    if q == 0:
                        act.wait_ge(exp_in, i * 2 + (s + 1))
                        nc.scalar.activation(EX[:, :, :, :], EX[:, :, :, :], ACT.Exp).then_inc(exp_done, 1)
                    act.wait_ge(gathered[s], i * (16 * S) + 16 * S * (q * ITERS + 1))
                    act.sem_inc(turn["act"], 1)
                    nc.scalar.copy(idx[:, s, :], SRC[:, bass.ds(i * (2 * S) + (2 * S + s * S), S)]).then_inc(idx_ready[s], 1)
                    if q in COUNT_PASSES:
                        n0 = COUNT_PASSES.index(q) * ITERS
                        act.wait_ge(counted_edges, i * (16 * 2 * CS) + 16 * (n0 * 2 * CS + (s + 1) * CS + 1))
                        act.sem_inc(turn["act"], 1)
                        cell_columns(bass.ds(i * (2 * CS) + ((n0 + 1) * 2 * CS + s * CS), CS), s)
            if q == 0:
                for r in range(ITERS - 1, 2 * CB):
                    zero_counts(slice(r * 64, (r + 1) * 64))
            for s in range(2):
                if q == 0:
                    act.wait_ge(exp_in, 2 * (ITERS - 1) + s + 1)
                    nc.scalar.activation(EX[:, :, :, :], EX[:, :, :, :], ACT.Exp).then_inc(exp_done, 1)
                if q < GATHER_PASSES - 1:
                    act.wait_ge(gathered[s], 16 * S * ITERS * (q + 1))
                    nc.scalar.copy(idx[:, s, :], SRC[:, s * S:(s + 1) * S]).then_inc(idx_ready[s], 1)
                if q == COUNT_PASSES[0]:
                    act.wait_ge(counted_edges, 16 * ((ITERS - 1) * 2 * CS + (s + 1) * CS + 1))
                    cell_columns(slice(ITERS * 2 * CS + s * CS, ITERS * 2 * CS + (s + 1) * CS), s)

        def carries(f):
            with act.Fori(0, NG) as g:
                act.wait_ge(out_ready, g + stage_base(f, "carry"))
                act.sem_inc(turn["act"], 1)
                nc.scalar.copy(STG[:, :], SEL[:, bass.ds(g * (GB * P), GB * P)]).then_inc(staged, 1)

        exps = [2 * ITERS]

        def exp(ap):
            exps[0] += 1
            act.wait_ge(exp_in, exps[0])
            nc.scalar.activation(ap, ap, ACT.Exp).then_inc(exp_done, 1)

        roots = [0]

        def root(ap):
            roots[0] += 1
            act.wait_ge(sqrt_in, roots[0])
            nc.scalar.activation(ap, ap, ACT.Sqrt).then_inc(sqrt_done, 1)

        act.wait_ge(inputs_loaded, ALL_LOADED)
        for s in range(2):
            nc.scalar.copy(idx[:, s, :], SRC[:, s * S:(s + 1) * S]).then_inc(idx_ready[s], 1)
        node_phase(ATT)
        root(dis[:, :])
        edge_pass(0)
        exp(QT[:, 1, :])
        exp(QT[:, 3, :])
        carries(ATT)
        exp(E3[:, :, :, :])
        node_phase(PROJ)
        root(stat[:, 1, :])
        root(stat[:, 1, :])
        for f in (MAX1, MAX2, MEAN1, MEAN2, GCN1, GCN2, GCN3):
            node_phase(f)
            if PASS_OF_PHASE[f] < GATHER_PASSES:
                edge_pass(PASS_OF_PHASE[f])
            elif f == MEAN1:
                act.wait_ge(small_ready, small_of_leads)
            carries(f)
            if f in (MAX2, MEAN2, GCN3):
                root(stat[:, 1, :])

    @block.vector
    def _(dve):
        steps = [0, 0]

        def link(ins):
            steps[0] += 1
            ins.then_inc(dve_step, 1)
            dve.wait_ge(dve_step, steps[1] + steps[0])

        def per(v, n, w):
            return v.unsqueeze(2).broadcast_to([P, n, w])

        def row(j, n):
            return rows[:, j:j + 1, :].broadcast_to([P, n, DIM])

        tt = nc.vector.tensor_tensor
        ts = nc.vector.tensor_scalar
        stt = nc.vector.scalar_tensor_tensor

        nc.vector.memset(X[96:P, NB - 1, :], 0.0).then_inc(pads_zeroed, 1)
        link(nc.vector.memset(H[:, :, :], 0.0))
        nc.vector.memset(zero64[:, :], 0.0).then_inc(filled, 1)
        link(nc.vector.memset(EAZ[:, :], 0.0))
        link(nc.vector.memset(count_one[:, 0:1], 0.0))
        link(nc.vector.memset(count_one[:, 1:2], 1.0))
        link(nc.vector.memset(ones[:, :], 1.0))
        link(nc.vector.memset(onesrow[:, :], 0.0))
        link(nc.vector.memset(onesrow[:, HDIM:SW:HW], 1.0))
        link(nc.vector.memset(Rm[:, :, :], 0.0))
        link(nc.vector.memset(deg[:, :], 0.0))
        nc.vector.memset(SEL[:, :], 0.0).then_inc(zero_ready, 1)
        dve.wait_ge(consts_made, 5)
        link(nc.vector.tensor_copy(iota_b[:, :], iota_i[:, :]))
        link(nc.vector.tensor_copy(bound[:, 0:1], bound_i[:, :]))
        link(nc.vector.tensor_copy(chunk_f[:, :], chunk_i[:, :]))
        link(ts(chunk_f[:, :], chunk_f[:, :], -float(P), None, ALU.add))
        link(ts(bound[:, 1:2], bound[:, 0:1], float(T), None, ALU.add))

        dve.wait_ge(inputs_loaded, ALL_LOADED)
        link(nc.vector.memset(WR[:, ATT, HDIM:SW:HW], 0.0))
        for j, a in enumerate((0, 1)):
            link(tt(attp[:, a, :].rearrange("k (h w) -> k h w", w=HDIM),
                    WR[:, ATT, 0:SW].rearrange("k (h w) -> k h w", w=HW)[:, :, 0:HDIM],
                    attv[:, a, :].rearrange("k (h w) -> k h w", w=HDIM), ALU.mult))
            link(nc.vector.reduce_sum(WR[:, ATT, SW + a * HEADS:SW + (a + 1) * HEADS],
                                      attp[:, a, :].rearrange("k (h w) -> k h w", w=HDIM), AX.X))
        nc.vector.memset(U[:, :], 0.0).then_inc(weights_made, 1)
        dve.sem_inc(out_used, 1)
        dve.sem_inc(block_done[0], 1)
        dve.sem_inc(block_done[1], 1)
        dve.sem_inc(pieces_used, NK)
        dve.sem_inc(sums_used[0], 1)
        dve.sem_inc(sums_used[1], 1)

        link(nc.vector.tensor_copy(dst0[:, :], DST[:, 0:1]))
        link(tt(same[:, :], DST, PREV, ALU.is_equal))
        link(nc.vector.tensor_reduce(whole[:, :], same[:, :], AX.X, ALU.min))
        link(ts(wdiag[:, :], ident[:, :], whole[:, 0:1], None, ALU.mult))
        link(nc.vector.tensor_tensor_scan(out=LEADS, data0=same[:, :], data1=same[:, :], initial=1.0,
                                          op0=ALU.mult, op1=ALU.mult))
        link(nc.vector.tensor_copy(lead[:, :], DST[:, 0:1]))
        link(stt(lead[:, :], lead[:, :], 1.0, same[:, 0:1], ALU.add, ALU.mult))
        link(ts(lead[:, :], lead[:, :], -1.0, None, ALU.add))
        link(ts(COLF, DST, -1.0, chunk_f[:, 0:1], ALU.mult, ALU.add))
        link(tt(COLF, COLF, LEADS, ALU.mult))
        link(tt(COLF, COLF, DST, ALU.add))
        link(ts(COLI, COLF, float(P), None, ALU.add))
        link(ts(CELL, COLI, 7, 20, ALU.logical_shift_right, ALU.logical_shift_left))
        link(ts(COLI, COLI, P - 1, None, ALU.bitwise_and))
        link(tt(CELL, CELL, COLI, ALU.bitwise_or))
        link(ts(COLI, SRC, P - 1, 13, ALU.bitwise_and, ALU.logical_shift_left))
        link(tt(CELL, CELL, COLI, ALU.bitwise_or))
        link(ts(COLI, SRC, (HI - 1) * P, None, ALU.bitwise_and))
        link(tt(CELL, CELL, COLI, ALU.bitwise_or))
        link(nc.vector.memset(same[:, 0:1], 0.0))
        link(ts(reset[:, :], same[:, :], -1.0, BIG, ALU.add, ALU.mult))
        link(ts(TMPI, DST, 7, None, ALU.logical_shift_right))
        link(nc.vector.tensor_copy(HIB, TMPI))
        link(ts(TMPI, DST, P - 1, None, ALU.bitwise_and))
        link(nc.vector.tensor_copy(LOB, TMPI))

        def node_rows(f):
            base = out_group_base(f, "rows")
            with dve.Fori(0, NG) as g:
                here = bass.ds(g * GB, GB)
                dve.wait_ge(out_ready, g + (base + 1))
                dve.sem_inc(turn["dve"], 1)
                if f == ATT:
                    tt(TB0[:, here, :], OUTG[:, :, 0:W0], onesrow[:, :].unsqueeze(1).broadcast_to([P, GB, W0]),
                       ALU.add).then_inc(table_made, 1)
                    ts(ADN[:, here, :], OUTG[:, :, W0:W0 + HEADS], 1.0, None, ALU.mult).then_inc(out_used, 1)
                elif f == PROJ:
                    tt(C[:, here, :], OUTG[:, :, 0:DIM], X[:, here, :], ALU.add).then_inc(out_used, 1)
                elif f in (MAX1, MAX2, MEAN1, MEAN2):
                    ts(TBW[:, here, :], OUTG[:, :, 0:DIM], 1.0, None, ALU.mult).then_inc(table_made, 1)
                    b = {MAX1: B_M1, MAX2: B_M2, MEAN1: B_S1, MEAN2: B_S2}[f]
                    tt(R[:, here, :], OUTG[:, :, DIM:2 * DIM], row(b, GB), ALU.add).then_inc(out_used, 1)
                else:
                    steps[0] += 1
                    base_step, steps[1] = steps[0], g
                    tt(TBW[:, here, :], OUTG[:, :, 0:DIM], dis[:, here].unsqueeze(2).broadcast_to([P, GB, DIM]),
                       ALU.mult).then_inc(table_made, 1)
                    steps[0] -= 1
                    steps[1] = 0
                    dve.wait_ge(table_made, g + (PASS_OF_PHASE[f] * NG + 1))
                    dve.sem_inc(out_used, 1)
            if f in PASS_OF_PHASE:
                dve.wait_ge(table_made, (PASS_OF_PHASE[f] + 1) * NG)
            dve.wait_ge(out_used, base + NG + 1)

        node_rows(ATT)
        dve.sem_inc(ad_made, 1)

        base = steps[0]
        with dve.Fori(0, T // (2 * HB)) as i:
            steps[1] = i * 4
            for s in range(2):
                here = bass.ds(i * (2 * HB) + s * HB, HB)
                for oh, key, m in ((OHHI, HIB, HI), (OHLO, LOB, P)):
                    ins = tt(oh[:, s, :, :], iota_b[:, 0:m].unsqueeze(1).broadcast_to([P, HB, m]),
                             key[:, here].unsqueeze(2).broadcast_to([P, HB, m]), ALU.is_equal)
                    if oh is OHHI:
                        link(ins)
                ins.then_inc(onehots[s], 1)
            for s in range(2):
                dve.wait_ge(counted[s], i + 1)
                link(tt(deg[:, :], deg[:, :], psM[s][0:HI, 0:P], ALU.add))
        steps[0] = base + 4 * (T // (2 * HB))
        steps[1] = 0

        link(nc.vector.tensor_tensor_scan(out=ends[:, :], data0=zero64[:, :], data1=deg[:, :], initial=0.0,
                                          op0=ALU.add, op1=ALU.add))
        dve.sem_inc(small_ready, 1)
        dve.wait_ge(small_done, 1)
        link(nc.vector.tensor_copy(offs[:, :], psA[0:HI, 0:1]))
        link(ts(ends[:, :], ends[:, :], offs[:, 0:1], None, ALU.add))
        link(tt(starts[:, :], ends[:, :], deg[:, :], ALU.subtract))
        link(ts(lastf[:, :], ends[:, :], -1.0, 0.0, ALU.add, ALU.max))
        dve.sem_inc(rows_out, 1)
        dve.sem_inc(small_ready, 1)
        dve.wait_ge(small_done, 2)
        link(nc.vector.tensor_copy(endN[:, :], psB[:, 0:HI]))
        link(nc.vector.tensor_copy(degN[:, :], psB[:, HI:2 * HI]))
        dve.sem_inc(small_ready, 1)
        link(ts(valid[:, :], degN[:, 0:NB], 1.0, None, ALU.min))
        link(ts(vpen[:, :], valid[:, :], -1.0, BIG, ALU.add, ALU.mult))
        link(ts(nf[:, :], endN[:, 0:NB], -1.0, 0.0, ALU.add, ALU.max))
        link(nc.vector.tensor_copy(last_i[:, :], nf[:, :]))
        link(tt(nf[:, :], endN[:, 0:NB], degN[:, 0:NB], ALU.subtract))
        link(stt(nf[:, :], valid[:, :], -float(2 * EPAD), nf[:, :], ALU.mult, ALU.add))
        link(ts(nf[:, :], nf[:, :], float(2 * EPAD), None, ALU.add))
        nc.vector.tensor_copy(start_i[:, :], nf[:, :]).then_inc(node_idx, 1)
        link(ts(rcnt[:, :], degN[:, 0:NB], 1.0, None, ALU.max))
        link(nc.vector.reciprocal(rcnt[:, :], rcnt[:, :]))
        link(ts(dis[:, :], degN[:, 0:NB], 1.0, None, ALU.add))
        roots = [1]
        dve.sem_inc(sqrt_in, 1)
        dve.wait_ge(sqrt_done, 1)
        link(nc.vector.reciprocal(dis[:, :], dis[:, :]))
        dve.wait_ge(small_done, 3)
        link(nc.vector.tensor_copy(wrow[:, :], psA[0:W0, 0:P]))
        link(ts(wneg[:, :], wrow[:, :], -1.0, BIG, ALU.add, ALU.mult))

        dve.wait_ge(rowb_loaded, 16)
        dve.wait_ge(starts_zeroed, 16)
        link(ts(SEL[:, :], ROWB, bound[:, 0:1], None, ALU.is_ge))
        link(stt(SEL[:, :], ROWB, bound[:, 1:2], SEL[:, :], ALU.is_lt, ALU.mult))
        dve.sem_inc(rowb_used, 1)
        dve.wait_ge(rowb_loaded, 32)
        link(stt(SEL[:, :], ROWB, bound[:, 0:1], SEL[:, :], ALU.is_lt, ALU.mult))
        dve.sem_inc(rowb_used, 1)
        dve.sem_inc(small_ready, 1)
        dve.wait_ge(small_done, 4)
        link(ts(cpen[:, :], psB[:, 0:NB], -1.0, BIG, ALU.add, ALU.mult))
        small = [4, 4]

        def small_sent():
            small[0] += 1
            dve.sem_inc(small_ready, 1)

        def small_got():
            small[1] += 1
            dve.wait_ge(small_done, small[1])

        dve.wait_ge(ad_first, 16)
        for h in range(HEADS):
            link(nc.vector.tensor_tensor_scan(out=AD[:, :, h], data0=same[:, :], data1=AD[:, :, h], initial=0.0,
                                              op0=ALU.mult, op1=ALU.add))

        def prev_state(view, s, k, w):
            return view[:, s, k - 1, 0:w] if k else view[:, 1 - s, S - 1, 0:w]

        def attention_pass():
            base = steps[0]
            with dve.Fori(0, ITERS) as i:
                for s in range(2):
                    here = bass.ds(i * (2 * S) + s * S, S)
                    steps[1] = i * (2 * ATT_LINKS)
                    dve.wait_ge(gathered[s], i * (16 * S) + 16 * S)
                    dve.sem_inc(turn["dve"], 1)
                    link(tt(Zs[:, :, :], G0[:, s, :, SW:W0], AD[:, here, :], ALU.add))
                    link(stt(Zs[:, :, :], Zs[:, :, :], 0.2, Zs[:, :, :], ALU.mult, ALU.max))
                    for h in range(HEADS):
                        link(nc.vector.tensor_tensor_scan(out=Rm[:, 1:S + 1, h], data0=reset[:, here], data1=Zs[:, :, h],
                                                          initial=Rm[:, 0:1, h], op0=ALU.add, op1=ALU.max))
                    link(tt(EX[:, 0, :, :], Rm[:, 0:S, :], reset[:, here].unsqueeze(2).broadcast_to([P, S, HEADS]), ALU.add))
                    link(tt(EX[:, 0, :, :], EX[:, 0, :, :], Rm[:, 1:S + 1, :], ALU.subtract))
                    link(tt(EX[:, 1, :, :], Zs[:, :, :], Rm[:, 1:S + 1, :], ALU.subtract))
                    dve.sem_inc(exp_in, 1)
                    dve.wait_ge(hist_stored[s], i * 16 + 32)
                    link(nc.vector.tensor_copy(H0[:, s, :, SW:W0], Rm[:, 1:S + 1, :]))
                    link(nc.vector.tensor_copy(Rm[:, 0, :], Rm[:, S, :]))
                    dve.wait_ge(exp_done, i * 2 + (s + 1))
                    link(tt(G0[:, s, :, 0:SW].rearrange("p k (h w) -> p k h w", w=HW),
                            G0[:, s, :, 0:SW].rearrange("p k (h w) -> p k h w", w=HW),
                            EX[:, 1, :, :].unsqueeze(3).broadcast_to([P, S, HEADS, HW]), ALU.mult))
                    for k in range(S):
                        link(tt(U[:, :].rearrange("p (h w) -> p h w", w=HW),
                                prev_state(H0, s, k, SW).rearrange("p (h w) -> p h w", w=HW),
                                EX[:, 0, k, :].unsqueeze(2).broadcast_to([P, HEADS, HW]), ALU.mult))
                        link(tt(H0[:, s, k, 0:SW], U[:, :], G0[:, s, k, 0:SW], ALU.add))
                    dve.sem_inc(block_done[s], 1)
                assert steps[0] - base == 2 * ATT_LINKS
            steps[0] = base + 2 * ATT_LINKS * ITERS
            steps[1] = 0

        ATT_LINKS = 2 + HEADS + 3 + 2 + 1 + 2 * S

        def running_pass(q):
            base = steps[0]
            biggest = q in MAX_PASSES
            mask, op0, op1 = (reset, ALU.add, ALU.max) if biggest else (same, ALU.mult, ALU.add)
            links = S + (2 if biggest else 0)
            with dve.Fori(0, ITERS) as i:
                for s in range(2):
                    steps[1] = i * (2 * links)
                    dve.wait_ge(gathered[s], i * (16 * S) + 16 * S * (q * ITERS + 1))
                    dve.sem_inc(turn["dve"], 1)
                    if biggest:
                        dve.wait_ge(eterm_ready[s], i + (MAX_PASSES.index(q) * ITERS + 1))
                        for h in range(2):
                            ks = slice(4 * h, 4 * h + 4)
                            link(tt(GW[:, s, ks, :], GW[:, s, ks, :],
                                    ETERM[:, s, h, 0:4 * DIM].rearrange("p (k w) -> p k w", w=DIM), ALU.add))
                    dve.wait_ge(hist_stored[s], i * 16 + 16 * (q * ITERS + 2))
                    dve.sem_inc(turn["dve"], 1)
                    for k in range(S):
                        link(stt(HWD[:, s, k, :], prev_state(HWD, s, k, DIM), mask[:, bass.ds(i * (2 * S) + (s * S + k), 1)],
                                 GW[:, s, k, :], op0, op1))
                    dve.sem_inc(block_done[s], 1)
                assert steps[0] - base == 2 * links
            steps[0] = base + 2 * links * ITERS
            steps[1] = 0

        def carries(f, q):
            base = out_group_base(f, "carry")
            if q == 0:
                link(nc.vector.tensor_copy(F0[:, 0:SW], H0[:, 1, S - 1, 0:SW]))
                link(nc.vector.tensor_copy(F0[:, W0:W0 + SW].rearrange("p (h w) -> p h w", w=HW),
                                           H0[:, 1, S - 1, SW:W0].unsqueeze(2).broadcast_to([P, HEADS, HW])))
                small_sent()
                small_got()
                link(nc.vector.tensor_tensor_scan(out=QT[:, 0, :], data0=wneg[0:SW, :], data1=psA[0:SW, P:2 * P],
                                                  initial=0.0, op0=ALU.add, op1=ALU.max))
                link(nc.vector.tensor_copy(QT[:, 1, 0:1], wneg[0:SW, 0:1]))
                link(tt(QT[:, 1, 1:P], QT[:, 0, 0:P - 1], wneg[0:SW, 1:P], ALU.add))
                link(tt(QT[:, 1, 1:P], QT[:, 1, 1:P], QT[:, 0, 1:P], ALU.subtract))
                link(tt(QT[:, 3, :], psA[0:SW, P:2 * P], QT[:, 0, :], ALU.subtract))
                dve.sem_inc(exp_in, 2)
                dve.wait_ge(exp_done, 2 * ITERS + 2)
                link(tt(QT[:, 3, :], QT[:, 3, :], psA[0:SW, 0:P], ALU.mult))
                link(nc.vector.tensor_tensor_scan(out=QT[:, 2, :], data0=QT[:, 1, :], data1=QT[:, 3, :],
                                                  initial=0.0, op0=ALU.mult, op1=ALU.add))
                small_sent()
                small_got()
                link(nc.vector.tensor_copy(Q[:, 0:SW], psB[:, 0:SW]))
                link(nc.vector.tensor_copy(Q[:, SW:W0], psB[:, P:P + SW:HW]))
                small_sent()
            else:
                wm, op0, op1 = (wneg, ALU.add, ALU.max) if q in MAX_PASSES else (wrow, ALU.mult, ALU.add)
                small_sent()
                small_got()
                link(nc.vector.tensor_tensor_scan(out=QT[0:DIM, 0, :], data0=wm[0:DIM, :], data1=psA[0:DIM, 0:P],
                                                  initial=0.0, op0=op0, op1=op1))
                small_sent()
                small_got()
                link(nc.vector.tensor_copy(Q[:, 0:DIM], psB[:, 0:DIM]))
                small_sent()
                dve.wait_ge(end_gathered, 16 * NB * (q + 1))
                if q not in MAX_PASSES:
                    link(tt(EGW, EGW, per(valid[:, :], NB, DIM), ALU.mult))
            start = steps[0]
            with dve.Fori(0, NG) as g:
                steps[1] = g
                here = bass.ds(g * GB, GB)
                dve.wait_ge(out_ready, g + (base + 1))
                dve.sem_inc(turn["dve"], 1)
                if q == 0:
                    link(ts(CQ[:, here, :], OUTG[:, :, 0:W0], 1.0, None, ALU.mult))
                elif q in MAX_PASSES:
                    steps[1] = g * 2
                    link(tt(C[:, here, :], OUTG[:, :, 0:DIM],
                            cpen[:, here].unsqueeze(2).broadcast_to([P, GB, DIM]), ALU.add))
                    link(tt(EGW[:, here, :], EGW[:, here, :], C[:, here, :], ALU.max))
                else:
                    link(tt(EGW[:, here, :], EGW[:, here, :], OUTG[:, :, 0:DIM], ALU.add))
                dve.sem_inc(out_used, 1)
            steps[0] = start + (steps[0] - start) * NG
            steps[1] = 0
            if q in MAX_PASSES:
                link(tt(EGW, EGW, per(valid[:, :], NB, DIM), ALU.mult))

        def sum_by_counts(f, n):
            with dve.Fori(0, CB // 2) as i:
                for half in range(2):
                    dve.wait_ge(sums_ready[half], i + (n * CB // 2 + 1))
                    ts(EGD[:, bass.ds(i * 2 + half, 1), :], psM[half][:, 0:DIM].unsqueeze(1), 1.0, None,
                       ALU.mult).then_inc(sums_used[half], 1)
            for half in range(2):
                dve.wait_ge(sums_used[half], (n + 1) * CB // 2 + 1)
            dve.sem_inc(small_ready, 1)
            base = out_group_base(f, "carry")
            start = steps[0]
            with dve.Fori(0, NG) as g:
                steps[1] = g
                dve.wait_ge(out_ready, g + (base + 1))
                dve.sem_inc(turn["dve"], 1)
                link(tt(EGD[:, bass.ds(g * GB + 1, GB), :], EGD[:, bass.ds(g * GB + 1, GB), :], OUTG[:, :, 0:DIM], ALU.add))
                dve.sem_inc(out_used, 1)
            steps[0] = start + NG
            steps[1] = 0

        def layernorm(V, tmp):
            link(nc.vector.reduce_sum(stat[:, 0, :], V, AX.X))
            link(ts(stat[:, 0, :], stat[:, 0, :], 1.0 / DIM, None, ALU.mult))
            link(tt(V, V, per(stat[:, 0, :], NB, DIM), ALU.subtract))
            link(tt(tmp, V, V, ALU.mult))
            link(nc.vector.reduce_sum(stat[:, 1, :], tmp, AX.X))
            link(ts(stat[:, 1, :], stat[:, 1, :], 1.0 / DIM, 1e-5, ALU.mult, ALU.add))
            roots[0] += 1
            dve.sem_inc(sqrt_in, 1)
            dve.wait_ge(sqrt_done, roots[0])
            link(nc.vector.reciprocal(stat[:, 1, :], stat[:, 1, :]))
            link(tt(V, V, per(stat[:, 1, :], NB, DIM), ALU.mult))

        def next_x(EGW=EGW):
            link(tt(X[:, :, :], X[:, :, :], EGW, ALU.add))
            layernorm(X[:, :, :], EGW)
            dve.sem_inc(rows_ready, 1)

        dve.sem_inc(end_free, 1)
        attention_pass()
        carries(ATT, 0)
        dve.wait_ge(end_gathered, 16 * NB)
        link(tt(zself[:, :, :], TB0[:, :, SW:W0], ADN[:, :, :], ALU.add))
        link(stt(zself[:, :, :], zself[:, :, :], 0.2, zself[:, :, :], ALU.mult, ALU.max))
        link(tt(EG0[:, :, SW:W0], EG0[:, :, SW:W0], per(vpen[:, :], NB, HEADS), ALU.add))
        link(tt(CQ[:, :, SW:W0], CQ[:, :, SW:W0], per(cpen[:, :], NB, HEADS), ALU.add))
        link(tt(mx[:, :, :], EG0[:, :, SW:W0], CQ[:, :, SW:W0], ALU.max))
        link(tt(mx[:, :, :], mx[:, :, :], zself[:, :, :], ALU.max))
        link(tt(E3[:, 0, :, :], EG0[:, :, SW:W0], mx[:, :, :], ALU.subtract))
        link(tt(E3[:, 1, :, :], CQ[:, :, SW:W0], mx[:, :, :], ALU.subtract))
        link(tt(E3[:, 2, :, :], zself[:, :, :], mx[:, :, :], ALU.subtract))
        dve.sem_inc(exp_in, 1)
        dve.wait_ge(exp_done, 2 * ITERS + 3)
        for j, V in enumerate((EG0, CQ, TB0)):
            Vh = V[:, :, 0:SW].rearrange("p b (h w) -> p b h w", w=HW)
            link(tt(Vh, Vh, E3[:, j, :, :].unsqueeze(3).broadcast_to([P, NB, HEADS, HW]), ALU.mult))
        link(tt(EG0[:, :, 0:SW], EG0[:, :, 0:SW], CQ[:, :, 0:SW], ALU.add))
        link(tt(EG0[:, :, 0:SW], EG0[:, :, 0:SW], TB0[:, :, 0:SW], ALU.add))
        link(nc.vector.reciprocal(rden[:, :, :], EG0[:, :, HDIM:SW:HW]))
        link(tt(C[:, :, :].rearrange("p b (h w) -> p b h w", w=HDIM),
                EG0[:, :, 0:SW].rearrange("p b (h w) -> p b h w", w=HW)[:, :, :, 0:HDIM],
                rden[:, :, :].unsqueeze(3).broadcast_to([P, NB, HEADS, HDIM]), ALU.mult))
        dve.sem_inc(rows_ready, 1)
        node_rows(PROJ)
        link(tt(C[:, :, :], C[:, :, :], row(PB, NB), ALU.add))
        layernorm(C[:, :, :], EGW)
        link(tt(C[:, :, :], C[:, :, :], row(LG, NB), ALU.mult))
        link(tt(EGW, C[:, :, :], row(LB, NB), ALU.add))
        next_x()

        for f in (MAX1, MAX2, MEAN1, MEAN2, GCN1, GCN2, GCN3):
            q = PASS_OF_PHASE[f]
            node_rows(f)
            EG_F = EGW if q < GATHER_PASSES else EGD[:, 1:CB, :]
            if q < GATHER_PASSES:
                dve.sem_inc(end_free, 1)
                running_pass(q)
                carries(f, q)
            else:
                sum_by_counts(f, q - GATHER_PASSES)
            if f in (MAX1, MAX2):
                link(tt(EG_F, EG_F, R, ALU.add))
                act_out = C[:, :, :] if f == MAX1 else EG_F
                link(stt(act_out, EG_F, 0.01, EG_F, ALU.mult, ALU.max))
            elif f in (MEAN1, MEAN2):
                link(tt(EG_F, EG_F, per(rcnt[:, :], NB, DIM), ALU.mult))
                link(tt(EG_F, EG_F, R, ALU.add))
                if f == MEAN1:
                    link(ts(C[:, :, :], EG_F, 0.0, None, ALU.max))
            else:
                link(tt(EG_F, EG_F, TBW, ALU.add))
                link(tt(EG_F, EG_F, per(dis[:, :], NB, DIM), ALU.mult))
                link(tt(EG_F, EG_F, row({GCN1: B_G1, GCN2: B_G2, GCN3: B_G3}[f], NB), ALU.add))
                if f != GCN3:
                    link(ts(C[:, :, :], EG_F, 0.0, None, ALU.max))
            if f == MAX2:
                dve.sem_inc(iota_wanted, 1)
                dve.wait_ge(iota_made, 1)
                link(ts(SEL[:, :], NODE_IOTA, lead[:, 0:1], None, ALU.is_equal))
            if f in (MAX2, MEAN2, GCN3):
                next_x(EG_F)
            else:
                dve.sem_inc(rows_ready, 1)

    ctx.close()


_INS = ["x", "src", "dst", "dst_before", "edge_attr", "L0_gnn_W", "L0_gnn_att_src", "L0_gnn_att_dst",
        "L0_gnn_gat_bias", "L0_gnn_proj_WT", "L0_gnn_proj_b", "L0_gnn_ln_g", "L0_gnn_ln_b",
        "L1_gnn_W1_msg", "L1_gnn_W1_edge", "L1_gnn_W1_root", "L1_gnn_b1",
        "L1_gnn_W2_msg", "L1_gnn_W2_edge", "L1_gnn_W2_root", "L1_gnn_b2",
        "L2_gnn_W1_l", "L2_gnn_b1", "L2_gnn_W1_r", "L2_gnn_W2_l", "L2_gnn_b2", "L2_gnn_W2_r",
        "L3_gnn_W1", "L3_gnn_b1", "L3_gnn_W2", "L3_gnn_b2", "L3_gnn_W3", "L3_gnn_b3"]


def kernel(**inputs):
    import numpy as _np
    import concourse.bacc as _bacc
    from concourse import mybir as _mybir
    from concourse.bass_utils import run_bass_kernel_spmd as _run

    src = _np.zeros((EPAD,), _np.int32)
    src[:EDGES] = inputs["src"]
    dst = _np.full((EPAD + 1,), NODES, _np.int32)
    dst[1:EDGES + 1] = inputs["dst"]
    attr = _np.zeros((EPAD, EDGE_DIM), _np.float32)
    attr[:EDGES] = inputs["edge_attr_32"]
    laid = dict(inputs)
    laid["src"] = src.reshape(P, T)
    laid["dst"] = dst[1:].reshape(P, T)
    laid["dst_before"] = dst[:-1].reshape(P, T)
    laid["edge_attr"] = attr.reshape(P, T, EDGE_DIM).transpose(2, 1, 0)
    laid["L0_gnn_proj_WT"] = _np.asarray(inputs["L0_gnn_proj_W"]).T

    nc = _bacc.Bacc("TRN2", target_bir_lowering=False, num_devices=1)
    arrays, args = {}, []
    for name in _INS:
        a = _np.ascontiguousarray(laid[name])
        arrays[f"in_{name}"] = a
        args.append(nc.dram_tensor(f"in_{name}", a.shape, _mybir.dt.from_np(a.dtype), kind="ExternalInput").ap())
    args.append(nc.dram_tensor("out_0", (NODES, DIM), F32, kind="ExternalOutput").ap())
    build(nc, *args)
    r = _run(nc, [arrays], core_ids=[0])
    return r.results[0]["out_0"]
```

```python
from contextlib import ExitStack

import concourse.bass as bass
from concourse import mybir

P = 128
NODES = 6250
EDGES = 200000
DIM = 96
HEADS = 4
HDIM = DIM // HEADS
EDGE_DIM = 32
NB = -(-NODES // P)
NPAD = NB * P
LAST = NODES - (NB - 1) * P
GB = 7
NG = NB // GB
S = 8
T = -(-EDGES // (P * 2 * S)) * 2 * S
EPAD = P * T
ITERS = T // (2 * S)
SAMPLES = 7
RUN = T // SAMPLES
assert RUN * SAMPLES == T
HW = HDIM + 1
SW = HEADS * HW
W0 = SW + HEADS
BIG = 1e30
OUT_COLS = 256
CB = NB + 1
ROW = 64 * P
KC = 7
NK = NB // KC
CS = 4
ZEROED = 4
ZERO_ITERS = -(-2 * CB // ZEROED) + 1
BETWEEN = 8 * 2 * CS
FULL_ITERS = (T - BETWEEN - 2 * (ITERS - ZERO_ITERS)) // (2 * CS) - ITERS
COUNTING = [(0, 0, ZERO_ITERS, 0), (0, ZERO_ITERS, ITERS, 1), (1, 0, ITERS, CS),
            (2, 0, FULL_ITERS, CS), (2, FULL_ITERS, ITERS, 0)]
assert ZEROED * (ZERO_ITERS - 1) == 2 * CB
assert sum(2 * n * (end - start) for _, start, end, n in COUNTING) + BETWEEN == T

F32 = mybir.dt.float32
I32 = mybir.dt.int32
BF16 = mybir.dt.bfloat16
ALU = mybir.AluOpType
ACT = mybir.ActivationFunctionType
AX = mybir.AxisListType

ATT, PROJ, MAX1, MAX2, MEAN1, MEAN2, GCN1, GCN2, GCN3 = range(9)
PHASE_COLS = [W0 + HEADS, DIM] + [2 * DIM] * 4 + [DIM] * 3
PASS_OF_PHASE = {ATT: 0, MAX1: 1, MAX2: 2, MEAN1: 3, MEAN2: 4, GCN1: 5, GCN2: 6, GCN3: 7}
GATHER_PASSES = 3
MAX_PASSES = (1, 2)


def counted_before(part):
    earlier = COUNTING[:COUNTING.index(part)]
    return (sum(2 * n * (end - start) for _, start, end, n in earlier) + (BETWEEN if part[0] > 0 else 0),
            sum(end - start for _, start, end, n in earlier if n))


def out_group_base(phase, kind):
    n = 0
    for f in range(9):
        if f == phase and kind == "rows":
            return n
        n += NG
        if PASS_OF_PHASE.get(f, GATHER_PASSES) < GATHER_PASSES:
            if f == phase:
                return n
            n += NG



def build(nc, x, src, dst, dst_before, edge_attr, att_W, att_src, att_dst, gat_bias, proj_WT, proj_b, ln_g, ln_b,
          m1_msg, m1_edge, m1_root, m1_b, m2_msg, m2_edge, m2_root, m2_b,
          s1_l, s1_b, s1_r, s2_l, s2_b, s2_r, g1_W, g1_b, g2_W, g2_b, g3_W, g3_b, out):
    ctx = ExitStack()

    def sb(name, shape, dt=F32):
        return ctx.enter_context(nc.sbuf_tensor(name, shape, dt))

    def sem(name):
        return ctx.enter_context(nc.semaphore(name))

    table0 = nc.dram_tensor("table0", (NPAD, W0), F32, kind="Internal").ap()
    table = nc.dram_tensor("table", (NPAD, DIM), F32, kind="Internal").ap()
    hist0 = nc.dram_tensor("hist0", (EPAD, W0), F32, kind="Internal").ap()
    hist = nc.dram_tensor("hist", (EPAD, DIM), F32, kind="Internal").ap()
    counts16 = nc.dram_tensor("counts16", (CB * P, ROW), BF16, kind="Internal").ap()
    cells = nc.dram_tensor("cells", (P, T), I32, kind="Internal").ap()
    counts = nc.dram_tensor("counts", (CB * P, ROW), F32, kind="Internal").ap()
    ad_nodes = nc.dram_tensor("ad_nodes", (NPAD, HEADS), F32, kind="Internal").ap()
    ad_starts = nc.dram_tensor("ad_starts", (EPAD, HEADS), F32, kind="Internal").ap()
    last_row = nc.dram_tensor("last_row", (NPAD,), F32, kind="Internal").ap()
    start_row = nc.dram_tensor("start_row", (NPAD + 1,), F32, kind="Internal").ap()

    X = sb("X", [P, NB, DIM])
    CG = sb("CG", [P, 4 * S * W0 + NB * DIM])
    C = CG[:, 4 * S * W0:].rearrange("p (b w) -> p b w", w=DIM)
    TB = sb("TB", [P, NB * W0])
    TB0 = TB[:, :].rearrange("p (b w) -> p b w", w=W0)
    TBW = TB[:, 0:NB * DIM].rearrange("p (b w) -> p b w", w=DIM)
    EG = sb("EG", [P, NB * W0])
    EG0 = EG[:, :].rearrange("p (b w) -> p b w", w=W0)
    EGW = EG[:, 0:NB * DIM].rearrange("p (b w) -> p b w", w=DIM)
    ARENA = sb("ARENA", [P, T * HEADS])
    AD = ARENA[:, :].rearrange("p (t h) -> p t h", h=HEADS)
    ROWB = ARENA[:, 0:NPAD]
    R = ARENA[:, 0:NB * DIM].rearrange("p (b w) -> p b w", w=DIM)
    CQ = ARENA[:, 0:NB * W0].rearrange("p (b w) -> p b w", w=W0)
    SEL = sb("SEL", [P, NPAD])
    EDG = sb("EDG", [P, 4, T])
    SRC, CELL = EDG[:, 0, :].bitcast(I32), EDG[:, 3, :].bitcast(I32)
    same, reset = EDG[:, 1, :], EDG[:, 2, :]
    CNT = EDG[:, :, :].rearrange("p a t -> p (a t)").rearrange("p (c k m) -> p c k m", c=NK, k=KC)
    CNT16 = EDG[:, :, :].rearrange("p a t -> p (a t)").bitcast(BF16).rearrange("p (c m) -> p c m", c=NK)[
        :, :, 0:KC * P].rearrange("p c (k m) -> p c k m", k=KC)
    G = CG[:, 0:2 * S * W0].rearrange("p (s w) -> p s w", s=2)
    H = CG[:, 2 * S * W0:4 * S * W0].rearrange("p (s w) -> p s w", s=2)
    PARTS = CG[:, 0:NB * 3 * DIM // 2].bitcast(BF16).rearrange("p (b w) -> p b w", w=3 * DIM)
    MOST = CG[:, NB * 3 * DIM // 2:NB * 3 * DIM // 2 + KC * P].bitcast(BF16).rearrange("p (a m) -> p a m", a=2)
    SEL16 = SEL[:, 0:NPAD // 2].bitcast(BF16)
    Q_REST = SEL[:, NPAD // 2 + 512:NPAD // 2 + 512 + W0]
    Q_PARTS = SEL[:, NPAD // 2 + 640:NPAD // 2 + 640 + 3 * W0 // 2].bitcast(BF16).rearrange("p (a w) -> p a w", a=3)
    LEAD_SUM = SEL[:, NPAD // 2:NPAD // 2 + DIM]
    LEAD_REST = SEL[:, NPAD // 2 + DIM:NPAD // 2 + 2 * DIM]
    LEAD_PARTS = SEL[:, NPAD // 2 + 2 * DIM:NPAD // 2 + 2 * DIM + 3 * DIM // 2].bitcast(BF16)
    G0 = G[:, :, :].rearrange("p s (k w) -> p s k w", w=W0)
    H0 = H[:, :, :].rearrange("p s (k w) -> p s k w", w=W0)
    GW = G[:, :, 0:S * DIM].rearrange("p s (k w) -> p s k w", w=DIM)
    HWD = H[:, :, 0:S * DIM].rearrange("p s (k w) -> p s k w", w=DIM)
    EAZ = sb("EAZ", [P, 2 * S * P])
    EA = EAZ[0:EDGE_DIM, :].rearrange("p (s k m) -> p s k m", s=2, k=S)
    cidx = sb("cidx", [P, 2, CS], I32)
    between_cells = sb("between_cells", [P, 2 * CS], I32)
    count_one = sb("count_one", [P, 2], BF16)
    lead = sb("lead", [P, 1])
    chunk_f = sb("chunk_f", [P, 1])
    chunk_i = sb("chunk_i", [P, 1], I32)
    idx = sb("idx", [P, 2, S], I32)
    Zs = sb("Zs", [P, S, HEADS])
    Rm = sb("Rm", [P, S + 1, HEADS])
    EX = sb("EX", [P, 2, S, HEADS])
    WR = sb("WR", [DIM, 9, 2 * DIM])
    WE = sb("WE", [EDGE_DIM, 2, DIM])
    attv = sb("attv", [DIM, 2, DIM])
    attp = sb("attp", [DIM, 2, DIM])
    gbT = sb("gbT", [DIM, 1])
    rows = sb("rows", [P, 10, DIM])
    XTQ = sb("XTQ", [SW, 2 * GB * P])
    XT = XTQ[0:DIM, :].rearrange("k (j m) -> k j m", j=2)
    STG = sb("STG", [P, 2 * GB * DIM])
    most_all = sb("most_all", [P, 1])
    most_row = sb("most_row", [1, 1])
    large = sb("large", [1, 1], I32)
    ident = sb("ident", [P, P])
    ones = sb("ones", [P, P])
    onesrow = sb("onesrow", [P, W0])
    node_i = sb("node_i", [P, NB], I32)
    node_f = sb("node_f", [P, NB])
    bound_i = sb("bound_i", [P, 1], I32)
    ones_b = sb("ones_b", [P, 2], BF16)
    zeros_b = sb("zeros_b", [P, NB + 1], BF16)
    samples = sb("samples", [P, SAMPLES])
    run_f = sb("run_f", [P, NB])
    run_i = sb("run_i", [P, NB], I32)
    inner = sb("inner", [P, NB])
    all_edges = sb("all_edges", [1, 1])
    bound = sb("bound", [P, 2])
    whole = sb("whole", [P, 1])
    wdiag = sb("wdiag", [P, P])
    wrow = sb("wrow", [W0, P])
    wneg = sb("wneg", [W0, P])
    ends = sb("ends", [NB, P])
    starts = sb("starts", [NB, P])
    lastf = sb("lastf", [NB, P])
    startN = sb("startN", [P, NB])
    degN = sb("degN", [P, NB])
    endN = sb("endN", [P, NB])
    valid = sb("valid", [P, NB])
    vpen = sb("vpen", [P, NB])
    cpen = sb("cpen", [P, NB])
    rcnt = sb("rcnt", [P, NB])
    dis = sb("dis", [P, NB])
    nf = sb("nf", [P, NB])
    last_i = sb("last_i", [P, NB], I32)
    start_i = sb("start_i", [P, NB], I32)
    ADN = sb("ADN", [P, NB, HEADS])
    small_G = G[:, :, :].rearrange("p s w -> p (s w)")[:, 0:6 * NB * HEADS].rearrange("p (a b h) -> p a b h", a=6, h=HEADS)
    E3, zself, mx, rden = small_G[:, 0:3], small_G[:, 3], small_G[:, 4], small_G[:, 5]
    stat = sb("stat", [P, 2, NB])
    dst0 = sb("dst0", [P, 1], I32)
    F0 = sb("F0", [P, W0 + SW])
    QT = XTQ[:, 0:4 * P].rearrange("k (a m) -> k a m", a=4)
    Q = sb("Q", [P, W0])
    LEADS = EG[:, 0:T]
    COLF = EG[:, T:2 * T]
    COLI = EG[:, 2 * T:3 * T].bitcast(I32)
    NODE_IOTA = ARENA[:, 0:NPAD].bitcast(I32)
    DST = C[:, :, :].rearrange("p b d -> p (b d)")[:, 0:T].bitcast(I32)
    PREV = C[:, :, :].rearrange("p b d -> p (b d)")[:, T:2 * T].bitcast(I32)
    BEYOND = SEL[:, :].bitcast(BF16).rearrange("p (s n) -> p s n", s=2)
    RUNS = EG[:, 0:2 * GB * RUN].bitcast(I32).rearrange("p (s j r) -> p s j r", s=2, j=GB)
    BELOW = EG[:, 2 * GB * RUN:3 * GB * RUN].rearrange("p (j r) -> p j r", j=GB)

    psX = ctx.enter_context(nc.psum_tensor("psX", [P, 1024], F32))
    psO = ctx.enter_context(nc.psum_tensor("psO", [P, 2048], F32))
    psA = ctx.enter_context(nc.psum_tensor("psA", [P, 512], F32))
    psB = ctx.enter_context(nc.psum_tensor("psB", [P, 512], F32))
    OUTG = psO[:, 0:GB * OUT_COLS].rearrange("p (j c) -> p j c", c=OUT_COLS)
    ETERM = psO[:, :].rearrange("p (s b c) -> p s b c", s=2, b=2)
    psM = [psA, psB]

    inputs_loaded = sem("inputs_loaded")
    pads_zeroed = sem("pads_zeroed")
    consts_made = sem("consts_made")
    filled = sem("filled")
    weights_made = sem("weights_made")
    rows_ready = sem("rows_ready")
    staged = sem("staged")
    transposed = sem("transposed")
    xt_copied = sem("xt_copied")
    out_ready = sem("out_ready")
    out_used = sem("out_used")
    table_made = sem("table_made")
    table_stored = sem("table_stored")
    edges_loaded = sem("edges_loaded")
    beyond_ready = sem("beyond_ready")
    beyond_added = sem("beyond_added")
    runs_wanted = sem("runs_wanted")
    runs_loaded = [sem("runs_loaded0"), sem("runs_loaded1")]
    runs_read = sem("runs_read")
    starts_out = sem("starts_out")
    starts_stored = sem("starts_stored")
    ends_back = sem("ends_back")
    small_ready = sem("small_ready")
    small_done = sem("small_done")
    rows_out = sem("rows_out")
    ends_stored = sem("ends_stored")
    rowb_used = sem("rowb_used")
    rowb_loaded = sem("rowb_loaded")
    node_idx = sem("node_idx")
    zero_ready = sem("zero_ready")
    starts_zeroed = sem("starts_zeroed")
    ad_made = sem("ad_made")
    ad_stored = sem("ad_stored")
    ad_scattered = sem("ad_scattered")
    ad_loaded = sem("ad_loaded")
    ad_first = sem("ad_first")
    gathered = [sem("gathered0"), sem("gathered1")]
    counts_zeroed = sem("counts_zeroed")
    counted_edges = sem("counted_edges")
    between_ready = sem("between_ready")
    cells_ready = [sem("cells_ready0"), sem("cells_ready1")]
    piece_loaded = [sem(f"piece_loaded{c}") for c in range(NK)]
    pieces_used = sem("pieces_used")
    pieces_seen = sem("pieces_seen")
    cells_made = sem("cells_made")
    cells_stored = sem("cells_stored")
    recount_ready = sem("recount_ready")
    recount_cell = sem("recount_cell")
    recounted = sem("recounted")
    again_loaded = [sem(f"again_loaded{c}") for c in range(NK)]
    again_used = sem("again_used")
    again_summed = sem("again_summed")
    again_taken = sem("again_taken")
    again_step = sem("again_step")
    large_known = sem("large_known")
    rest_made = sem("rest_made")
    second_made = sem("second_made")
    parts_made = sem("parts_made")
    leads_ready = sem("leads_ready")
    sums_ready = [sem("sums_ready0"), sem("sums_ready1")]
    sums_used = [sem("sums_used0"), sem("sums_used1")]
    iota_wanted = sem("iota_wanted")
    iota_made = sem("iota_made")
    idx_ready = [sem("idx_ready0"), sem("idx_ready1")]
    rows_used = [sem("rows_used0"), sem("rows_used1")]
    block_done = [sem("block_done0"), sem("block_done1")]
    hist_stored = [sem("hist_stored0"), sem("hist_stored1")]
    ea_loaded = [sem("ea_loaded0"), sem("ea_loaded1")]
    eterm_ready = [sem("eterm_ready0"), sem("eterm_ready1")]
    exp_in = sem("exp_in")
    exp_done = sem("exp_done")
    sqrt_in = sem("sqrt_in")
    sqrt_done = sem("sqrt_done")
    end_gathered = [sem(f"end_gathered{g}") for g in range(NG)]
    end_free = sem("end_free")
    turn = {e: sem(f"turn_{e}") for e in ("pe", "act", "dve", "pool", "sp")}
    dve_step = sem("dve_step")
    out_stored = sem("out_stored")

    block = ctx.enter_context(nc.Block())
    vec_rows = [proj_b, ln_g, ln_b, m1_b, m2_b, s1_b, s2_b, g1_b, g2_b, g3_b]
    PB, LG, LB, B_M1, B_M2, B_S1, B_S2, B_G1, B_G2, B_G3 = range(10)

    input_loads = [(X[:, 0:NB - 1, :], x[0:(NB - 1) * P, :].rearrange("(b p) d -> p b d", p=P)),
                   (X[0:LAST, NB - 1, :], x[(NB - 1) * P:NODES, :]),
                   (WR[:, 0, 0:SW].rearrange("k (h w) -> k h w", w=HW)[:, :, 0:HDIM],
                    att_W.rearrange("k (h w) -> k h w", w=HDIM)),
                   (attv[:, 0, :], att_src.rearrange("h k -> (h k)").partition_broadcast(DIM)),
                   (attv[:, 1, :], att_dst.rearrange("h k -> (h k)").partition_broadcast(DIM)),
                   (gbT[:, :], gat_bias.rearrange("(k a) -> k a", a=1)),
                   (WR[:, PROJ, 0:DIM], proj_WT),
                   (WR[:, MAX1, 0:DIM], m1_msg), (WR[:, MAX1, DIM:2 * DIM], m1_root),
                   (WR[:, MAX2, 0:DIM], m2_msg), (WR[:, MAX2, DIM:2 * DIM], m2_root),
                   (WE[:, 0, :], m1_edge), (WE[:, 1, :], m2_edge),
                   (WR[:, MEAN1, 0:DIM], s1_l), (WR[:, MEAN1, DIM:2 * DIM], s1_r),
                   (WR[:, MEAN2, 0:DIM], s2_l), (WR[:, MEAN2, DIM:2 * DIM], s2_r),
                   (WR[:, GCN1, 0:DIM], g1_W), (WR[:, GCN2, 0:DIM], g2_W), (WR[:, GCN3, 0:DIM], g3_W)]
    input_loads += [(rows[:, j, :], v.partition_broadcast(P)) for j, v in enumerate(vec_rows)]
    ALL_LOADED = 16 * len(input_loads)
    edge_loads = [(DST, dst), (PREV, dst_before), (SRC[:, :], src)]
    EDGES_LOADED = 16 * len(edge_loads)

    @block.gpsimd
    def _(pool):
        nc.gpsimd.memset(ident[:, :], 0.0).then_inc(turn["pool"], 1)
        pool.wait_ge(turn["pool"], 1)
        nc.gpsimd.affine_select(out=ident[:, :], in_=ident[:, :], compare_op=ALU.not_equal, fill=1.0, base=0,
                                pattern=[[-1, P]], channel_multiplier=1).then_inc(consts_made, 1)
        nc.gpsimd.iota(NODE_IOTA, pattern=[[1, NPAD]], base=0, channel_multiplier=0).then_inc(consts_made, 1)
        nc.gpsimd.iota(node_i[:, :], pattern=[[P, NB]], base=0, channel_multiplier=1).then_inc(consts_made, 1)
        nc.gpsimd.iota(bound_i[:, :], pattern=[[0, 1]], base=T, channel_multiplier=T).then_inc(consts_made, 1)
        nc.gpsimd.iota(chunk_i[:, :], pattern=[[0, 1]], base=0, channel_multiplier=1).then_inc(consts_made, 1)

        pool.wait_ge(runs_wanted, 1)
        dst_runs = dst.rearrange("p (r c) -> (p r) c", c=RUN)
        for b in range(NB):
            g, j = b // GB, b % GB
            if j == 0 and g >= 2:
                pool.wait_ge(runs_read, g - 1)
            pool.indirect_dma_start(out=RUNS[:, g % 2, j, :], out_offset=None, in_=dst_runs,
                                    in_offset=bass.IndirectOffsetOnAxis(ap=run_i[:, b:b + 1], axis=0)
                                    ).then_inc(runs_loaded[g % 2], 16)

        pool.wait_ge(node_idx, 1)
        pool.wait_ge(ad_made, 1)
        pool.wait_ge(starts_zeroed, 16)
        for b in range(NB):
            pool.indirect_dma_start(out=ad_starts, out_offset=bass.IndirectOffsetOnAxis(ap=start_i[:, b:b + 1], axis=0),
                                    in_=ADN[:, b, :], in_offset=None,
                                    bounds_check=EPAD - 1, oob_is_err=False).then_inc(ad_scattered, 16)
        pool.wait_ge(ad_stored, 16)
        pool.wait_ge(ad_loaded, 16)
        pool.indirect_dma_start(out=AD[:, 0, :], out_offset=None, in_=ad_nodes,
                                in_offset=bass.IndirectOffsetOnAxis(ap=dst0[:, 0:1], axis=0)).then_inc(ad_first, 16)

        def second_and_third_parts(n):
            with pool.Fori(0, NG) as g:
                here = bass.ds(g * GB, GB)
                pool.wait_ge(rest_made, g + (n * NG + 1))
                pool.sem_inc(turn["pool"], 1)
                nc.gpsimd.tensor_copy(PARTS[:, here, DIM:2 * DIM], EGW[:, here, :]).then_inc(second_made, 1)
                pool.wait_ge(second_made, g + (n * NG + 1))
                pool.sem_inc(turn["pool"], 1)
                nc.gpsimd.tensor_tensor(PARTS[:, here, 2 * DIM:3 * DIM], EGW[:, here, :], PARTS[:, here, DIM:2 * DIM],
                                        ALU.subtract).then_inc(parts_made, 1)

        count_cells = counts16.rearrange("r (c o) -> (r c) o", o=1)

        def count_edges(column, cells):
            pool.indirect_dma_start(out=count_cells, out_offset=bass.IndirectOffsetOnAxis(ap=cells, axis=0),
                                    in_=count_one[:, column:column + 1], in_offset=None,
                                    compute_op=ALU.add).then_inc(counted_edges, 16)

        def gather_part(q, tab, width, first, end, counting, steps0, slots0):
            with pool.Fori(first, end) as i:
                for s in range(2):
                    if counting:
                        pool.wait_ge(cells_ready[s], i + (slots0 - first + 1))
                        pool.sem_inc(turn["pool"], 1)
                    pool.wait_ge(idx_ready[s], i + (q * ITERS + 1))
                    pool.sem_inc(turn["pool"], 1)
                    pool.wait_ge(rows_used[s], i + (q * ITERS + 1))
                    pool.sem_inc(turn["pool"], 1)
                    done = 0
                    for k in range(S):
                        pool.indirect_dma_start(
                            out=G[:, s, k * width:(k + 1) * width], out_offset=None, in_=tab,
                            in_offset=bass.IndirectOffsetOnAxis(ap=idx[:, s, k:k + 1], axis=0)).then_inc(
                                gathered[s], 16)
                        if counting and (k + 1) % (S // counting) == 0:
                            pool.wait_ge(counted_edges, i * (16 * 2 * counting)
                                         + 16 * (steps0 - first * 2 * counting + s * counting + done + 1))
                            pool.sem_inc(turn["pool"], 1)
                            count_edges(1, cidx[:, s, done:done + 1])
                            done += 1

        for q in range(GATHER_PASSES):
            tab = table0 if q == 0 else table
            rec = hist0 if q == 0 else hist
            width = W0 if q == 0 else DIM
            pool.wait_ge(table_stored, 16 * NG * (q + 1))
            for part in [c for c in COUNTING if c[0] == q]:
                _, first, end, counting = part
                steps0, slots0 = counted_before(part)
                if counting and steps0 == 0:
                    pool.wait_ge(counts_zeroed, 16 * 2 * CB)
                    pool.wait_ge(cells_ready[0], 1)
                    count_edges(0, cidx[:, 0, 0:1])
                gather_part(q, tab, width, first, end, counting, steps0, slots0)
            pool.wait_ge(hist_stored[0], 32 + 16 * ITERS * (q + 1))
            pool.wait_ge(hist_stored[1], 32 + 16 * ITERS * (q + 1))
            pool.wait_ge(end_free, q + 1)
            for b in range(NB):
                pool.indirect_dma_start(
                    out=EG[:, b * width:(b + 1) * width], out_offset=None, in_=rec,
                    in_offset=bass.IndirectOffsetOnAxis(ap=last_i[:, b:b + 1], axis=0)).then_inc(end_gathered[b // GB], 16)
            if q == 0:
                before = counted_before(COUNTING[2])[0] - BETWEEN
                with pool.Fori(0, BETWEEN // (2 * CS)) as i:
                    nc.gpsimd.tensor_copy(between_cells[:, :], CELL[:, bass.ds(i * (2 * CS) + before, 2 * CS)]
                                          ).then_inc(between_ready, 1)
                    pool.wait_ge(between_ready, i + 1)
                    pool.sem_inc(turn["pool"], 1)
                    for k in range(2 * CS):
                        pool.wait_ge(counted_edges, i * (16 * 2 * CS) + 16 * (before + k + 1))
                        pool.sem_inc(turn["pool"], 1)
                        count_edges(1, between_cells[:, k:k + 1])
                    pool.wait_ge(counted_edges, i * (16 * 2 * CS) + 16 * (before + 2 * CS + 1))
                    pool.sem_inc(turn["pool"], 1)
        pool.wait_ge(iota_wanted, 1)
        nc.gpsimd.iota(NODE_IOTA, pattern=[[1, NPAD]], base=0, channel_multiplier=0).then_inc(iota_made, 1)
        second_and_third_parts(0)
        pool.wait_ge(large_known, 1)
        flag = pool.value_load(large[0:1, 0:1], min_val=0, max_val=1)
        with pool.If(flag == 1):
            pool.wait_ge(recount_ready, 16 * (CB + 1))
            with pool.Fori(0, T) as t:
                nc.gpsimd.tensor_copy(cidx[:, 0, 0:1], CELL[:, bass.ds(t, 1)]).then_inc(recount_cell, 1)
                pool.wait_ge(recount_cell, t + 1)
                pool.sem_inc(turn["pool"], 1)
                pool.indirect_dma_start(out=counts.rearrange("r (c o) -> (r c) o", o=1),
                                        out_offset=bass.IndirectOffsetOnAxis(ap=cidx[:, 0, 0:1], axis=0),
                                        in_=ones[:, 0:1], in_offset=None, compute_op=ALU.add).then_inc(recounted, 16)
                pool.wait_ge(recounted, t * 16 + 16)
                pool.sem_inc(turn["pool"], 1)
        for n in range(1, 8 - GATHER_PASSES):
            second_and_third_parts(n)

    @block.sync
    def _(sp):
        for a, b in edge_loads:
            sp.dma_start(a, b).then_inc(edges_loaded, 16)
        sp.wait_ge(pads_zeroed, 1)
        for a, b in input_loads:
            sp.dma_start(a, b).then_inc(inputs_loaded, 16)
        sp.wait_ge(filled, 1)
        hv0 = hist0.rearrange("(p t) w -> p (t w)", p=P)
        hv = hist.rearrange("(p t) w -> p (t w)", p=P)
        for s in range(2):
            sp.dma_start(hv0[:, s * S * W0:(s + 1) * S * W0], H[:, s, :]).then_inc(hist_stored[s], 16)
            sp.dma_start(hv[:, s * S * DIM:(s + 1) * S * DIM], H[:, s, 0:S * DIM]).then_inc(hist_stored[s], 16)
        sp.wait_ge(zero_ready, 1)
        sp.dma_start(ad_starts.rearrange("(p a t) h -> p a (t h)", p=P, a=NK),
                     EAZ[:, 0:KC * P].unsqueeze(1).broadcast_to([P, NK, KC * P])).then_inc(starts_zeroed, 16)
        sp.dma_start(start_row[NPAD:NPAD + 1].rearrange("(a b) -> a b", b=1), all_edges[:, :]).then_inc(starts_stored, 16)
        ea = edge_attr

        def store_table(q):
            tab = (table0 if q == 0 else table).rearrange("(b p) w -> p b w", p=P)
            tv = TB0 if q == 0 else TBW
            with sp.Fori(0, NG) as g:
                sp.wait_ge(table_made, g + (q * NG + 1))
                sp.dma_start(tab[:, bass.ds(g * GB, GB), :], tv[:, bass.ds(g * GB, GB), :]).then_inc(table_stored, 16)

        def edge_pass(q):
            rec = hv0 if q == 0 else hv
            width = W0 if q == 0 else DIM
            if q in MAX_PASSES:
                sp.wait_ge(counts_zeroed, 16 * 2 * CB)
                for s in range(2):
                    if q == MAX_PASSES[1]:
                        sp.wait_ge(eterm_ready[s], ITERS)
                    sp.dma_start(EA[:, s, :, :], ea[:, s * S:(s + 1) * S, :]).then_inc(ea_loaded[s], 16)

            def store(i, s):
                sp.wait_ge(block_done[s], i + (q * ITERS + 1))
                sp.dma_start(rec[:, bass.ds(i * (2 * S * width) + s * S * width, S * width)],
                             H[:, s, 0:S * width]).then_inc(hist_stored[s], 16)

            if q in MAX_PASSES:
                n0 = MAX_PASSES.index(q) * ITERS
                with sp.Fori(0, ITERS - 1) as i:
                    for s in range(2):
                        store(i, s)
                        sp.wait_ge(eterm_ready[s], i + (n0 + 1))
                        sp.dma_start(EA[:, s, :, :], ea[:, bass.ds(i * (2 * S) + (s * S + 2 * S), S), :]).then_inc(ea_loaded[s], 16)
                for s in range(2):
                    sp.wait_ge(block_done[s], (q + 1) * ITERS)
                    sp.dma_start(rec[:, (T - 2 * S + s * S) * width:(T - 2 * S + s * S + S) * width],
                                 H[:, s, 0:S * width]).then_inc(hist_stored[s], 16)
            else:
                with sp.Fori(0, ITERS) as i:
                    for s in range(2):
                        store(i, s)

        store_table(0)
        sp.wait_ge(ad_made, 1)
        sp.dma_start(ad_nodes.rearrange("(b p) h -> p b h", p=P), ADN[:, :, :]).then_inc(ad_stored, 16)
        sp.wait_ge(starts_out, 1)
        sp.dma_start(start_row[0:NPAD].rearrange("(a b) -> a b", b=P), starts[:, :]).then_inc(starts_stored, 16)
        sp.wait_ge(starts_stored, 32)
        sp.dma_start(ends[:, :], start_row[1:NPAD + 1].rearrange("(a b) -> a b", b=P)).then_inc(ends_back, 16)
        sp.wait_ge(rows_out, 1)
        sp.dma_start(last_row.rearrange("(a b) -> a b", b=P), lastf[:, :]).then_inc(ends_stored, 16)
        sp.wait_ge(ends_stored, 16)
        sp.dma_start(ROWB, last_row[0:NPAD].partition_broadcast(P)).then_inc(rowb_loaded, 16)
        sp.wait_ge(rowb_used, 1)
        sp.dma_start(ROWB, start_row[0:NPAD].partition_broadcast(P)).then_inc(rowb_loaded, 16)
        sp.wait_ge(rowb_used, 2)
        sp.wait_ge(ad_scattered, 16 * NB)
        sp.dma_start(ARENA[:, :], ad_starts.rearrange("(p t) h -> p (t h)", p=P)).then_inc(ad_loaded, 16)
        sp.wait_ge(cells_made, 1)
        sp.dma_start(cells, CELL).then_inc(cells_stored, 16)
        for q in range(GATHER_PASSES):
            if q > 0:
                store_table(q)
            edge_pass(q)
        sp.wait_ge(counted_edges, 16 * (T + 1))
        sp.wait_ge(rows_ready, MEAN1 * NG)
        blocks = counts.rearrange("(b p) c -> b p c", p=P)
        blocks16 = counts16.rearrange("(b p) c -> b p c", p=P)

        def load_pieces(n, exact16):
            source, room = (blocks16, CNT16) if exact16 else (blocks, CNT)
            with sp.Fori(0, CB // 2) as i:
                for half in range(2):
                    for c in range(0, NK, 2):
                        if n == 0:
                            sp.wait_ge(pieces_seen, i * (2 * NK) + (half * NK + c + 1))
                            sp.sem_inc(turn["sp"], 1)
                        if c == NK - 1:
                            sp.wait_ge(sums_ready[1 - half], i + (n * CB // 2 + half + 1))
                        else:
                            sp.wait_ge(pieces_used, i * (2 * NK - 2) + ((n * CB + half) * (NK - 1) + c + 1))
                        sp.sem_inc(turn["sp"], 1)
                        sp.dma_start(room[:, c, :, :].rearrange("p k m -> p (k m)"),
                                     source[bass.ds(i * 2 + half, 1), :, c * KC * P:(c + 1) * KC * P].rearrange(
                                         "a p c -> (a p) c")).then_inc(piece_loaded[c], 16)

        load_pieces(0, True)
        sp.wait_ge(large_known, 1)
        flag = sp.value_load(large[0:1, 0:1], min_val=0, max_val=1)
        with sp.If(flag == 1):
            sp.wait_ge(cells_stored, 16)
            sp.dma_start(CELL, cells).then_inc(recount_ready, 16)
            with sp.Fori(0, CB) as b:
                sp.dma_start(blocks[bass.ds(b, 1), :, 0:NB * P].rearrange("a p (k c) -> (a p) k c", k=NK),
                             EAZ[:, 0:KC * P].unsqueeze(1).broadcast_to([P, NK, KC * P])).then_inc(recount_ready, 16)
            sp.wait_ge(recounted, 16 * T)
            with sp.Fori(0, CB) as b:
                for c in range(NK):
                    sp.wait_ge(again_used, b * NK + (c + 1))
                    sp.dma_start(CNT[:, c, :, :].rearrange("p k m -> p (k m)"),
                                 blocks[bass.ds(b, 1), :, c * KC * P:(c + 1) * KC * P].rearrange("a p c -> (a p) c")
                                 ).then_inc(again_loaded[c], 16)
            sp.wait_ge(again_used, (CB + 1) * NK)
        for n in range(1, 8 - GATHER_PASSES):
            flag = sp.value_load(large[0:1, 0:1], min_val=0, max_val=1)
            with sp.If(flag == 0):
                load_pieces(n, True)
            with sp.Else():
                load_pieces(n, False)
        sp.wait_ge(rows_ready, 9 * NG)
        sp.dma_start(out[0:(NB - 1) * P, :].rearrange("(b p) d -> p b d", p=P), X[:, 0:NB - 1, :]).then_inc(out_stored, 16)
        sp.dma_start(out[(NB - 1) * P:NODES, :], X[0:LAST, NB - 1, :]).then_inc(out_stored, 16)
        sp.wait_ge(out_stored, 32)

    @block.tensor
    def _(pe):
        def node_phase(f):
            cols = PHASE_COLS[f]
            base = out_group_base(f, "rows")

            def transpose_group(g, j):
                pe.wait_ge(staged, g + (f * NG + 1))
                pe.sem_inc(turn["pe"], 1)
                for k in range(GB):
                    mm = pe.transpose(psX[0:DIM, k * P:(k + 1) * P],
                                      STG[:, (j * GB + k) * DIM:(j * GB + k + 1) * DIM], ident[:, :])
                mm.then_inc(transposed, 1)

            def multiply_group(g, j):
                pe.wait_ge(out_used, g + (base + 1))
                pe.sem_inc(turn["pe"], 1)
                for k in range(GB):
                    mm = pe.matmul(OUTG[:, k, 0:cols], XT[:, j, k * P:(k + 1) * P], WR[:, f, 0:cols], start=True, stop=True)
                mm.then_inc(out_ready, 1)

            transpose_group(0, 0)
            with pe.Fori(0, NG // 2) as i:
                for j in range(2):
                    pe.wait_ge(xt_copied, i * 2 + (f * NG + j + 1))
                    pe.sem_inc(turn["pe"], 1)
                    transpose_group(i * 2 + (j + 1), 1 - j)
                    multiply_group(i * 2 + j, j)
            pe.wait_ge(xt_copied, (f + 1) * NG)
            multiply_group(NG - 1, 0)

        def edge_terms(q):
            n0 = MAX_PASSES.index(q) * ITERS
            pe.wait_ge(out_used, out_group_base({1: MAX1, 2: MAX2}[q], "carry") + 1)
            with pe.Fori(0, ITERS) as i:
                for s in range(2):
                    pe.wait_ge(ea_loaded[s], i * 16 + 16 * (n0 + 1))
                    pe.sem_inc(turn["pe"], 1)
                    pe.wait_ge(rows_used[s], i + (q * ITERS + 1))
                    pe.sem_inc(turn["pe"], 1)
                    for k in range(S):
                        mm = pe.matmul(ETERM[:, s, k // 4, (k % 4) * DIM:(k % 4 + 1) * DIM], EA[:, s, k, :],
                                       WE[:, n0 // ITERS, :], start=True, stop=True)
                    mm.then_inc(eterm_ready[s], 1)

        def sum_by_counts(n, exact16):
            def sum_block(i, half, lead):
                pe.wait_ge(sums_used[half], i + (n * CB // 2 + 1))
                pe.sem_inc(turn["pe"], 1)
                if not exact16:
                    pe.matmul(psM[half][:, 0:3 * DIM], ident[:, :], EAZ[:, 0:3 * DIM], start=True, stop=False,
                              skip_group_check=True)
                for c in range(NK):
                    if lead is None:
                        pe.wait_ge(parts_made, n * NG + c + 1)
                    pe.wait_ge(piece_loaded[c], i * 32 + 16 * (n * CB + half + 1))
                    for k in range(KC):
                        b = c * KC + k
                        last = b == NB - 1 and lead is None
                        if exact16:
                            mm = pe.matmul(psM[half][:, 0:3 * DIM], CNT16[:, c, k, :], PARTS[:, b, :],
                                           start=b == 0, stop=last, skip_group_check=True)
                        else:
                            mm = pe.matmul(psM[half][:, 0:DIM], CNT[:, c, k, :], TBW[:, b, :],
                                           start=False, stop=last, skip_group_check=True)
                    if c < NK - 1:
                        mm.then_inc(pieces_used, 1)
                if lead is not None:
                    if lead == 0:
                        pe.wait_ge(leads_ready, n + 1)
                        lead = slice(0, P)
                    mm = pe.matmul(psM[half][:, 0:3 * DIM], SEL16[:, lead], LEAD_PARTS, start=False, stop=True,
                                   skip_group_check=True)
                mm.then_inc(sums_ready[half], 1)

            sum_block(0, 0, None)
            sum_block(0, 1, 0)
            with pe.Fori(1, CB // 2) as i:
                for half in range(2):
                    sum_block(i, half, bass.ds(i * (2 * P) + (half - 1) * P, P))

        def sum_again():
            def sum_block(b, lead):
                pe.wait_ge(again_taken, b + 1)
                pe.sem_inc(turn["pe"], 1)
                pe.matmul(psA[:, 0:3 * DIM], ident[:, :], EAZ[:, 0:3 * DIM], start=True, stop=False,
                          skip_group_check=True)
                for c in range(NK):
                    pe.wait_ge(again_loaded[c], b * 16 + 16)
                    for k in range(KC):
                        mm = pe.matmul(psA[:, 0:DIM], CNT[:, c, k, :], TBW[:, c * KC + k, :], start=False,
                                       stop=lead is None and (c, k) == (NK - 1, KC - 1), skip_group_check=True)
                    mm.then_inc(again_used, 1)
                if lead is not None:
                    mm = pe.matmul(psA[:, 0:3 * DIM], SEL16[:, lead], LEAD_PARTS, start=False, stop=True,
                                   skip_group_check=True)
                    mm.then_inc(again_summed, 1)
                else:
                    pe.wait_ge(again_used, 2 * NK)
                    pe.sem_inc(again_summed, 1)

            pe.sem_inc(again_used, NK)
            sum_block(0, None)
            with pe.Fori(1, CB) as b:
                sum_block(b, bass.ds(b * P - P, P))

        small = [0]

        def carries(f, q):
            def wait_small():
                small[0] += 1
                pe.wait_ge(small_ready, small[0])
            wait_small()
            if q == 0:
                pe.transpose(psA[0:SW, 0:P], F0[:, 0:SW], ident[:, :])
                pe.transpose(psA[0:SW, P:2 * P], F0[:, W0:W0 + SW], ident[:, :]).then_inc(small_done, 1)
                wait_small()
                pe.transpose(psB[:, 0:SW], QT[:, 2, :], ident[0:SW, 0:SW])
                pe.transpose(psB[:, P:P + SW], QT[:, 0, :], ident[0:SW, 0:SW]).then_inc(small_done, 1)
            else:
                pe.transpose(psA[0:DIM, 0:P], HWD[:, 1, S - 1, :], ident[:, :]).then_inc(small_done, 1)
                wait_small()
                pe.transpose(psB[:, 0:DIM], QT[0:DIM, 0, :], ident[0:DIM, 0:DIM]).then_inc(small_done, 1)
            wait_small()
            width = W0 if q == 0 else DIM
            base = out_group_base(f, "carry")
            with pe.Fori(0, NG) as g:
                pe.wait_ge(out_used, g + (base + 1))
                pe.sem_inc(turn["pe"], 1)
                for j in range(GB):
                    for a in range(3):
                        mm = pe.matmul(OUTG[:, j, 0:width], SEL16[:, bass.ds(g * (GB * P) + j * P, P)],
                                       Q_PARTS[:, a, 0:width], start=a == 0, stop=a == 2)
                mm.then_inc(out_ready, 1)

        pe.wait_ge(consts_made, 5)
        pe.wait_ge(beyond_ready, 1)
        pe.matmul(psA[:, 0:NB], BEYOND[:, 0, 0:P], zeros_b[:, 0:NB], start=True, stop=False, skip_group_check=True)

        def add_sample(j, last):
            for b in range(NB):
                mm = pe.matmul(psA[:, b:b + 1], BEYOND[:, j, b * P:(b + 1) * P], ones_b[:, 0:1], start=False, stop=last,
                               skip_group_check=True)
            mm.then_inc(beyond_added, 1)

        with pe.Fori(0, SAMPLES // 2) as i:
            for j in range(2):
                pe.wait_ge(beyond_ready, i * 2 + (j + 1))
                pe.sem_inc(turn["pe"], 1)
                add_sample(j, False)
        pe.wait_ge(beyond_ready, SAMPLES)
        add_sample(0, True)
        pe.wait_ge(weights_made, 1)
        pe.wait_ge(inputs_loaded, ALL_LOADED)
        node_phase(ATT)
        small[0] += 1
        pe.wait_ge(small_ready, small[0])
        pe.transpose(psA[0:NB, 0:P], startN[:, :], ident[:, :]).then_inc(small_done, 1)
        small[0] += 1
        pe.wait_ge(small_ready, small[0])
        pe.transpose(psB[:, 0:NB], ends[:, :], ident[0:NB, 0:NB]).then_inc(small_done, 1)
        small[0] += 1
        pe.wait_ge(small_ready, small[0])
        pe.matmul(psA[0:W0, 0:P], ones[:, 0:W0], wdiag[:, :], start=True, stop=True).then_inc(small_done, 1)
        small[0] += 1
        pe.wait_ge(small_ready, small[0])
        for b in range(NB):
            mm = pe.matmul(psB[:, b:b + 1], SEL16[:, b * P:(b + 1) * P], ones_b[:, 0:1], start=True, stop=True)
        mm.then_inc(small_done, 1)

        carries(ATT, 0)
        node_phase(PROJ)
        for f in (MAX1, MAX2, MEAN1, MEAN2, GCN1, GCN2, GCN3):
            q = PASS_OF_PHASE[f]
            node_phase(f)
            if q in MAX_PASSES:
                edge_terms(q)
                carries(f, q)
            else:
                n = q - GATHER_PASSES
                if n == 0:
                    sum_by_counts(0, True)
                    small[0] += 1
                    pe.wait_ge(small_ready, small[0])
                    pe.transpose(psA[0:1, 0:P], most_all[:, :], ident[:, :]).then_inc(small_done, 1)
                    pe.wait_ge(large_known, 1)
                    flag = pe.value_load(large[0:1, 0:1], min_val=0, max_val=1)
                    with pe.If(flag == 1):
                        sum_again()
                else:
                    flag = pe.value_load(large[0:1, 0:1], min_val=0, max_val=1)
                    with pe.If(flag == 0):
                        sum_by_counts(n, True)
                    with pe.Else():
                        sum_by_counts(n, False)

    @block.scalar
    def _(act):
        def node_phase(f):
            rowsrc = X if f in (ATT, MAX1, MEAN1, GCN1) else C if f in (PROJ, MAX2) else EGW
            base = out_group_base(f, "rows")

            def stage(g):
                if f > 0:
                    act.wait_ge(rows_ready, (f - 1) * NG + g + 1)
                    act.sem_inc(turn["act"], 1)
                if g >= 2:
                    act.wait_ge(transposed, f * NG + g - 1)
                nc.scalar.copy(STG[:, g % 2 * GB * DIM:(g % 2 + 1) * GB * DIM].rearrange("p (j d) -> p j d", d=DIM),
                               rowsrc[:, g * GB:(g + 1) * GB, :]).then_inc(staged, 1)

            if f > 0:
                act.wait_ge(out_ready, base)
                act.sem_inc(turn["act"], 1)
            stage(0)
            stage(1)
            for g in range(NG):
                act.wait_ge(transposed, f * NG + g + 1)
                if g >= 2:
                    act.wait_ge(out_ready, base + g - 1)
                    act.sem_inc(turn["act"], 1)
                if f == PROJ:
                    nc.scalar.activation(XT[:, g % 2, :], psX[0:DIM, 0:GB * P], ACT.Identity,
                                         bias=gbT[:, 0:1]).then_inc(xt_copied, 1)
                else:
                    nc.scalar.copy(XT[:, g % 2, :], psX[0:DIM, 0:GB * P]).then_inc(xt_copied, 1)
                if g + 2 < NG:
                    stage(g + 2)

        def load_pieces(n, exact16):
            blocks = counts.rearrange("(b p) c -> b p c", p=P)
            blocks16 = counts16.rearrange("(b p) c -> b p c", p=P)
            source, room = (blocks16, CNT16) if exact16 else (blocks, CNT)
            if n == 0:
                act.wait_ge(counted_edges, 16 * (T + 1))
                act.wait_ge(rows_ready, MEAN1 * NG)
            with act.Fori(0, CB) as b:
                for c in range(1, NK, 2):
                    if n == 0:
                        act.wait_ge(pieces_seen, b * NK + (c + 1))
                    act.wait_ge(pieces_used, b * (NK - 1) + (n * CB * (NK - 1) + c + 1))
                    act.dma_start(room[:, c, :, :].rearrange("p k m -> p (k m)"),
                                  source[bass.ds(b, 1), :, c * KC * P:(c + 1) * KC * P].rearrange("a p c -> (a p) c")
                                  ).then_inc(piece_loaded[c], 16)

        def zero_counts(rows64):
            act.dma_start(counts16[rows64, 0:NB * P].rearrange("p (a c) -> p a c", a=NK),
                          EAZ[0:64, 0:KC * P // 2].bitcast(BF16).unsqueeze(1).broadcast_to([64, NK, KC * P])).then_inc(counts_zeroed, 16)

        def next_cells(count, steps, s):
            nc.scalar.copy(cidx[:, s, 0:count], CELL[:, steps]).then_inc(cells_ready[s], 1)

        counted_last = [0]

        def edge_pass(q):
            def weights(i, s):
                act.wait_ge(exp_in, i * 2 + (s + 1))
                nc.scalar.activation(EX[:, :, :, :], EX[:, :, :, :], ACT.Exp).then_inc(exp_done, 1)

            def next_indices(i, s, steps):
                act.wait_ge(gathered[s], i * (16 * S) + 16 * S * (q * ITERS + 1))
                act.sem_inc(turn["act"], 1)
                nc.scalar.copy(idx[:, s, :], SRC[:, steps]).then_inc(idx_ready[s], 1)

            for part in [c for c in COUNTING if c[0] == q]:
                _, first, end, counting = part
                steps0, _ = counted_before(part)
                if counting:
                    for s in range(2):
                        if steps0:
                            act.wait_ge(counted_edges, 16 * (steps0 - (1 - s) * counted_last[0] + 1))
                            act.sem_inc(turn["act"], 1)
                        next_cells(counting, slice(steps0 + s * counting, steps0 + (s + 1) * counting), s)
                    counted_last[0] = counting
                with act.Fori(first, end - 1) as i:
                    if part == COUNTING[0]:
                        for k in range(ZEROED):
                            zero_counts(bass.ds(i * (64 * ZEROED) + 64 * k, 64))
                    for s in range(2):
                        if q == 0:
                            weights(i, s)
                        next_indices(i, s, bass.ds(i * (2 * S) + (2 * S + s * S), S))
                        if counting:
                            act.wait_ge(counted_edges, i * (16 * 2 * counting)
                                        + 16 * (steps0 - first * 2 * counting + (s + 1) * counting + 1))
                            act.sem_inc(turn["act"], 1)
                            next_cells(counting, bass.ds(i * (2 * counting) + (
                                steps0 - first * 2 * counting + (2 + s) * counting), counting), s)
                for s in range(2):
                    if q == 0:
                        weights(end - 1, s)
                    if end < ITERS:
                        next_indices(end - 1, s, slice(end * 2 * S + s * S, end * 2 * S + (s + 1) * S))
                    elif q < GATHER_PASSES - 1:
                        next_indices(end - 1, s, slice(s * S, (s + 1) * S))

        exps = [2 * ITERS]

        def exp(ap):
            exps[0] += 1
            act.wait_ge(exp_in, exps[0])
            nc.scalar.activation(ap, ap, ACT.Exp).then_inc(exp_done, 1)

        roots = [0]

        def root(ap):
            roots[0] += 1
            act.wait_ge(sqrt_in, roots[0])
            nc.scalar.activation(ap, ap, ACT.Sqrt).then_inc(sqrt_done, 1)

        act.wait_ge(edges_loaded, EDGES_LOADED)
        act.wait_ge(inputs_loaded, ALL_LOADED)
        for s in range(2):
            nc.scalar.copy(idx[:, s, :], SRC[:, s * S:(s + 1) * S]).then_inc(idx_ready[s], 1)
        node_phase(ATT)
        root(dis[:, :])
        edge_pass(0)
        exp(QT[:, 1, :])
        exp(QT[:, 3, :])
        for g in range(NG):
            exp(E3[:, :, g * GB:(g + 1) * GB, :])
        node_phase(PROJ)
        root(stat[:, 1, :])
        root(stat[:, 1, :])
        for f in (MAX1, MAX2, MEAN1, MEAN2, GCN1, GCN2, GCN3):
            node_phase(f)
            if PASS_OF_PHASE[f] < GATHER_PASSES:
                edge_pass(PASS_OF_PHASE[f])
            else:
                n = PASS_OF_PHASE[f] - GATHER_PASSES
                if n == 0:
                    load_pieces(0, True)
                    act.wait_ge(large_known, 1)
                else:
                    flag = act.value_load(large[0:1, 0:1], min_val=0, max_val=1)
                    with act.If(flag == 0):
                        load_pieces(n, True)
                    with act.Else():
                        load_pieces(n, False)
            if f in (MAX2, MEAN2, GCN3):
                root(stat[:, 1, :])

    @block.vector
    def _(dve):
        steps = [0, 0]

        def link(ins, behind=0):
            steps[0] += 1
            ins.then_inc(dve_step, 1)
            dve.wait_ge(dve_step, steps[1] + (steps[0] - behind))

        def per(v, n, w):
            return v.unsqueeze(2).broadcast_to([P, n, w])

        def row(j, n):
            return rows[:, j:j + 1, :].broadcast_to([P, n, DIM])

        tt = nc.vector.tensor_tensor
        ts = nc.vector.tensor_scalar
        stt = nc.vector.scalar_tensor_tensor

        nc.vector.memset(X[96:P, NB - 1, :], 0.0).then_inc(pads_zeroed, 1)
        link(nc.vector.memset(EAZ[:, :], 0.0))
        nc.vector.memset(all_edges[:, :], float(EPAD)).then_inc(zero_ready, 1)
        link(nc.vector.memset(ones_b[:, :], 1.0))
        link(nc.vector.memset(zeros_b[:, :], 0.0))
        dve.wait_ge(consts_made, 5)
        dve.wait_ge(edges_loaded, EDGES_LOADED)
        link(nc.vector.tensor_copy(samples[:, :], DST[:, 0:T:RUN]))
        for j in range(SAMPLES):
            if j >= 2:
                dve.wait_ge(beyond_added, j - 1)
            ts(BEYOND[:, j % 2, :], NODE_IOTA, samples[:, j:j + 1], None, ALU.is_gt).then_inc(beyond_ready, 1)
        link(nc.vector.tensor_copy(node_f[:, :], node_i[:, :]))
        dve.wait_ge(beyond_added, SAMPLES)
        link(ts(run_f[:, :], psA[:, 0:NB], -1.0, 0.0, ALU.add, ALU.max))
        link(nc.vector.tensor_copy(run_i[:, :], run_f[:, :]))
        dve.sem_inc(runs_wanted, 1)

        link(nc.vector.memset(H[:, :, :], 0.0))
        dve.sem_inc(filled, 1)
        link(nc.vector.memset(count_one[:, 0:1], 0.0))
        link(nc.vector.memset(count_one[:, 1:2], 1.0))
        link(nc.vector.memset(ones[:, :], 1.0))
        link(nc.vector.memset(onesrow[:, :], 0.0))
        link(nc.vector.memset(onesrow[:, HDIM:SW:HW], 1.0))
        link(nc.vector.memset(Rm[:, :, :], 0.0))
        link(nc.vector.tensor_copy(bound[:, 0:1], bound_i[:, :]))
        link(nc.vector.tensor_copy(chunk_f[:, :], chunk_i[:, :]))
        link(ts(chunk_f[:, :], chunk_f[:, :], -float(P), None, ALU.add))
        link(ts(bound[:, 1:2], bound[:, 0:1], float(T), None, ALU.add))

        dve.wait_ge(inputs_loaded, ALL_LOADED)
        link(nc.vector.memset(WR[:, ATT, HDIM:SW:HW], 0.0))
        for a in range(2):
            link(tt(attp[:, a, :].rearrange("k (h w) -> k h w", w=HDIM),
                    WR[:, ATT, 0:SW].rearrange("k (h w) -> k h w", w=HW)[:, :, 0:HDIM],
                    attv[:, a, :].rearrange("k (h w) -> k h w", w=HDIM), ALU.mult))
            link(nc.vector.reduce_sum(WR[:, ATT, SW + a * HEADS:SW + (a + 1) * HEADS],
                                      attp[:, a, :].rearrange("k (h w) -> k h w", w=HDIM), AX.X))
        dve.sem_inc(weights_made, 1)
        dve.sem_inc(out_used, 1)
        dve.sem_inc(rows_used[0], 1)
        dve.sem_inc(rows_used[1], 1)
        dve.sem_inc(pieces_used, NK - 1)
        dve.sem_inc(pieces_seen, NK)
        dve.sem_inc(sums_used[0], 1)
        dve.sem_inc(sums_used[1], 1)
        dve.sem_inc(sums_ready[0], 1)
        dve.sem_inc(sums_ready[1], 1)

        SPLIT_LINKS = 2
        PROJ_LINKS = 7

        def split(here, g):
            n0 = steps[0]
            steps[1] = g * SPLIT_LINKS
            rest = EGW[:, here, :]
            link(nc.vector.tensor_copy(PARTS[:, here, 0:DIM], TBW[:, here, :]))
            link(tt(rest, TBW[:, here, :], PARTS[:, here, 0:DIM], ALU.subtract))
            dve.sem_inc(rest_made, 1)
            steps[0] = n0

        def center(V, tmp, here):
            link(nc.vector.reduce_sum(stat[:, 0, here], V, AX.X))
            link(ts(stat[:, 0, here], stat[:, 0, here], 1.0 / DIM, None, ALU.mult))
            link(tt(V, V, stat[:, 0, here].unsqueeze(2).broadcast_to([P, GB, DIM]), ALU.subtract))
            link(tt(tmp, V, V, ALU.mult))
            link(nc.vector.reduce_sum(stat[:, 1, here], tmp, AX.X))

        def take_rows(f, g, here):
            dve.wait_ge(out_ready, g + (out_group_base(f, "rows") + 1))
            dve.sem_inc(turn["dve"], 1)
            if f == PROJ:
                n0 = steps[0]
                steps[1] = g * PROJ_LINKS
                link(tt(C[:, here, :], OUTG[:, :, 0:DIM], X[:, here, :], ALU.add))
                dve.sem_inc(out_used, 1)
                link(tt(C[:, here, :], C[:, here, :], row(PB, GB), ALU.add))
                center(C[:, here, :], EGW[:, here, :], here)
                assert steps[0] == n0 + PROJ_LINKS
                steps[0] = n0
            elif f in (MAX1, MAX2, MEAN1, MEAN2):
                ts(TBW[:, here, :], OUTG[:, :, 0:DIM], 1.0, None, ALU.mult).then_inc(table_made, 1)
                b = {MAX1: B_M1, MAX2: B_M2, MEAN1: B_S1, MEAN2: B_S2}[f]
                tt(R[:, here, :], OUTG[:, :, DIM:2 * DIM], row(b, GB), ALU.add).then_inc(out_used, 1)
                if f in (MEAN1, MEAN2):
                    dve.wait_ge(table_made, g + (PASS_OF_PHASE[f] * NG + 1))
                    dve.sem_inc(turn["dve"], 1)
                    split(here, g)
            else:
                tt(TBW[:, here, :], OUTG[:, :, 0:DIM], dis[:, here].unsqueeze(2).broadcast_to([P, GB, DIM]),
                   ALU.mult).then_inc(table_made, 1)
                dve.wait_ge(table_made, g + (PASS_OF_PHASE[f] * NG + 1))
                dve.sem_inc(out_used, 1)
                split(here, g)

        def node_rows(f):
            with dve.Fori(0, NG) as g:
                take_rows(f, g, bass.ds(g * GB, GB))
            if f in (MEAN1, MEAN2, GCN1, GCN2, GCN3):
                steps[0] += SPLIT_LINKS * NG
                steps[1] = 0
            if f == PROJ:
                steps[0] += PROJ_LINKS * NG
                steps[1] = 0
            rows_taken(f)

        def rows_taken(f):
            if f in PASS_OF_PHASE:
                dve.wait_ge(table_made, (PASS_OF_PHASE[f] + 1) * NG)
            dve.wait_ge(out_used, out_group_base(f, "rows") + NG + 1)

        for g in range(NG):
            here = slice(g * GB, (g + 1) * GB)
            dve.wait_ge(out_ready, g + 1)
            tt(TB0[:, here, :], OUTG[:, :, 0:W0], onesrow[:, :].unsqueeze(1).broadcast_to([P, GB, W0]),
               ALU.add).then_inc(table_made, 1)
            ts(ADN[:, here, :], OUTG[:, :, W0:W0 + HEADS], 1.0, None, ALU.mult).then_inc(out_used, 1)
            dve.wait_ge(runs_loaded[g % 2], 16 * GB * (g // 2 + 1))
            link(tt(BELOW, RUNS[:, g % 2, :, :], node_f[:, here].unsqueeze(2).broadcast_to([P, GB, RUN]), ALU.is_lt))
            dve.sem_inc(runs_read, 1)
            link(nc.vector.reduce_sum(inner[:, here], BELOW, AX.X))
        dve.wait_ge(table_made, NG)
        dve.wait_ge(out_used, NG + 1)
        dve.sem_inc(ad_made, 1)
        link(stt(startN[:, :], run_f[:, :], float(RUN), inner[:, :], ALU.mult, ALU.add))
        dve.sem_inc(small_ready, 1)
        dve.wait_ge(small_done, 1)
        link(nc.vector.tensor_copy(starts[:, :], psA[0:NB, 0:P]))
        dve.sem_inc(starts_out, 1)
        dve.wait_ge(ends_back, 16)
        dve.sem_inc(small_ready, 1)
        dve.wait_ge(small_done, 2)
        link(nc.vector.tensor_copy(endN[:, :], psB[:, 0:NB]))
        link(tt(degN[:, :], endN[:, :], startN[:, :], ALU.subtract))
        link(ts(valid[:, :], degN[:, :], 1.0, None, ALU.min))
        link(stt(nf[:, :], valid[:, :], -float(2 * EPAD), startN[:, :], ALU.mult, ALU.add))
        link(ts(nf[:, :], nf[:, :], float(2 * EPAD), None, ALU.add))
        link(nc.vector.tensor_copy(dst0[:, :], DST[:, 0:1]))
        nc.vector.tensor_copy(start_i[:, :], nf[:, :]).then_inc(node_idx, 1)
        link(ts(lastf[:, :], ends[:, :], -1.0, 0.0, ALU.add, ALU.max))
        dve.sem_inc(rows_out, 1)
        dve.wait_ge(node_idx, 1)
        link(ts(nf[:, :], endN[:, :], -1.0, 0.0, ALU.add, ALU.max))
        link(nc.vector.tensor_copy(last_i[:, :], nf[:, :]))

        link(tt(same[:, :], DST, PREV, ALU.is_equal))
        link(nc.vector.tensor_reduce(whole[:, :], same[:, :], AX.X, ALU.min))
        link(ts(wdiag[:, :], ident[:, :], whole[:, 0:1], None, ALU.mult))
        dve.sem_inc(small_ready, 1)
        link(nc.vector.tensor_tensor_scan(out=LEADS, data0=same[:, :], data1=same[:, :], initial=1.0,
                                          op0=ALU.mult, op1=ALU.mult))
        link(nc.vector.tensor_copy(lead[:, :], DST[:, 0:1]))
        link(stt(lead[:, :], lead[:, :], 1.0, same[:, 0:1], ALU.add, ALU.mult))
        link(ts(lead[:, :], lead[:, :], -1.0, None, ALU.add))
        link(nc.vector.memset(same[:, 0:1], 0.0))
        link(ts(reset[:, :], same[:, :], -1.0, BIG, ALU.add, ALU.mult))

        dve.wait_ge(rowb_loaded, 16)
        link(ts(SEL16, ROWB, bound[:, 0:1], None, ALU.is_ge))
        link(stt(SEL16, ROWB, bound[:, 1:2], SEL16, ALU.is_lt, ALU.mult))
        dve.sem_inc(rowb_used, 1)
        link(ts(vpen[:, :], valid[:, :], -1.0, BIG, ALU.add, ALU.mult))
        link(ts(rcnt[:, :], degN[:, :], 1.0, None, ALU.max))
        link(nc.vector.reciprocal(rcnt[:, :], rcnt[:, :]))
        link(ts(dis[:, :], degN[:, :], 1.0, None, ALU.add))
        roots = [1]
        dve.sem_inc(sqrt_in, 1)
        dve.wait_ge(sqrt_done, 1)
        link(nc.vector.reciprocal(dis[:, :], dis[:, :]))
        dve.wait_ge(small_done, 3)
        link(nc.vector.tensor_copy(wrow[:, :], psA[0:W0, 0:P]))
        link(ts(wneg[:, :], wrow[:, :], -1.0, BIG, ALU.add, ALU.mult))
        dve.wait_ge(rowb_loaded, 32)
        link(stt(SEL16, ROWB, bound[:, 0:1], SEL16, ALU.is_lt, ALU.mult))
        dve.sem_inc(rowb_used, 1)
        dve.sem_inc(small_ready, 1)
        link(ts(COLF, DST, -1.0, chunk_f[:, 0:1], ALU.mult, ALU.add))
        link(tt(COLF, COLF, LEADS, ALU.mult))
        link(tt(COLF, COLF, DST, ALU.add))
        link(ts(COLI, COLF, float(P), None, ALU.add))
        link(ts(CELL, COLI, 7, 20, ALU.logical_shift_right, ALU.logical_shift_left))
        link(ts(COLI, COLI, P - 1, None, ALU.bitwise_and))
        link(tt(CELL, CELL, COLI, ALU.bitwise_or))
        link(ts(COLI, SRC, P - 1, 13, ALU.bitwise_and, ALU.logical_shift_left))
        link(tt(CELL, CELL, COLI, ALU.bitwise_or))
        link(ts(COLI, SRC, (64 - 1) * P, None, ALU.bitwise_and))
        link(tt(CELL, CELL, COLI, ALU.bitwise_or))
        dve.sem_inc(cells_made, 1)
        dve.wait_ge(small_done, 4)
        link(ts(cpen[:, :], psB[:, 0:NB], -1.0, BIG, ALU.add, ALU.mult))
        small = [4, 4]

        def small_sent():
            small[0] += 1
            dve.sem_inc(small_ready, 1)

        def small_got():
            small[1] += 1
            dve.wait_ge(small_done, small[1])

        dve.wait_ge(ad_first, 16)
        for h in range(HEADS):
            link(nc.vector.tensor_tensor_scan(out=AD[:, :, h], data0=same[:, :], data1=AD[:, :, h], initial=0.0,
                                              op0=ALU.mult, op1=ALU.add))

        def prev_state(view, s, k, w):
            return view[:, s, k - 1, 0:w] if k else view[:, 1 - s, S - 1, 0:w]

        def attention_pass():
            base = steps[0]
            with dve.Fori(0, ITERS) as i:
                for s in range(2):
                    here = bass.ds(i * (2 * S) + s * S, S)
                    steps[1] = i * (2 * ATT_LINKS)
                    dve.wait_ge(gathered[s], i * (16 * S) + 16 * S)
                    dve.sem_inc(turn["dve"], 1)
                    link(tt(Zs[:, :, :], G0[:, s, :, SW:W0], AD[:, here, :], ALU.add))
                    link(stt(Zs[:, :, :], Zs[:, :, :], 0.2, Zs[:, :, :], ALU.mult, ALU.max))
                    for h in range(HEADS):
                        link(nc.vector.tensor_tensor_scan(out=Rm[:, 1:S + 1, h], data0=reset[:, here], data1=Zs[:, :, h],
                                                          initial=Rm[:, 0:1, h], op0=ALU.add, op1=ALU.max),
                             behind=0 if h == HEADS - 1 else h + 1)
                    link(tt(EX[:, 0, :, :], Rm[:, 0:S, :], reset[:, here].unsqueeze(2).broadcast_to([P, S, HEADS]), ALU.add))
                    link(tt(EX[:, 0, :, :], EX[:, 0, :, :], Rm[:, 1:S + 1, :], ALU.subtract))
                    link(tt(EX[:, 1, :, :], Zs[:, :, :], Rm[:, 1:S + 1, :], ALU.subtract))
                    dve.sem_inc(exp_in, 1)
                    dve.wait_ge(hist_stored[s], i * 16 + 32)
                    link(nc.vector.tensor_copy(H0[:, s, :, SW:W0], Rm[:, 1:S + 1, :]))
                    link(nc.vector.tensor_copy(Rm[:, 0, :], Rm[:, S, :]))
                    dve.wait_ge(exp_done, i * 2 + (s + 1))
                    link(tt(H0[:, s, :, 0:SW].rearrange("p k (h w) -> p k h w", w=HW),
                            G0[:, s, :, 0:SW].rearrange("p k (h w) -> p k h w", w=HW),
                            EX[:, 1, :, :].unsqueeze(3).broadcast_to([P, S, HEADS, HW]), ALU.mult))
                    dve.sem_inc(rows_used[s], 1)
                    for k in range(S):
                        for h in range(HEADS):
                            head = slice(h * HW, (h + 1) * HW)
                            link(stt(H0[:, s, k, head], prev_state(H0, s, k, SW)[:, head], EX[:, 0, k, h:h + 1],
                                     H0[:, s, k, head], ALU.mult, ALU.add),
                                 behind=0 if (k, h) == (S - 1, HEADS - 1) else HEADS - 1)
                    dve.sem_inc(block_done[s], 1)
                assert steps[0] - base == 2 * ATT_LINKS
            steps[0] = base + 2 * ATT_LINKS * ITERS
            steps[1] = 0

        ATT_LINKS = 2 + HEADS + 3 + 2 + 1 + 4 * S

        def running_pass(q):
            base = steps[0]
            links = S + 2
            with dve.Fori(0, ITERS) as i:
                for s in range(2):
                    steps[1] = i * (2 * links)
                    dve.wait_ge(gathered[s], i * (16 * S) + 16 * S * (q * ITERS + 1))
                    dve.sem_inc(turn["dve"], 1)
                    dve.wait_ge(hist_stored[s], i * 16 + 16 * (q * ITERS + 2))
                    dve.sem_inc(turn["dve"], 1)
                    dve.wait_ge(eterm_ready[s], i + (MAX_PASSES.index(q) * ITERS + 1))
                    for h in range(2):
                        ks = slice(4 * h, 4 * h + 4)
                        link(tt(HWD[:, s, ks, :], GW[:, s, ks, :],
                                ETERM[:, s, h, 0:4 * DIM].rearrange("p (k w) -> p k w", w=DIM), ALU.add))
                    dve.sem_inc(rows_used[s], 1)
                    for k in range(S):
                        link(stt(HWD[:, s, k, :], prev_state(HWD, s, k, DIM), reset[:, bass.ds(i * (2 * S) + (s * S + k), 1)],
                                 HWD[:, s, k, :], ALU.add, ALU.max))
                    dve.sem_inc(block_done[s], 1)
                assert steps[0] - base == 2 * links
            steps[0] = base + 2 * links * ITERS
            steps[1] = 0

        def split_carries(w):
            link(nc.vector.tensor_copy(Q_PARTS[:, 0, 0:w], Q[:, 0:w]))
            link(tt(Q_REST[:, 0:w], Q[:, 0:w], Q_PARTS[:, 0, 0:w], ALU.subtract))
            link(nc.vector.tensor_copy(Q_PARTS[:, 1, 0:w], Q_REST[:, 0:w]))
            link(tt(Q_PARTS[:, 2, 0:w], Q_REST[:, 0:w], Q_PARTS[:, 1, 0:w], ALU.subtract))

        def carries(f, q):
            base = out_group_base(f, "carry")
            if q == 0:
                link(nc.vector.tensor_copy(F0[:, 0:SW], H0[:, 1, S - 1, 0:SW]))
                link(nc.vector.tensor_copy(F0[:, W0:W0 + SW].rearrange("p (h w) -> p h w", w=HW),
                                           H0[:, 1, S - 1, SW:W0].unsqueeze(2).broadcast_to([P, HEADS, HW])))
                small_sent()
                small_got()
                link(nc.vector.tensor_tensor_scan(out=QT[:, 0, :], data0=wneg[0:SW, :], data1=psA[0:SW, P:2 * P],
                                                  initial=0.0, op0=ALU.add, op1=ALU.max))
                link(nc.vector.tensor_copy(QT[:, 1, 0:1], wneg[0:SW, 0:1]))
                link(tt(QT[:, 1, 1:P], QT[:, 0, 0:P - 1], wneg[0:SW, 1:P], ALU.add))
                link(tt(QT[:, 1, 1:P], QT[:, 1, 1:P], QT[:, 0, 1:P], ALU.subtract))
                link(tt(QT[:, 3, :], psA[0:SW, P:2 * P], QT[:, 0, :], ALU.subtract))
                dve.sem_inc(exp_in, 2)
                dve.wait_ge(exp_done, 2 * ITERS + 2)
                link(tt(QT[:, 3, :], QT[:, 3, :], psA[0:SW, 0:P], ALU.mult))
                link(nc.vector.tensor_tensor_scan(out=QT[:, 2, :], data0=QT[:, 1, :], data1=QT[:, 3, :],
                                                  initial=0.0, op0=ALU.mult, op1=ALU.add))
                small_sent()
                small_got()
                link(nc.vector.tensor_copy(Q[:, 0:SW], psB[:, 0:SW]))
                link(nc.vector.tensor_copy(Q[:, SW:W0], psB[:, P:P + SW:HW]))
                split_carries(W0)
                small_sent()
            else:
                small_sent()
                small_got()
                link(nc.vector.tensor_tensor_scan(out=QT[0:DIM, 0, :], data0=wneg[0:DIM, :], data1=psA[0:DIM, 0:P],
                                                  initial=0.0, op0=ALU.add, op1=ALU.max))
                small_sent()
                small_got()
                link(nc.vector.tensor_copy(Q[:, 0:DIM], psB[:, 0:DIM]))
                split_carries(DIM)
                small_sent()
            start = steps[0]
            with dve.Fori(0, NG) as g:
                steps[1] = g
                here = bass.ds(g * GB, GB)
                dve.wait_ge(out_ready, g + (base + 1))
                dve.sem_inc(turn["dve"], 1)
                if q == 0:
                    link(ts(CQ[:, here, :], OUTG[:, :, 0:W0], 1.0, None, ALU.mult))
                else:
                    link(tt(C[:, here, :], OUTG[:, :, 0:DIM],
                            cpen[:, here].unsqueeze(2).broadcast_to([P, GB, DIM]), ALU.add))
                dve.sem_inc(out_used, 1)
            steps[0] = start + (steps[0] - start) * NG
            steps[1] = 0

        def finish_maxima(f, q, g):
            here = slice(g * GB, (g + 1) * GB)
            part = EGW[:, here, :]
            dve.wait_ge(end_gathered[g], 16 * GB * (q + 1))
            link(tt(part, part, C[:, here, :], ALU.max))
            link(tt(part, part, per(valid[:, here], GB, DIM), ALU.mult))
            link(tt(part, part, R[:, here, :], ALU.add))
            if f == MAX1:
                link(stt(C[:, here, :], part, 0.01, part, ALU.mult, ALU.max))
                dve.sem_inc(rows_ready, 1)
            else:
                link(stt(part, part, 0.01, part, ALU.mult, ALU.max))
                link(tt(X[:, here, :], X[:, here, :], part, ALU.add))
                center(X[:, here, :], part, here)

        def finish_block(f, here):
            part = EGW[:, here, :]
            if f in (MEAN1, MEAN2):
                link(stt(part, part, rcnt[:, here], R[:, here, :], ALU.mult, ALU.add))
            else:
                link(tt(part, part, TBW[:, here, :], ALU.add))
                link(stt(part, part, dis[:, here], row({GCN1: B_G1, GCN2: B_G2, GCN3: B_G3}[f], 1), ALU.mult, ALU.add))
            if f in (MEAN1, GCN1, GCN2):
                link(ts(part, part, 0.0, None, ALU.max))
            else:
                link(tt(X[:, here, :], X[:, here, :], part, ALU.add))
                link(nc.vector.reduce_sum(stat[:, 0, here], X[:, here, :], AX.X))
                link(ts(stat[:, 0, here], stat[:, 0, here], 1.0 / DIM, None, ALU.mult))
                link(ts(X[:, here, :], X[:, here, :], stat[:, 0, here], None, ALU.subtract))
                link(tt(part, X[:, here, :], X[:, here, :], ALU.mult))
                link(nc.vector.reduce_sum(stat[:, 1, here], part, AX.X))

        def sum_of_parts(ps, into):
            return nc.vector.reduce_sum(into, ps[:, 0:3 * DIM].rearrange("p (a w) -> p w a", w=DIM), AX.X)

        def split_leads():
            link(nc.vector.tensor_copy(LEAD_PARTS[:, 0:DIM], LEAD_SUM))
            link(tt(LEAD_REST, LEAD_SUM, LEAD_PARTS[:, 0:DIM], ALU.subtract))
            link(nc.vector.tensor_copy(LEAD_PARTS[:, DIM:2 * DIM], LEAD_REST))
            link(tt(LEAD_PARTS[:, 2 * DIM:3 * DIM], LEAD_REST, LEAD_PARTS[:, DIM:2 * DIM], ALU.subtract))

        def sum_by_counts(f, n):
            if n == 0:
                link(nc.vector.memset(MOST, 0.0))

            def take_block(i, half, here):
                if n == 0:
                    for c in range(NK):
                        j = half * NK + c
                        dve.wait_ge(piece_loaded[c], i * 32 + 16 * (half + 1))
                        dve.sem_inc(turn["dve"], 1)
                        dve.wait_ge(pieces_seen, i * (2 * NK) + (NK + j - 1))
                        tt(MOST[:, j % 2, :], MOST[:, j % 2, :], CNT16[:, c, :, :].rearrange("p k m -> p (k m)"),
                           ALU.max).then_inc(pieces_seen, 1)
                dve.wait_ge(sums_ready[half], i + (n * CB // 2 + 2))
                dve.sem_inc(turn["dve"], 1)
                into = LEAD_SUM if here is None else EGW[:, here, :].rearrange("p a w -> p (a w)")
                sum_of_parts(psM[half], into).then_inc(sums_used[half], 1)
                dve.wait_ge(sums_used[half], i + (n * CB // 2 + 2))
                dve.sem_inc(turn["dve"], 1)
                if here is None:
                    split_leads()
                    dve.sem_inc(leads_ready, 1)
                else:
                    finish_block(f, here)

            take_block(0, 0, None)
            start = steps[0]
            take_block(0, 1, slice(0, 1))
            links = 2 * (steps[0] - start)
            base = steps[0]
            steps[0] -= links
            with dve.Fori(1, CB // 2) as i:
                for half in range(2):
                    steps[1] = i * links
                    take_block(i, half, bass.ds(i * 2 + (half - 1), 1))
            assert steps[0] == base
            steps[0] = base + links * (CB // 2 - 1)
            steps[1] = 0
            if n == 0:
                dve.wait_ge(pieces_seen, NK * (CB + 1))
                link(nc.vector.tensor_reduce(most_all[:, :], MOST, AX.XY, ALU.max))
                small_sent()
                small_got()
                link(nc.vector.tensor_reduce(most_row[:, :], psA[0:1, 0:P], AX.X, ALU.max))
                link(ts(most_row[:, :], most_row[:, :], 256.0, None, ALU.is_ge))
                link(nc.vector.tensor_copy(large[:, :], most_row[:, :]))
                link(nc.vector.memset(EAZ[:, :], 0.0))
                dve.sem_inc(large_known, 1)
                flag = dve.value_load(large[0:1, 0:1], min_val=0, max_val=1)
                with dve.If(flag == 1):
                    dve.sem_inc(again_taken, 1)

                    def take_again(b, here):
                        dve.wait_ge(again_summed, b + 1)
                        dve.sem_inc(turn["dve"], 1)
                        into = LEAD_SUM if here is None else EGW[:, here, :].rearrange("p a w -> p (a w)")
                        sum_of_parts(psA, into).then_inc(again_step, 1)
                        dve.wait_ge(again_step, b * AGAIN_LINKS + 1)
                        dve.sem_inc(turn["dve"], 1)
                        if here is None:
                            again(nc.vector.tensor_copy(LEAD_PARTS[:, 0:DIM], LEAD_SUM), 2)
                            again(tt(LEAD_REST, LEAD_SUM, LEAD_PARTS[:, 0:DIM], ALU.subtract), 3)
                            again(nc.vector.tensor_copy(LEAD_PARTS[:, DIM:2 * DIM], LEAD_REST), 4)
                            again(tt(LEAD_PARTS[:, 2 * DIM:3 * DIM], LEAD_REST, LEAD_PARTS[:, DIM:2 * DIM],
                                     ALU.subtract), AGAIN_LINKS)
                        else:
                            part = EGW[:, here, :]
                            again(stt(part, part, rcnt[:, here], R[:, here, :], ALU.mult, ALU.add), b * AGAIN_LINKS + 2)
                            again(ts(part, part, 0.0, None, ALU.max), b * AGAIN_LINKS + 3)
                            dve.sem_inc(again_step, AGAIN_LINKS - 3)
                        dve.sem_inc(again_taken, 1)

                    AGAIN_LINKS = 5

                    def again(ins, count):
                        ins.then_inc(again_step, 1)
                        dve.wait_ge(again_step, count)

                    take_again(0, None)
                    with dve.Fori(1, CB) as b:
                        take_again(b, bass.ds(b - 1, 1))

        def inverse_deviations():
            link(ts(stat[:, 1, :], stat[:, 1, :], 1.0 / DIM, 1e-5, ALU.mult, ALU.add))
            roots[0] += 1
            dve.sem_inc(sqrt_in, 1)
            dve.wait_ge(sqrt_done, roots[0])
            link(nc.vector.reciprocal(stat[:, 1, :], stat[:, 1, :]))

        def scale_x():
            inverse_deviations()
            for g in range(NG):
                here = slice(g * GB, (g + 1) * GB)
                link(tt(X[:, here, :], X[:, here, :], per(stat[:, 1, here], GB, DIM), ALU.mult))
                dve.sem_inc(rows_ready, 1)

        dve.sem_inc(end_free, 1)
        attention_pass()
        carries(ATT, 0)
        link(tt(zself[:, :, :], TB0[:, :, SW:W0], ADN[:, :, :], ALU.add))
        link(stt(zself[:, :, :], zself[:, :, :], 0.2, zself[:, :, :], ALU.mult, ALU.max))
        link(tt(CQ[:, :, SW:W0], CQ[:, :, SW:W0], per(cpen[:, :], NB, HEADS), ALU.add))
        for g in range(NG):
            here = slice(g * GB, (g + 1) * GB)
            dve.wait_ge(end_gathered[g], 16 * GB)
            link(tt(EG0[:, here, SW:W0], EG0[:, here, SW:W0], per(vpen[:, here], GB, HEADS), ALU.add))
            link(tt(mx[:, here, :], EG0[:, here, SW:W0], CQ[:, here, SW:W0], ALU.max))
            link(tt(mx[:, here, :], mx[:, here, :], zself[:, here, :], ALU.max))
            link(tt(E3[:, 0, here, :], EG0[:, here, SW:W0], mx[:, here, :], ALU.subtract))
            link(tt(E3[:, 1, here, :], CQ[:, here, SW:W0], mx[:, here, :], ALU.subtract))
            link(tt(E3[:, 2, here, :], zself[:, here, :], mx[:, here, :], ALU.subtract))
            dve.sem_inc(exp_in, 1)
            dve.wait_ge(exp_done, 2 * ITERS + 3 + g)
            for j, V in enumerate((EG0, CQ, TB0)):
                Vh = V[:, here, 0:SW].rearrange("p b (h w) -> p b h w", w=HW)
                link(tt(Vh, Vh, E3[:, j, here, :].unsqueeze(3).broadcast_to([P, GB, HEADS, HW]), ALU.mult))
            link(tt(EG0[:, here, 0:SW], EG0[:, here, 0:SW], CQ[:, here, 0:SW], ALU.add))
            link(tt(EG0[:, here, 0:SW], EG0[:, here, 0:SW], TB0[:, here, 0:SW], ALU.add))
            link(nc.vector.reciprocal(rden[:, here, :], EG0[:, here, HDIM:SW:HW]))
            link(tt(C[:, here, :].rearrange("p b (h w) -> p b h w", w=HDIM),
                    EG0[:, here, 0:SW].rearrange("p b (h w) -> p b h w", w=HW)[:, :, :, 0:HDIM],
                    rden[:, here, :].unsqueeze(3).broadcast_to([P, GB, HEADS, HDIM]), ALU.mult))
            dve.sem_inc(rows_ready, 1)
        node_rows(PROJ)
        inverse_deviations()
        for g in range(NG):
            here = slice(g * GB, (g + 1) * GB)
            rows_c = C[:, here, :]
            link(tt(rows_c, rows_c, per(stat[:, 1, here], GB, DIM), ALU.mult))
            link(tt(rows_c, rows_c, row(LG, GB), ALU.mult))
            link(tt(rows_c, rows_c, row(LB, GB), ALU.add))
            link(tt(X[:, here, :], X[:, here, :], rows_c, ALU.add))
            center(X[:, here, :], rows_c, here)
        scale_x()

        for f in (MAX1, MAX2, MEAN1, MEAN2, GCN1, GCN2, GCN3):
            q = PASS_OF_PHASE[f]
            if f != MAX2:
                node_rows(f)
            if q < GATHER_PASSES:
                dve.sem_inc(end_free, 1)
                running_pass(q)
                carries(f, q)
                for g in range(NG):
                    finish_maxima(f, q, g)
                    if f == MAX1 and g >= 2:
                        take_rows(MAX2, g - 2, slice((g - 2) * GB, (g - 1) * GB))
                if f == MAX1:
                    for g in range(NG - 2, NG):
                        take_rows(MAX2, g, slice(g * GB, (g + 1) * GB))
                    rows_taken(MAX2)
                else:
                    dve.sem_inc(iota_wanted, 1)
                    dve.wait_ge(iota_made, 1)
                    link(ts(SEL16, NODE_IOTA, lead[:, 0:1], None, ALU.is_equal))
                    scale_x()
            else:
                sum_by_counts(f, q - GATHER_PASSES)
                if f in (MEAN2, GCN3):
                    scale_x()
                else:
                    dve.sem_inc(rows_ready, NG)

    ctx.close()


_INS = ["x", "src", "dst", "dst_before", "edge_attr", "L0_gnn_W", "L0_gnn_att_src", "L0_gnn_att_dst",
        "L0_gnn_gat_bias", "L0_gnn_proj_WT", "L0_gnn_proj_b", "L0_gnn_ln_g", "L0_gnn_ln_b",
        "L1_gnn_W1_msg", "L1_gnn_W1_edge", "L1_gnn_W1_root", "L1_gnn_b1",
        "L1_gnn_W2_msg", "L1_gnn_W2_edge", "L1_gnn_W2_root", "L1_gnn_b2",
        "L2_gnn_W1_l", "L2_gnn_b1", "L2_gnn_W1_r", "L2_gnn_W2_l", "L2_gnn_b2", "L2_gnn_W2_r",
        "L3_gnn_W1", "L3_gnn_b1", "L3_gnn_W2", "L3_gnn_b2", "L3_gnn_W3", "L3_gnn_b3"]


def kernel(**inputs):
    import numpy as _np
    import concourse.bacc as _bacc
    from concourse import mybir as _mybir
    from concourse.bass_utils import run_bass_kernel_spmd as _run

    src = _np.arange(-EDGES, EPAD - EDGES, dtype=_np.int32)
    src[:EDGES] = inputs["src"]
    dst = _np.full((EPAD + 1,), NODES, _np.int32)
    dst[1:EDGES + 1] = inputs["dst"]
    attr = _np.zeros((EPAD, EDGE_DIM), _np.float32)
    attr[:EDGES] = inputs["edge_attr_32"]
    laid = dict(inputs)
    laid["src"] = src.reshape(P, T)
    laid["dst"] = dst[1:].reshape(P, T)
    laid["dst_before"] = dst[:-1].reshape(P, T)
    laid["edge_attr"] = attr.reshape(P, T, EDGE_DIM).transpose(2, 1, 0)
    laid["L0_gnn_proj_WT"] = _np.asarray(inputs["L0_gnn_proj_W"]).T

    nc = _bacc.Bacc("TRN2", target_bir_lowering=False, num_devices=1)
    arrays, args = {}, []
    for name in _INS:
        a = _np.ascontiguousarray(laid[name])
        arrays[f"in_{name}"] = a
        args.append(nc.dram_tensor(f"in_{name}", a.shape, _mybir.dt.from_np(a.dtype), kind="ExternalInput").ap())
    args.append(nc.dram_tensor("out_0", (NODES, DIM), F32, kind="ExternalOutput").ap())
    build(nc, *args)
    r = _run(nc, [arrays], core_ids=[0])
    return r.results[0]["out_0"]
```
